# Optimizing a Trainium2 kernel written in Bass

```python
import numpy as np
import jax
import jax.numpy as jnp

def _softmax(x, axis=-1):
    return jax.nn.softmax(x, axis=axis)

def _gelu(x):
    return jax.nn.gelu(x, approximate=True)

def _silu(x):
    return jax.nn.silu(x)

def _sigmoid(x):
    return jax.nn.sigmoid(x)

def _layernorm(x, axis=-1, eps=1e-05):
    m = jnp.mean(x, axis=axis, keepdims=True)
    v = jnp.var(x, axis=axis, keepdims=True)
    return (x - m) / jnp.sqrt(v + eps)

def _scatter_add(tgt, idx, src, axis=0):
    return tgt.at[idx].add(src)

def _segment_sum(src, seg, n):
    return jax.ops.segment_sum(src, seg, n)
kernel_name = 'mk_xattn_ffn_d4_seqx_r8_4bf929'

def setup_inputs(seed: int=0):
    np.random.seed(seed)
    _w = jnp.asarray

    def _rec_inputs():
        import jax
        import jax.numpy as jnp
        _rk = jax.random.key(seed)
        x = -0.0003929 + 0.9999 * jax.random.normal(jax.random.fold_in(_rk, 1), (16, 128, 256), jnp.float32)
        _lenS = 128 - jax.random.randint(jax.random.fold_in(_rk, 7), (16,), 0, max(1, 128 // 4) + 1, jnp.int32)
        _lenS2 = 128 - jax.random.randint(jax.random.fold_in(_rk, 8), (16,), 0, max(1, 128 // 4) + 1, jnp.int32)
        _ctx_2048P = jax.random.normal(jax.random.fold_in(_rk, 11), (16, 16, 256), jnp.float32)
        _ctx_2048c = jax.random.dirichlet(jax.random.fold_in(_rk, 511), 0.3 * jnp.ones((16,), jnp.float32), (16, 128))
        _ctx_2048t = jnp.einsum('bsk,bkd->bsd', _ctx_2048c, _ctx_2048P)
        _ctx_2048t = _ctx_2048t * jax.lax.rsqrt(jnp.mean(jnp.square(_ctx_2048t)) + 1e-12) * 0.953939
        ctx_2048 = -0.000514642 + 1.00011 * (_ctx_2048t + 0.3 * jax.random.normal(jax.random.fold_in(_rk, 611), (16, 128, 256), jnp.float32))
        itok_BxS_0_1023 = jax.random.randint(jax.random.fold_in(_rk, 12), (16, 128), 0, 128, jnp.int32)
        _validS = jnp.arange(128)[None, :] < _lenS[:, None]
        _validS2 = jnp.arange(128)[None, :] < _lenS2[:, None]
        _causal = jnp.tril(jnp.ones((128, 128), dtype=bool))
        mask_BxS2_bk0 = jnp.logical_not(jnp.broadcast_to(_validS2[:, :], (16, 128)))
        mask_BxS2_if1 = jnp.where(jnp.ones((16, 128), dtype=bool), 1, 0).astype(jnp.int32)
        return (x, ctx_2048, itok_BxS_0_1023, mask_BxS2_bk0, mask_BxS2_if1)
    x, ctx_2048, itok_BxS_0_1023, mask_BxS2_bk0, mask_BxS2_if1 = _rec_inputs()

    def _L0_xattn_setup():
        import jax, jax.numpy as jnp
        import numpy as np
        FEAT = 256
        G = 16
        DG = FEAT // G
        key = jax.random.key(seed)
        ks = jax.random.split(key, 8)
        bs, N1, N2 = (2, 512, 64)
        s = 1.0 / np.sqrt(FEAT)
        return {'ref_feat': jax.random.normal(ks[0], (bs, N1, FEAT), jnp.float32), 'sup_feat': jax.random.normal(ks[1], (bs, N2, FEAT), jnp.float32), 'W_fc': jax.random.normal(ks[2], (FEAT, FEAT), jnp.float32) * s, 'b_fc': jnp.zeros((FEAT,), jnp.float32), 'W_q': jax.random.normal(ks[3], (FEAT, FEAT), jnp.float32) * s, 'b_q': jnp.zeros((FEAT,), jnp.float32), 'W_k': jax.random.normal(ks[4], (FEAT, FEAT), jnp.float32) * s, 'b_k': jnp.zeros((FEAT,), jnp.float32), 'W_v': jax.random.normal(ks[5], (FEAT, FEAT, 1, 1), jnp.float32) * 0.01, 'b_v': jnp.zeros((FEAT,), jnp.float32)}
    _L0_xattn_all = _L0_xattn_setup()
    _L0_xattn_in = {k: v for k, v in _L0_xattn_all.items() if k in ('W_fc', 'b_fc', 'W_q', 'b_q', 'W_k', 'b_k', 'W_v', 'b_v')}
    del _L0_xattn_all

    def _L0_ffn_setup():
        import jax, jax.numpy as jnp
        import numpy as np
        B, T, D = (4, 128, 256)
        N, S, H = (8, 8, 8)
        ETA = 1.0
        key = jax.random.key(seed)
        ks = jax.random.split(key, 9)
        return {'x': jax.random.normal(ks[0], (B, T, D), jnp.float32), 'select_weight': jax.random.normal(ks[1], (N, D, S), jnp.float32) / D, 'select_mean_diff': jax.random.normal(ks[2], (N, D), jnp.float32) / D, 'imp_center': jax.random.normal(ks[3], (N,), jnp.float32), 'imp_slope': jax.random.normal(ks[4], (N,), jnp.float32) * 5.0, 'lora_update': jax.random.normal(ks[5], (N, D, H), jnp.float32) * 0.02, 'lora_degen': jax.random.normal(ks[6], (N, D, H), jnp.float32) * 0.02, 'bias_w': jax.random.normal(ks[7], (N, D), jnp.float32) * 0.02, 'debias_w': jax.random.normal(ks[8], (N, D), jnp.float32) * 0.02}
    _L0_ffn_all = _L0_ffn_setup()
    _L0_ffn_in = {k: v for k, v in _L0_ffn_all.items() if k in ('select_weight', 'select_mean_diff', 'imp_center', 'imp_slope', 'lora_update', 'lora_degen', 'bias_w', 'debias_w')}
    del _L0_ffn_all

    def _L1_xattn_setup():
        import jax, jax.numpy as jnp
        import numpy as np
        B, Lq, Lk = (2, 512, 128)
        Q_DIM, KV_DIM = (256, 256)
        H, HD = (16, 128)
        KVC, QC, R = (64, 96, 64)
        LOOKBACK = 8
        NEG = -1e+30

        def _rope(x, L):
            half = x.shape[-1] // 2
            inv_freq = 1.0 / 10000.0 ** (jnp.arange(half, dtype=jnp.float32) / half)
            ang = jnp.arange(L, dtype=jnp.float32)[:, None] * inv_freq
            cos, sin = (jnp.cos(ang), jnp.sin(ang))
            x1, x2 = (x[..., :half], x[..., half:])
            return jnp.concatenate([x1 * cos - x2 * sin, x1 * sin + x2 * cos], axis=-1)
        key = jax.random.key(seed)
        ks = jax.random.split(key, 11)

        def w(k, shape, fan_in):
            return jax.random.normal(k, shape, jnp.float32) / np.sqrt(fan_in).astype(np.float32)
        return {'q': jax.random.normal(ks[0], (B, Lq, Q_DIM), jnp.float32), 'kv': jax.random.normal(ks[1], (B, Lk, KV_DIM), jnp.float32), 'seg_id': jnp.sort(jax.random.randint(ks[2], (B, Lq), 0, Lk), axis=-1), 'W_kvc': w(ks[3], (KV_DIM, KVC), KV_DIM), 'W_dq': w(ks[4], (Q_DIM, QC), Q_DIM), 'W_uq': w(ks[5], (QC, H * HD), QC), 'W_qr': w(ks[6], (QC, H * R), QC), 'W_uk': w(ks[7], (KVC, H * HD), KVC), 'W_kr': w(ks[8], (KVC, R), KVC), 'W_uv': w(ks[9], (KVC, H * HD), KVC), 'W_o': w(ks[10], (H * HD, Q_DIM), H * HD)}
    _L1_xattn_all = _L1_xattn_setup()
    _L1_xattn_in = {k: v for k, v in _L1_xattn_all.items() if k in ('W_kvc', 'W_dq', 'W_uq', 'W_qr', 'W_uk', 'W_kr', 'W_uv', 'W_o')}
    del _L1_xattn_all

    def _L1_ffn_setup():
        import jax, jax.numpy as jnp
        import numpy as np
        B, S, H = (4, 128, 256)
        NH = 16
        HD = H // NH
        RD = HD // 2
        LAT = H // 4
        I = 128
        NE = 8
        NSH = 1
        NR = NE - NSH
        TOPK = 2
        EPS = 1e-05
        SCALING = 8.0

        def _w(key, shape, fan_in):
            return jax.random.normal(key, shape, dtype=jnp.float32) / np.sqrt(fan_in)

        def rmsnorm(x, w):
            rms = jax.lax.rsqrt(jnp.mean(x * x, axis=-1, keepdims=True) + EPS)
            return w * rms * x

        def rope_cos_sin(seq_len):
            inv_freq = 1.0 / 10000.0 ** (jnp.arange(0, RD, 2, dtype=jnp.float32) / RD)
            t = jnp.arange(seq_len, dtype=jnp.float32)
            ang = jnp.outer(t, inv_freq)
            emb = jnp.concatenate([ang, ang], axis=-1)
            return (jnp.cos(emb), jnp.sin(emb))

        def apply_rope(x, cos, sin):
            c = cos[None, :, None, :]
            s = sin[None, :, None, :]
            x1, x2 = jnp.split(x, 2, axis=-1)
            rot = jnp.concatenate([-x2, x1], axis=-1)
            return x * c + rot * s

        def expert_ffn(x, wg, wu, wd):
            h = jax.nn.silu(x @ wg) * (x @ wu) / SCALING
            return h @ wd

        def attention(x, kv_d_w, q_d_w, k_u_w, v_u_w, q_u_w, rope_k_w, rope_q_w, o_w):
            b, s, _ = x.shape
            kv_d = x @ kv_d_w
            q_d = x @ q_d_w
            k_p = (kv_d @ k_u_w).reshape(b, s, NH, RD)
            q_p = (q_d @ q_u_w).reshape(b, s, NH, RD)
            v = (kv_d @ v_u_w).reshape(b, s, NH, HD)
            k_r = (x @ rope_k_w).reshape(b, s, NH, RD)
            q_r = (q_d @ rope_q_w).reshape(b, s, NH, RD)
            cos, sin = rope_cos_sin(s)
            k_r = apply_rope(k_r, cos, sin)
            q_r = apply_rope(q_r, cos, sin)
            k = jnp.concatenate([k_p, k_r], axis=-1)
            q = jnp.concatenate([q_p, q_r], axis=-1)
            scale = 1.0 / np.sqrt(HD)
            scores = jnp.einsum('bqhd,bkhd->bhqk', q, k) * scale
            causal = jnp.tril(jnp.ones((s, s), dtype=bool))
            scores = jnp.where(causal[None, None], scores, jnp.finfo(scores.dtype).min)
            probs = jax.nn.softmax(scores, axis=-1)
            out = jnp.einsum('bhqk,bkhd->bqhd', probs, v).reshape(b, s, H)
            return out @ o_w

        def moe(x, sh_gate, sh_up, sh_down, r_gate, r_up, r_down, router_w, router_b):
            shared = expert_ffn(x, sh_gate, sh_up, sh_down)
            logits = x @ router_w + router_b
            probs = jax.nn.sigmoid(logits)
            scores, idx = jax.lax.top_k(probs, TOPK)
            scores = scores / jnp.sum(scores, axis=-1, keepdims=True)
            w = jnp.sum(jax.nn.one_hot(idx, NR, dtype=x.dtype) * scores[..., None], axis=-2)
            combined = jnp.zeros_like(x)
            for e in range(NR):
                combined = combined + w[..., e:e + 1] * expert_ffn(x, r_gate[e], r_up[e], r_down[e])
            return shared + combined
        key = jax.random.key(seed)
        ks = jax.random.split(key, 24)
        return {'x': jax.random.normal(ks[0], (B, S, H), dtype=jnp.float32), 'ln1_w': jnp.ones((H,), jnp.float32), 'ln2_w': jnp.ones((H,), jnp.float32), 'kv_d_w': _w(ks[1], (H, LAT), H), 'q_d_w': _w(ks[2], (H, LAT), H), 'k_u_w': _w(ks[3], (LAT, H // 2), LAT), 'v_u_w': _w(ks[4], (LAT, H), LAT), 'q_u_w': _w(ks[5], (LAT, H // 2), LAT), 'rope_k_w': _w(ks[6], (H, H // 2), H), 'rope_q_w': _w(ks[7], (LAT, H // 2), LAT), 'o_w': _w(ks[8], (H, H), H), 'sh_gate': _w(ks[9], (H, I), H), 'sh_up': _w(ks[10], (H, I), H), 'sh_down': _w(ks[11], (I, H), I), 'r_gate': _w(ks[12], (NR, H, I), H), 'r_up': _w(ks[13], (NR, H, I), H), 'r_down': _w(ks[14], (NR, I, H), I), 'router_w': _w(ks[15], (H, NR), H), 'router_b': jnp.zeros((NR,), jnp.float32)}
    _L1_ffn_all = _L1_ffn_setup()
    _L1_ffn_in = {k: v for k, v in _L1_ffn_all.items() if k in ('ln1_w', 'ln2_w', 'kv_d_w', 'q_d_w', 'k_u_w', 'v_u_w', 'q_u_w', 'rope_k_w', 'rope_q_w', 'o_w', 'sh_gate', 'sh_up', 'sh_down', 'r_gate', 'r_up', 'r_down', 'router_w', 'router_b')}
    del _L1_ffn_all

    def _L2_xattn_setup():
        import jax, jax.numpy as jnp
        import numpy as np
        key = jax.random.key(seed)
        k1, k2, k3 = jax.random.split(key, 3)
        B, S, D, M = (8, 256, 256, 128)
        hidden_states = jax.random.normal(k1, (B, S, D), dtype=jnp.float32)
        memory_tokens = jax.random.normal(k2, (B, M, D), dtype=jnp.float32)
        memory_mask = jax.random.randint(k3, (B, M), 0, 2).astype(jnp.bool_)
        return {'hidden_states': hidden_states, 'memory_tokens': memory_tokens, 'memory_mask': memory_mask}
    _L2_xattn_all = _L2_xattn_setup()
    _L2_xattn_in = {k: v for k, v in _L2_xattn_all.items() if k in ()}
    del _L2_xattn_all

    def _L2_ffn_setup():
        import jax, jax.numpy as jnp
        import numpy as np

        def binarize_weight(w):
            alpha = jnp.mean(jnp.abs(w), axis=tuple(range(1, w.ndim)), keepdims=True)
            bw = jnp.where(w >= 0, 1.0, -1.0) * alpha
            return jax.lax.stop_gradient(bw - w) + w
        key = jax.random.key(seed)
        k1, k2, k3 = jax.random.split(key, 3)
        in_features, out_features = (256, 256)
        x = jax.random.normal(k1, (8, 256, in_features), dtype=jnp.float32)
        std = np.sqrt(2.0 / out_features).astype(np.float32)
        weight = jax.random.normal(k2, (out_features, in_features), dtype=jnp.float32) * std
        bias = jax.random.normal(k3, (out_features,), dtype=jnp.float32) * 0.01
        return {'x': x, 'weight': weight, 'bias': bias}
    _L2_ffn_all = _L2_ffn_setup()
    _L2_ffn_in = {k: v for k, v in _L2_ffn_all.items() if k in ('weight', 'bias')}
    del _L2_ffn_all

    def _L3_xattn_setup():
        import jax, jax.numpy as jnp
        import numpy as np
        D_MODEL = 256
        N_HEADS = 32
        N_GROUPS = 8
        HEAD_DIM = D_MODEL // N_HEADS
        BATCH, SEQ = (2, 128)
        NEG_INF = float('-inf')
        key = jax.random.key(seed)
        ks = jax.random.split(key, 9)
        s = 0.02
        return {'Q': jax.random.normal(ks[0], (BATCH, SEQ, D_MODEL), jnp.float32), 'K': jax.random.normal(ks[1], (BATCH, SEQ, D_MODEL), jnp.float32), 'V': jax.random.normal(ks[2], (BATCH, SEQ, D_MODEL), jnp.float32), 'attention_mask': jnp.ones((BATCH, SEQ), jnp.int32), 'w_q': jax.random.normal(ks[3], (D_MODEL, D_MODEL), jnp.float32) * s, 'w_k': jax.random.normal(ks[4], (HEAD_DIM * N_GROUPS, D_MODEL), jnp.float32) * s, 'w_v': jax.random.normal(ks[5], (HEAD_DIM * N_GROUPS, D_MODEL), jnp.float32) * s, 'w_o': jax.random.normal(ks[6], (D_MODEL, D_MODEL), jnp.float32) * s, 'b_o': jnp.zeros((D_MODEL,), jnp.float32)}
    _L3_xattn_all = _L3_xattn_setup()
    _L3_xattn_in = {k: v for k, v in _L3_xattn_all.items() if k in ('w_q', 'w_k', 'w_v', 'w_o', 'b_o')}
    del _L3_xattn_all

    def _L3_ffn_setup():
        import jax, jax.numpy as jnp
        import numpy as np
        B, S, D, H = (8, 512, 256, 640)

        def ternarize_weight(w):
            abs_mean = jnp.maximum(jnp.mean(jnp.abs(w)), 1e-05)
            thr = 0.7 * abs_mean
            one = jnp.ones((), dtype=w.dtype)
            q = jnp.where(w > thr, one, jnp.where(w < -thr, -one, jnp.zeros((), dtype=w.dtype)))
            return w + jax.lax.stop_gradient(q * abs_mean - w)
        key = jax.random.key(seed)
        k1, k2, k3 = jax.random.split(key, 3)
        x = jax.random.normal(k1, (B, S, D), dtype=jnp.float32)
        w_fc = jax.random.normal(k2, (H, D), dtype=jnp.float32) / np.sqrt(D).astype(np.float32)
        w_proj = jax.random.normal(k3, (D, H), dtype=jnp.float32) / np.sqrt(H).astype(np.float32)
        return {'x': x, 'w_fc': w_fc, 'w_proj': w_proj}
    _L3_ffn_all = _L3_ffn_setup()
    _L3_ffn_in = {k: v for k, v in _L3_ffn_all.items() if k in ('w_fc', 'w_proj')}
    del _L3_ffn_all
    return {'x': x, 'ctx_2048': ctx_2048, 'itok_BxS_0_1023': itok_BxS_0_1023, 'mask_BxS2_bk0': mask_BxS2_bk0, 'mask_BxS2_if1': mask_BxS2_if1, 'L0_xattn_W_fc': _L0_xattn_in['W_fc'], 'L0_xattn_b_fc': _L0_xattn_in['b_fc'], 'L0_xattn_W_q': _L0_xattn_in['W_q'], 'L0_xattn_b_q': _L0_xattn_in['b_q'], 'L0_xattn_W_k': _L0_xattn_in['W_k'], 'L0_xattn_b_k': _L0_xattn_in['b_k'], 'L0_xattn_W_v': _L0_xattn_in['W_v'], 'L0_xattn_b_v': _L0_xattn_in['b_v'], 'L0_ffn_select_weight': _L0_ffn_in['select_weight'], 'L0_ffn_select_mean_diff': _L0_ffn_in['select_mean_diff'], 'L0_ffn_imp_center': _L0_ffn_in['imp_center'], 'L0_ffn_imp_slope': _L0_ffn_in['imp_slope'], 'L0_ffn_lora_update': _L0_ffn_in['lora_update'], 'L0_ffn_lora_degen': _L0_ffn_in['lora_degen'], 'L0_ffn_bias_w': _L0_ffn_in['bias_w'], 'L0_ffn_debias_w': _L0_ffn_in['debias_w'], 'L1_xattn_W_kvc': _L1_xattn_in['W_kvc'], 'L1_xattn_W_dq': _L1_xattn_in['W_dq'], 'L1_xattn_W_uq': _L1_xattn_in['W_uq'], 'L1_xattn_W_qr': _L1_xattn_in['W_qr'], 'L1_xattn_W_uk': _L1_xattn_in['W_uk'], 'L1_xattn_W_kr': _L1_xattn_in['W_kr'], 'L1_xattn_W_uv': _L1_xattn_in['W_uv'], 'L1_xattn_W_o': _L1_xattn_in['W_o'], 'L1_ffn_ln1_w': _L1_ffn_in['ln1_w'], 'L1_ffn_ln2_w': _L1_ffn_in['ln2_w'], 'L1_ffn_kv_d_w': _L1_ffn_in['kv_d_w'], 'L1_ffn_q_d_w': _L1_ffn_in['q_d_w'], 'L1_ffn_k_u_w': _L1_ffn_in['k_u_w'], 'L1_ffn_v_u_w': _L1_ffn_in['v_u_w'], 'L1_ffn_q_u_w': _L1_ffn_in['q_u_w'], 'L1_ffn_rope_k_w': _L1_ffn_in['rope_k_w'], 'L1_ffn_rope_q_w': _L1_ffn_in['rope_q_w'], 'L1_ffn_o_w': _L1_ffn_in['o_w'], 'L1_ffn_sh_gate': _L1_ffn_in['sh_gate'], 'L1_ffn_sh_up': _L1_ffn_in['sh_up'], 'L1_ffn_sh_down': _L1_ffn_in['sh_down'], 'L1_ffn_r_gate': _L1_ffn_in['r_gate'], 'L1_ffn_r_up': _L1_ffn_in['r_up'], 'L1_ffn_r_down': _L1_ffn_in['r_down'], 'L1_ffn_router_w': _L1_ffn_in['router_w'], 'L1_ffn_router_b': _L1_ffn_in['router_b'], 'L2_ffn_weight': _L2_ffn_in['weight'], 'L2_ffn_bias': _L2_ffn_in['bias'], 'L3_xattn_w_q': _L3_xattn_in['w_q'], 'L3_xattn_w_k': _L3_xattn_in['w_k'], 'L3_xattn_w_v': _L3_xattn_in['w_v'], 'L3_xattn_w_o': _L3_xattn_in['w_o'], 'L3_xattn_b_o': _L3_xattn_in['b_o'], 'L3_ffn_w_fc': _L3_ffn_in['w_fc'], 'L3_ffn_w_proj': _L3_ffn_in['w_proj']}

def reference(x, ctx_2048, itok_BxS_0_1023, mask_BxS2_bk0, mask_BxS2_if1, L0_xattn_W_fc, L0_xattn_b_fc, L0_xattn_W_q, L0_xattn_b_q, L0_xattn_W_k, L0_xattn_b_k, L0_xattn_W_v, L0_xattn_b_v, L0_ffn_select_weight, L0_ffn_select_mean_diff, L0_ffn_imp_center, L0_ffn_imp_slope, L0_ffn_lora_update, L0_ffn_lora_degen, L0_ffn_bias_w, L0_ffn_debias_w, L1_xattn_W_kvc, L1_xattn_W_dq, L1_xattn_W_uq, L1_xattn_W_qr, L1_xattn_W_uk, L1_xattn_W_kr, L1_xattn_W_uv, L1_xattn_W_o, L1_ffn_ln1_w, L1_ffn_ln2_w, L1_ffn_kv_d_w, L1_ffn_q_d_w, L1_ffn_k_u_w, L1_ffn_v_u_w, L1_ffn_q_u_w, L1_ffn_rope_k_w, L1_ffn_rope_q_w, L1_ffn_o_w, L1_ffn_sh_gate, L1_ffn_sh_up, L1_ffn_sh_down, L1_ffn_r_gate, L1_ffn_r_up, L1_ffn_r_down, L1_ffn_router_w, L1_ffn_router_b, L2_ffn_weight, L2_ffn_bias, L3_xattn_w_q, L3_xattn_w_k, L3_xattn_w_v, L3_xattn_w_o, L3_xattn_b_o, L3_ffn_w_fc, L3_ffn_w_proj):
    import jax
    import jax.numpy as jnp

    def _L0_xattn_ref(ref_feat, sup_feat, W_fc, b_fc, W_q, b_q, W_k, b_k, W_v, b_v):
        import jax, jax.numpy as jnp
        import numpy as np
        FEAT = 256
        G = 16
        DG = FEAT // G
        bs, N1, _ = ref_feat.shape
        sup = jax.nn.relu(sup_feat @ W_fc.T + b_fc)
        ref = jax.nn.relu(ref_feat @ W_fc.T + b_fc)
        q = (ref @ W_q.T + b_q).reshape(bs, N1, G, DG)
        k = (sup @ W_k.T + b_k).reshape(bs, -1, G, DG)
        aff = jnp.einsum('bqhd,bkhd->bhqk', q, k) * (1.0 / np.sqrt(DG))
        p = jax.nn.softmax(aff, axis=-1)
        out_h = jnp.einsum('bhqk,bkf->bhqf', p, sup)
        Wv = W_v.reshape(G, DG, FEAT)
        attn = jnp.einsum('bhqf,hjf->bqhj', out_h, Wv).reshape(bs, N1, FEAT) + b_v
        return ref + attn

    def _L0_ffn_ref(x, select_weight, select_mean_diff, imp_center, imp_slope, lora_update, lora_degen, bias_w, debias_w):
        import jax, jax.numpy as jnp
        import numpy as np
        B, T, D = (4, 128, 256)
        N, S, H = (8, 8, 8)
        ETA = 1.0
        x_diff = x[:, None, :, :] - select_mean_diff[None, :, None, :]
        x_diff = x_diff / jnp.linalg.norm(x_diff, axis=3, keepdims=True)
        cont = jnp.einsum('nds,bntd->bnts', select_weight, x_diff) ** 2
        score = cont.sum(axis=-1)
        gate = jax.nn.sigmoid(imp_slope[None, :, None] * (score - imp_center[None, :, None]))
        sel_scale = gate.max(axis=1)[..., None]
        sel_idx = gate.argmax(axis=1)
        debias = jnp.take(debias_w, sel_idx, axis=0)
        bias = jnp.take(bias_w, sel_idx, axis=0)
        upd = jnp.take(lora_update, sel_idx, axis=0)
        dgn = jnp.take(lora_degen, sel_idx, axis=0)
        x_debias = x - debias
        mod_x = jnp.einsum('btdh,btd->bth', upd, x_debias)
        degen_up = jnp.einsum('btdh,bth->btd', dgn, mod_x)
        mod_x_bias = ETA * (bias + degen_up)
        return (1.0 - sel_scale) * x + sel_scale * mod_x_bias

    def _L1_xattn_ref(q, kv, seg_id, W_kvc, W_dq, W_uq, W_qr, W_uk, W_kr, W_uv, W_o):
        import jax, jax.numpy as jnp
        import numpy as np
        B, Lq, Lk = (2, 512, 128)
        Q_DIM, KV_DIM = (256, 256)
        H, HD = (16, 128)
        KVC, QC, R = (64, 96, 64)
        LOOKBACK = 8
        NEG = -1e+30

        def _rope(x, L):
            half = x.shape[-1] // 2
            inv_freq = 1.0 / 10000.0 ** (jnp.arange(half, dtype=jnp.float32) / half)
            ang = jnp.arange(L, dtype=jnp.float32)[:, None] * inv_freq
            cos, sin = (jnp.cos(ang), jnp.sin(ang))
            x1, x2 = (x[..., :half], x[..., half:])
            return jnp.concatenate([x1 * cos - x2 * sin, x1 * sin + x2 * cos], axis=-1)
        b, lq, _ = q.shape
        lk = kv.shape[1]
        kv_c = kv @ W_kvc
        q_c = q @ W_dq
        q_nope = (q_c @ W_uq).reshape(b, lq, H, HD).transpose(0, 2, 1, 3)
        q_rope = (q_c @ W_qr).reshape(b, lq, H, R).transpose(0, 2, 1, 3)
        k_nope = (kv_c @ W_uk).reshape(b, lk, H, HD)
        v = (kv_c @ W_uv).reshape(b, lk, H, HD)
        k_rope = kv_c @ W_kr
        q_rope = _rope(q_rope, lq)
        k_rope = _rope(k_rope, lk)
        scale = 1.0 / np.sqrt(HD + R).astype(np.float32)
        scores = (jnp.einsum('bhqd,bkhd->bhqk', q_nope, k_nope) + jnp.einsum('bhqr,bkr->bhqk', q_rope, k_rope)) * scale
        k_ids = jnp.arange(lk)[None, None, :]
        qs = seg_id[:, :, None]
        good = (k_ids <= qs) & (k_ids >= qs - LOOKBACK)
        scores = jnp.where(good[:, None, :, :], scores, NEG)
        attn = jax.nn.softmax(scores, axis=-1)
        out = jnp.einsum('bhqk,bkhd->bqhd', attn, v).reshape(b, lq, H * HD)
        return out @ W_o

    def _L1_ffn_ref(x, ln1_w, ln2_w, kv_d_w, q_d_w, k_u_w, v_u_w, q_u_w, rope_k_w, rope_q_w, o_w, sh_gate, sh_up, sh_down, r_gate, r_up, r_down, router_w, router_b):
        import jax, jax.numpy as jnp
        import numpy as np
        B, S, H = (4, 128, 256)
        NH = 16
        HD = H // NH
        RD = HD // 2
        LAT = H // 4
        I = 128
        NE = 8
        NSH = 1
        NR = NE - NSH
        TOPK = 2
        EPS = 1e-05
        SCALING = 8.0

        def _w(key, shape, fan_in):
            return jax.random.normal(key, shape, dtype=jnp.float32) / np.sqrt(fan_in)

        def rmsnorm(x, w):
            rms = jax.lax.rsqrt(jnp.mean(x * x, axis=-1, keepdims=True) + EPS)
            return w * rms * x

        def rope_cos_sin(seq_len):
            inv_freq = 1.0 / 10000.0 ** (jnp.arange(0, RD, 2, dtype=jnp.float32) / RD)
            t = jnp.arange(seq_len, dtype=jnp.float32)
            ang = jnp.outer(t, inv_freq)
            emb = jnp.concatenate([ang, ang], axis=-1)
            return (jnp.cos(emb), jnp.sin(emb))

        def apply_rope(x, cos, sin):
            c = cos[None, :, None, :]
            s = sin[None, :, None, :]
            x1, x2 = jnp.split(x, 2, axis=-1)
            rot = jnp.concatenate([-x2, x1], axis=-1)
            return x * c + rot * s

        def expert_ffn(x, wg, wu, wd):
            h = jax.nn.silu(x @ wg) * (x @ wu) / SCALING
            return h @ wd

        def attention(x, kv_d_w, q_d_w, k_u_w, v_u_w, q_u_w, rope_k_w, rope_q_w, o_w):
            b, s, _ = x.shape
            kv_d = x @ kv_d_w
            q_d = x @ q_d_w
            k_p = (kv_d @ k_u_w).reshape(b, s, NH, RD)
            q_p = (q_d @ q_u_w).reshape(b, s, NH, RD)
            v = (kv_d @ v_u_w).reshape(b, s, NH, HD)
            k_r = (x @ rope_k_w).reshape(b, s, NH, RD)
            q_r = (q_d @ rope_q_w).reshape(b, s, NH, RD)
            cos, sin = rope_cos_sin(s)
            k_r = apply_rope(k_r, cos, sin)
            q_r = apply_rope(q_r, cos, sin)
            k = jnp.concatenate([k_p, k_r], axis=-1)
            q = jnp.concatenate([q_p, q_r], axis=-1)
            scale = 1.0 / np.sqrt(HD)
            scores = jnp.einsum('bqhd,bkhd->bhqk', q, k) * scale
            causal = jnp.tril(jnp.ones((s, s), dtype=bool))
            scores = jnp.where(causal[None, None], scores, jnp.finfo(scores.dtype).min)
            probs = jax.nn.softmax(scores, axis=-1)
            out = jnp.einsum('bhqk,bkhd->bqhd', probs, v).reshape(b, s, H)
            return out @ o_w

        def moe(x, sh_gate, sh_up, sh_down, r_gate, r_up, r_down, router_w, router_b):
            shared = expert_ffn(x, sh_gate, sh_up, sh_down)
            logits = x @ router_w + router_b
            probs = jax.nn.sigmoid(logits)
            scores, idx = jax.lax.top_k(probs, TOPK)
            scores = scores / jnp.sum(scores, axis=-1, keepdims=True)
            w = jnp.sum(jax.nn.one_hot(idx, NR, dtype=x.dtype) * scores[..., None], axis=-2)
            combined = jnp.zeros_like(x)
            for e in range(NR):
                combined = combined + w[..., e:e + 1] * expert_ffn(x, r_gate[e], r_up[e], r_down[e])
            return shared + combined
        h = x + attention(rmsnorm(x, ln1_w), kv_d_w, q_d_w, k_u_w, v_u_w, q_u_w, rope_k_w, rope_q_w, o_w)
        out = h + moe(rmsnorm(h, ln2_w), sh_gate, sh_up, sh_down, r_gate, r_up, r_down, router_w, router_b)
        return out

    def _L2_xattn_ref(hidden_states, memory_tokens, memory_mask):
        import jax, jax.numpy as jnp
        import numpy as np
        B, S, D = hidden_states.shape
        scale = 1.0 / jnp.sqrt(jnp.asarray(D, hidden_states.dtype))
        scores = jnp.einsum('bsd,bmd->bsm', hidden_states, memory_tokens) * scale
        neg_inf = jnp.asarray(-1e+30, scores.dtype)
        scores = jnp.where(memory_mask[:, None, :], scores, neg_inf)
        attn = jax.nn.softmax(scores, axis=-1)
        readout = jnp.einsum('bsm,bmd->bsd', attn, memory_tokens)
        valid_b = jnp.any(memory_mask, axis=-1)
        out = jnp.where(valid_b[:, None, None], readout, jnp.zeros_like(readout))
        return out

    def _L2_ffn_ref(x, weight, bias):
        import jax, jax.numpy as jnp
        import numpy as np

        def binarize_weight(w):
            alpha = jnp.mean(jnp.abs(w), axis=tuple(range(1, w.ndim)), keepdims=True)
            bw = jnp.where(w >= 0, 1.0, -1.0) * alpha
            return jax.lax.stop_gradient(bw - w) + w
        bw = binarize_weight(weight)
        return jnp.einsum('bsi,oi->bso', x, bw) + bias

    def _L3_xattn_ref(Q, K, V, attention_mask, w_q, w_k, w_v, w_o, b_o):
        import jax, jax.numpy as jnp
        import numpy as np
        D_MODEL = 256
        N_HEADS = 32
        N_GROUPS = 8
        HEAD_DIM = D_MODEL // N_HEADS
        BATCH, SEQ = (2, 128)
        NEG_INF = float('-inf')
        B, S, D = Q.shape
        G, HG, HD = (N_GROUPS, N_HEADS // N_GROUPS, HEAD_DIM)
        q = (Q @ w_q.T).reshape(B, S, G, HG, HD)
        k = (K @ w_k.T).reshape(B, S, G, HD)
        v = (V @ w_v.T).reshape(B, S, G, HD)
        scale = jnp.sqrt(jnp.float32(HD))
        scores = jnp.einsum('bnghd,bmgd->bnghm', q, k) / scale
        pad = (attention_mask == 0)[:, None, None, None, :]
        scores = jnp.where(pad, NEG_INF, scores)
        causal = jnp.tril(jnp.ones((S, S), bool))[None, :, None, None, :]
        scores = jnp.where(causal, scores, NEG_INF)
        attn = jax.nn.softmax(scores, axis=-1)
        out = jnp.einsum('bnghm,bmgd->bnghd', attn, v).reshape(B, S, D)
        return out @ w_o.T + b_o

    def _L3_ffn_ref(x, w_fc, w_proj):
        import jax, jax.numpy as jnp
        import numpy as np
        B, S, D, H = (8, 512, 256, 640)

        def ternarize_weight(w):
            abs_mean = jnp.maximum(jnp.mean(jnp.abs(w)), 1e-05)
            thr = 0.7 * abs_mean
            one = jnp.ones((), dtype=w.dtype)
            q = jnp.where(w > thr, one, jnp.where(w < -thr, -one, jnp.zeros((), dtype=w.dtype)))
            return w + jax.lax.stop_gradient(q * abs_mean - w)
        h = jnp.einsum('bsd,hd->bsh', x, ternarize_weight(w_fc))
        h = jnp.square(jax.nn.relu(h))
        return jnp.einsum('bsh,dh->bsd', h, ternarize_weight(w_proj))
    x = x + _L0_xattn_ref(_layernorm(x, axis=-1), ctx_2048, L0_xattn_W_fc, L0_xattn_b_fc, L0_xattn_W_q, L0_xattn_b_q, L0_xattn_W_k, L0_xattn_b_k, L0_xattn_W_v, L0_xattn_b_v)
    x = x + _L0_ffn_ref(_layernorm(x, axis=-1), L0_ffn_select_weight, L0_ffn_select_mean_diff, L0_ffn_imp_center, L0_ffn_imp_slope, L0_ffn_lora_update, L0_ffn_lora_degen, L0_ffn_bias_w, L0_ffn_debias_w)
    x = x + _L1_xattn_ref(_layernorm(x, axis=-1), ctx_2048, itok_BxS_0_1023, L1_xattn_W_kvc, L1_xattn_W_dq, L1_xattn_W_uq, L1_xattn_W_qr, L1_xattn_W_uk, L1_xattn_W_kr, L1_xattn_W_uv, L1_xattn_W_o)
    x = x + _L1_ffn_ref(_layernorm(x, axis=-1), L1_ffn_ln1_w, L1_ffn_ln2_w, L1_ffn_kv_d_w, L1_ffn_q_d_w, L1_ffn_k_u_w, L1_ffn_v_u_w, L1_ffn_q_u_w, L1_ffn_rope_k_w, L1_ffn_rope_q_w, L1_ffn_o_w, L1_ffn_sh_gate, L1_ffn_sh_up, L1_ffn_sh_down, L1_ffn_r_gate, L1_ffn_r_up, L1_ffn_r_down, L1_ffn_router_w, L1_ffn_router_b)
    x = x + _L2_xattn_ref(_layernorm(x, axis=-1), ctx_2048, mask_BxS2_bk0)
    x = x + _L2_ffn_ref(_layernorm(x, axis=-1), L2_ffn_weight, L2_ffn_bias)
    x = x + _L3_xattn_ref(_layernorm(x, axis=-1), ctx_2048, ctx_2048, mask_BxS2_if1, L3_xattn_w_q, L3_xattn_w_k, L3_xattn_w_v, L3_xattn_w_o, L3_xattn_b_o)
    x = x + _L3_ffn_ref(_layernorm(x, axis=-1), L3_ffn_w_fc, L3_ffn_w_proj)
    return x

_drawn_inputs = setup_inputs


def setup_inputs(seed=0):
    import zlib

    import numpy as np

    out = dict(_drawn_inputs(seed))
    spreads = {'L0_xattn_b_fc': (0.0, 0.1),
     'L0_xattn_b_q': (0.0, 0.8),
     'L0_xattn_b_k': (0.0, 0.8),
     'L0_xattn_b_v': (0.0, 0.1),
     'L1_ffn_ln1_w': (1.0, 0.2),
     'L1_ffn_ln2_w': (1.0, 0.6),
     'L1_ffn_router_b': (0.0, 0.8),
     'L3_xattn_b_o': (0.0, 0.1)}
    factors = {'L0_xattn_W_q': 8.0,
     'L0_xattn_W_k': 8.0,
     'L0_ffn_select_weight': 8.0,
     'L0_ffn_imp_slope': 2.708,
     'L0_ffn_lora_update': 4.217,
     'L0_ffn_lora_degen': 4.078,
     'L0_ffn_bias_w': 3.666,
     'L0_ffn_debias_w': 8.0,
     'L1_ffn_r_gate': 2.733,
     'L1_ffn_router_w': 2.983,
     'L2_ffn_bias': 8.0,
     'L3_xattn_w_q': 8.0,
     'L3_xattn_w_k': 8.0,
     'L3_xattn_w_v': 2.977,
     'L3_xattn_w_o': 3.014}
    for name, (base, spread) in spreads.items():
        noise = np.random.default_rng([zlib.crc32(name.encode()), seed]).standard_normal(out[name].shape)
        drawn = base * np.exp(spread * noise) if base else spread * noise
        out[name] = jnp.asarray(drawn.astype(out[name].dtype))
    for name, factor in factors.items():
        out[name] = (out[name] * factor).astype(out[name].dtype)
    return out
```

```python
from contextlib import ExitStack

import numpy as np

import concourse.bass as bass
from concourse import mybir

F32 = mybir.dt.float32
BF16 = mybir.dt.bfloat16
I32 = mybir.dt.int32
U8 = mybir.dt.uint8
ALU = mybir.AluOpType
ACT = mybir.ActivationFunctionType
X_AXIS = mybir.AxisListType.X

P = 128
SEQUENCES, TOKENS, WIDTH = 16, 128, 256
KB = WIDTH // P
STREAMS = 4
ROUNDS = SEQUENCES // STREAMS
EPS = 1e-5
MASKED = -1e30
LAYERS = 8
STEPS = 1024

H0, HD0 = 16, 16
N_SEL, SEL, LORA = 8, 8, 8
H1, HD1, KVC, QC, ROPE = 16, 128, 64, 96, 64
LOOKBACK = 8
LF, RD, LATENT = 16, 8, 64
EXPERTS, INNER, EXPERT_SCALE = 8, 128, 8.0
H3, HD3, G3 = 32, 8, 8
HPG = H3 // G3
FF3 = 640
FB3 = FF3 // P
SLOT = 32
GROUP = 8

ROW_NAMES = [("b_v", WIDTH), ("ln1", WIDTH), ("ln2", WIDTH), ("bias2", WIDTH), ("b_o", WIDTH),
             ("router_b", EXPERTS), ("center", N_SEL), ("slope", N_SEL)]
CONST_NAMES = [("ident", P), ("even", 1), ("odd", 1), ("quarter", HPG), ("key", P), ("falling", EXPERTS),
               ("cos_q", ROPE), ("sin_q", ROPE), ("cos_kT", P), ("sin_kT", P), ("cos_f", RD), ("sin_f", RD)]
W0_NAMES = [("fc", KB * WIDTH), ("q", KB * WIDTH), ("k", KB * WIDTH), ("v", KB * WIDTH),
            ("b_fc", KB), ("b_q", KB), ("b_k", KB)]
SELW = N_SEL * SEL + N_SEL * LORA + N_SEL
W0F_NAMES = [("sel", KB * SELW), ("debias", KB * N_SEL), ("lift", WIDTH)]
W1_NAMES = [("kvc", KB * KVC), ("dq", KB * QC)]
W1P_NAMES = [("uqT", H1 * QC), ("ukT", H1 * KVC), ("uvT", H1 * KVC), ("o", H1 * WIDTH),
             ("kvcT", KB * P), ("qr", H1 * ROPE), ("kr", 2 * ROPE)]
W1F_NAMES = [("down_kq", KB * P), ("up", 3 * P + WIDTH), ("rope_k", KB * P), ("o", KB * WIDTH),
             ("router", KB * EXPERTS)]
WM_NAMES = [("gate_up", KB * EXPERTS * 2 * INNER), ("down", EXPERTS * WIDTH)]
W3_NAMES = [("q", KB * WIDTH), ("k", KB * WIDTH), ("v", KB * G3 * HD3), ("o", KB * WIDTH)]
W3F_NAMES = [("fc", KB * FF3), ("proj", FB3 * WIDTH)]


def width(names):
    return sum(n for _, n in names)


def columns(tile, names):
    out, at = {}, 0
    for name, n in names:
        out[name] = tile[:, at:at + n]
        at += n
    return out


def blocks(ap, n):
    return ap.rearrange("p (b n) -> p b n", b=n)


class Ring:

    def __init__(self, jobs, slots):
        self.place, self.uses = {}, [0] * slots
        for n, job in enumerate(jobs):
            assert job not in self.place, job
            self.uses[n % slots] += 1
            self.place[job] = (n % slots, self.uses[n % slots])


def each(*names):
    return [(name, s) for name in names for s in range(STREAMS)]


def units(groups):
    return [(s, g) for s in range(STREAMS) for g in range(groups)]


TAGS = ["0", "0f", "1", "1f", "2", "2f", "3", "3f"]


def program(nc, A, layers=LAYERS):
    tags = TAGS[:layers]
    FINAL = {"0": "0 ref rows", "0f": "0f mod", "1": "1 out", "1f": "1f moe", "2": "2 av", "2f": "2f out", "3": "3 out", "3f": "3f out"}[tags[-1]]

    def attn(layer, groups, per=1):
        return [(f"{layer} av", s, g, a) for s, g in units(groups) for a in range(per)]

    def narrow_attn(layer, groups):
        order = units(groups)
        return [job for t in range(len(order) + 1)
                for job in ([(f"{layer} av",) + order[t]] if t < len(order) else [])
                + ([(f"{layer} ao",) + order[t - 1]] if t else [])]

    general_jobs = (
        each("0 sup", "0 zT", "0 ref", "0 k", "0 v", "0 q") + narrow_attn("0", 2) + each("0 ref rows")
        + each("0f zT", "0f sel") + each("0f mod")
        + each("1 k", "1 kv", "1 zT", "1 qc") + attn("1", 2, 2) + each("1 out")
        + each("1f zT", "1f kq") + narrow_attn("1f", 2) + each("1f out", "1f router", "1f moe")
        + each("2 zT") + attn("2", 1) + each("2f zT", "2f out")
        + each("3 k", "3 v", "3 zT", "3 q") + narrow_attn("3", 4) + each("3 out")
        + each("3f zT", "3f out"))
    score_jobs = (
        [("0 s",) + u for u in units(2)] + [("1 q",) + u for u in units(2)] + [("1 s",) + u for u in units(2)]
        + each("1f rows") + [("1f s",) + u for u in units(2)] + [("1f gu",) + u for u in units(2)]
        + [("2 s",) + u for u in units(1)] + [("3 s",) + u for u in units(4)] + each("3f h"))
    turn_jobs = (
        [("0 t",) + u + (a,) for u in units(2) for a in range(2)] + each("0f onehot")
        + [("1 q",) + u + (a,) for u in units(2) for a in range(2)]
        + [("1 t",) + u + (a,) for u in units(2) for a in range(2)]
        + [("1 o", s, a) for s in range(STREAMS) for a in range(2)]
        + each("1f qk") + [("1f t",) + u + (a,) for u in units(2) for a in range(2)] + each("1f o", "1f h")
        + [("1f m",) + u for u in units(2)]
        + [("2 t",) + u + (0,) for u in units(1)] + [("3 t",) + u + (a,) for u in units(4) for a in range(2)]
        + each("3 o"))
    def kept(jobs):
        return [j for j in jobs if (j if isinstance(j, str) else j[0]).split()[0] in tags]

    general, score, turn = (Ring(kept(jobs), 2) for jobs in (general_jobs, score_jobs, turn_jobs))
    powers = [(n, s) for n in kept(["0", "0f", "1", "1f", "1f rms", "1f h", "2", "2f", "3", "3f"]) for s in range(STREAMS)]
    normalised = [(n, s) for n in tags for s in range(STREAMS)]
    biased = [(n, s) for n in kept(["0", "1f", "2f", "3"]) for s in range(STREAMS)]
    weighted_rows = [(n, s) for n in kept(["1f z", "1f h"]) for s in range(STREAMS)]
    act_reads = kept([("1 q",) + u for u in units(2)] + each("1f rows"))
    attention = [(tag, s, g) for tag, groups in (("0", 2), ("1", 2), ("1f", 2), ("2", 1), ("3", 4)) if tag in tags
                 for s, g in units(groups)]
    prob_jobs = [(tag, s, g, a) for tag, s, g in attention for a in range(1 if tag == "2" else 2)]

    with ExitStack() as ctx:
        def sb(name, cols, dt=F32):
            return ctx.enter_context(nc.sbuf_tensor(name, [P, cols], dt))

        def sem(name):
            return ctx.enter_context(nc.semaphore(name))

        const = sb("const", width(CONST_NAMES))
        C = columns(const, CONST_NAMES)
        constb = sb("constb", 2 * P, BF16)
        ident_b, causal_b = constb[:, 0:P], constb[:, P:2 * P]
        rows = sb("rows", width(ROW_NAMES))
        R = columns(rows, ROW_NAMES)
        w0, w0f, w1 = sb("w0", width(W0_NAMES)), sb("w0f", width(W0F_NAMES)), sb("w1", width(W1_NAMES))
        w1f, wm = sb("w1f", width(W1F_NAMES)), sb("wm", width(WM_NAMES))
        w2f = sb("w2f", KB * WIDTH)
        w3, w3f = sb("w3", width(W3_NAMES)), sb("w3f", width(W3F_NAMES))
        W0, W0F, W1, W1F = columns(w0, W0_NAMES), columns(w0f, W0F_NAMES), columns(w1, W1_NAMES), columns(w1f, W1F_NAMES)
        WM, W3, W3F = columns(wm, WM_NAMES), columns(w3, W3_NAMES), columns(w3f, W3F_NAMES)
        w_query = sb("w_query", H1 * P)
        w_kv = sb("w_kv", KB * P)
        w_kv_swap = sb("w_kv_swap", KB * ROPE)
        w_out = sb("w_out", H1 // 2 * WIDTH)
        sel_const = sb("sel_const", P + N_SEL)
        ones = sb("ones", P)
        minus_half = sb("minus_half", 1)

        def per_stream(name, cols, dt=F32):
            return [sb(f"{name}{s}", cols, dt) for s in range(STREAMS)]
        x_in, x, z = (per_stream(n, WIDTH) for n in ("x_in", "x", "z"))
        zT = per_stream("zT", WIDTH)
        cx, cxT = per_stream("cx", WIDTH + 2), per_stream("cxT", WIDTH)
        tA, tB = (per_stream(n, WIDTH) for n in ("tA", "tB"))
        hres, headsT, hrow = tA, tA, tB
        big = per_stream("big", 2048)
        heads_out = [b[:, 1024:2048] for b in big]
        values = per_stream("values", H0 * SLOT)
        values1 = per_stream("values1", KVC + 1)
        qcT, kcT = per_stream("qcT", P), per_stream("kcT", P)
        sel = per_stream("sel", P + 4 * N_SEL)
        onehot, onehotT = per_stream("onehot", P), per_stream("onehotT", P)
        stats = per_stream("stats", 6)
        mean_var = per_stream("mean_var", 2)
        var_eps, rstd = per_stream("var_eps", 1), per_stream("rstd", 1)
        small = per_stream("small", 112)
        expert_w = per_stream("expert_w", EXPERTS)
        seg_i, keep_i, pad_i = sb("seg_i", STREAMS, I32), sb("keep_i", STREAMS * P, U8), sb("pad_i", STREAMS * P, I32)
        seg_f, seg_lo = sb("seg_f", STREAMS), sb("seg_lo", STREAMS)
        valid = sb("valid", STREAMS)
        above, below = sb("above", STREAMS * P), sb("below", STREAMS * P)
        mask1, mask2, mask3 = (per_stream(n, P, BF16) for n in ("mask1", "mask2", "mask3"))
        shifted = sb("shifted", 2 * GROUP * P)
        probs = sb("probs", 4 * 4 * P)
        narrow_out = sb("narrow_out", 2 * GROUP * SLOT)
        peak = sb("peak", 2 * GROUP)
        inverse = sb("inverse", 2 * GROUP)
        q_rows, q_swap = shifted, probs
        tiny = sb("tiny", 9)

        score_psum = [ctx.enter_context(nc.psum_tensor(f"score_psum{i}", [P, 1024], F32)) for i in range(2)]
        turn_psum = [ctx.enter_context(nc.psum_tensor(f"turn_psum{i}", [P, 512], F32)) for i in range(2)]
        general_psum = [ctx.enter_context(nc.psum_tensor(f"general_psum{i}", [P, 512], F32)) for i in range(2)]

        for ring, name, banks in ((score, "score", score_psum), (turn, "turn", turn_psum), (general, "general", general_psum)):
            ring.banks = banks
            ring.filled = [sem(f"{name}_filled{i}") for i in range(2)]
            ring.emptied = [sem(f"{name}_emptied{i}") for i in range(2)]

        loaded = {n: sem(f"{n}_loaded") for n in
                  ["w0", "w0f", "w1", "w1f", "wm", "w2f", "w3", "w3f", "const", "constb", "rows", "prep"]}
        x_loaded, cx_loaded, cxT_loaded = ([sem(f"{n}_loaded{s}") for s in range(STREAMS)] for n in ("x", "cx", "cxT"))
        masks_loaded, x_stored = sem("masks_loaded"), sem("x_stored")
        prep_filled, prep_steps, prep_done = sem("prep_filled"), sem("prep_steps"), sem("prep_done")
        vec_steps = sem("vec_steps")
        power_in, power_out = sem("power_in"), sem("power_out")
        z_ready = sem("z_ready")
        x_biased = sem("x_biased")
        act_read = sem("act_read")
        q_rotated, qk_ready = sem("q_rotated"), sem("qk_ready")
        gates_in, gates_exp = sem("gates_in"), sem("gates_exp")
        z_squared, h_squared = sem("z_squared"), sem("h_squared")
        onehot_ready = sem("onehot_ready")
        rows_ready = sem("rows_ready")
        router_exp = sem("router_exp")
        tanh_done = sem("tanh_done")
        relu_squared = sem("relu_squared")
        mask_steps, masks_ready = sem("mask_steps"), sem("masks_ready")
        ones_ready, holds = sem("ones_ready"), sem("holds")

        def count(r, events, *event):
            return r * len(events) + events.index(event) + 1

        def nth(r, s):
            return r * STREAMS + s + 1

        waited = {}

        def wait_slot(eng, semaphore, r, uses, k):
            if waited.get((eng, semaphore.name), 0) < k:
                waited[eng, semaphore.name] = k
                eng.wait_ge(semaphore, r * uses + k)

        def filled(eng, ring, r, *job):
            slot, k = ring.place[job]
            wait_slot(eng, ring.filled[slot], r, ring.uses[slot], k)
            return ring.banks[slot]

        def hold(eng):
            eng.sem_inc(holds, 1)

        def free(eng, ring, r, *job):
            slot, k = ring.place[job]
            wait_slot(eng, ring.emptied[slot], r, ring.uses[slot], k)
            return ring.banks[slot]

        def moved(eng, ring, r, *job):
            slot, k = ring.place[job]
            wait_slot(eng, ring.emptied[slot], r, ring.uses[slot], k + 1)

        def all_moved(eng, ring, r, jobs):
            for job in sorted(jobs, key=lambda job: -ring.place[job][1]):
                moved(eng, ring, r, *job)

        def emptied(ring, *job):
            return ring.emptied[ring.place[job][0]]

        def round_over(eng, r):
            for slot in range(2):
                eng.wait_ge(general.emptied[slot], r * general.uses[slot] + 1)

        def fill(ring, *job):
            return ring.filled[ring.place[job][0]]

        def heads(ap, n):
            return ap.rearrange("p (h n) -> p h n", h=n)

        def spread(ap, n):
            return ap.unsqueeze(2).to_broadcast([P, ap.shape[1], n])

        def repeat(ap, n):
            return ap.unsqueeze(1).to_broadcast([P, n, ap.shape[1]])

        def same_slot_before(tag, s, g):
            at = attention.index((tag, s, g))
            slot = score.place[(f"{tag} s", s, g)][0]
            for u in reversed(attention[:at]):
                if score.place[(f"{u[0]} s", u[1], u[2])][0] == slot:
                    return u
            return None

        def last_turn(tag, s, g):
            return (f"{tag} t", s, g, 0 if tag == "2" else 1)

        def small_head(g, i):
            q, c, e = i // 4, (i % 4) // 2, i % 2
            return c * 8 + 4 * g + 2 * q + e

        W1P = {"uqT": big[0][:, 0:H1 * QC], "ukT": big[1][:, 0:H1 * KVC], "uvT": big[1][:, 1024:1024 + H1 * KVC],
               "o0": big[2][:, :], "o1": big[3][:, :],
               "kvcT": shifted[:, 0:KB * P], "qr": shifted[:, 256:256 + H1 * ROPE], "kr": shifted[:, 1280:1280 + 2 * ROPE]}
        w2f_rows = shifted[:, 1408:1408 + KB * WIDTH]
        sel_prod = big[0][:, H1 * QC:H1 * QC + KB * SELW]
        alpha, total, ternary = inverse[:, 0:KB], inverse[:, 2:4], inverse[:, 4:10]

        block = ctx.enter_context(nc.Block())

        @block.sync
        def _(sp):
            sp.dma_start(const[:, :], A["const"]).then_inc(loaded["const"], 16)
            sp.dma_start(w1[:, :], A["w1"]).then_inc(loaded["w1"], 16)
            at = 0
            for part in W1P.values():
                cols = part.shape[1]
                sp.dma_start(part, A["w1p"][:, at:at + cols]).then_inc(loaded["prep"], 16)
                at += cols
            sp.dma_start(w0f[:, :], A["w0f"]).then_inc(loaded["w0f"], 16)
            sp.dma_start(w2f_rows[:, :], A["w2f"]).then_inc(loaded["w2f"], 16)
            sp.dma_start(w3f[:, :], A["w3f"]).then_inc(loaded["w3f"], 16)
            sp.dma_start(constb[:, :], A["constb"]).then_inc(loaded["constb"], 16)
            sp.dma_start(rows[:, :], A["rows"].partition_broadcast(P)).then_inc(loaded["rows"], 16)
            sp.dma_start(w0[:, :], A["w0"]).then_inc(loaded["w0"], 16)
            with sp.Fori(0, ROUNDS) as r:
                round_over(sp, r)
                hold(sp)
                for s in range(STREAMS):
                    own = bass.ds(r * STREAMS + s, 1)
                    sp.dma_start(cxT[s][:, :], A["ctxT"][own].squeeze(0)).then_inc(cxT_loaded[s], 16)
                    sp.dma_start(x_in[s][:, :], A["x"][own].squeeze(0)).then_inc(x_loaded[s], 16)
                    sp.dma_start(cx[s][:, 0:WIDTH], A["ctx"][own].squeeze(0)).then_inc(cx_loaded[s], 16)
                now = bass.ds(r, 1)
                sp.dma_start(seg_i[:, :], A["seg"][now].squeeze(0)).then_inc(masks_loaded, 16)
                sp.dma_start(keep_i[:, :], A["keep"][now].to_broadcast([P, STREAMS * P])).then_inc(masks_loaded, 16)
                sp.dma_start(pad_i[:, :], A["pad"][now].to_broadcast([P, STREAMS * P])).then_inc(masks_loaded, 16)
                for s in range(STREAMS):
                    moved(sp, general, r, FINAL, s)
                    hold(sp)
                    sp.dma_start(A["out"][bass.ds(r * STREAMS + s, 1)].squeeze(0), x[s][:, :]).then_inc(x_stored, 16)
                sp.wait_ge(x_stored, r * (16 * STREAMS) + 16 * STREAMS)
                hold(sp)

        @block.gpsimd
        def _(pool):
            for name in ("wm", "w1f", "w3"):
                tile = {"wm": wm, "w1f": w1f, "w3": w3}[name]
                pool.dma_start(tile[:, :], A[name]).then_inc(loaded[name], 16)
            nc.gpsimd.memset(minus_half[:, :], -0.5)
            for s in range(STREAMS):
                for tile in (values[s], values1[s]):
                    nc.gpsimd.memset(tile[:, :], 1.0)
                nc.gpsimd.memset(cx[s][:, WIDTH:WIDTH + 2], 1.0)
                nc.gpsimd.memset(onehot[s][:, :], 0.0)
                nc.gpsimd.memset(expert_w[s][:, :], 0.5 / EXPERT_SCALE)
            nc.gpsimd.memset(ones[:, :], 1.0).then_inc(ones_ready, 1)
            pool.wait_ge(ones_ready, 1)
            for name in ("const", "constb", "rows"):
                pool.wait_ge(loaded[name], 16)

            def power(r, name):
                for s in range(STREAMS):
                    pool.wait_ge(power_in, count(r, powers, name, s))
                    nc.gpsimd.tensor_tensor(rstd[s][:, :], var_eps[s][:, :], minus_half[:, :], ALU.pow).then_inc(power_out, 1)

            def add_bias(r, tag, tile, bias):
                for s in range(STREAMS):
                    pool.wait_ge(z_ready, count(r, normalised, tag, s))
                    nc.gpsimd.tensor_tensor(tile[s][:, :], tile[s][:, :], bias, ALU.add).then_inc(x_biased, 1)

            with pool.Fori(0, ROUNDS) as r:
                power(r, "0")
                pool.wait_ge(masks_loaded, r * 48 + 48)
                hold(pool)
                nc.gpsimd.tensor_copy(seg_f[:, :], seg_i[:, :]).then_inc(mask_steps, 1)
                pool.wait_ge(mask_steps, r * 3 + 1)
                hold(pool)
                nc.gpsimd.tensor_scalar(seg_lo[:, :], seg_f[:, :], float(LOOKBACK), None, ALU.subtract)
                for s in range(STREAMS):
                    own = slice(s * P, s * P + P)
                    nc.gpsimd.tensor_scalar(above[:, own], C["key"], seg_f[:, s:s + 1], MASKED, ALU.is_gt, ALU.mult)
                    nc.gpsimd.tensor_scalar(mask2[s][:, :], keep_i[:, own], 1.0, -MASKED, ALU.subtract, ALU.mult)
                    ins = nc.gpsimd.tensor_scalar(mask3[s][:, :], pad_i[:, own], 0.0, MASKED, ALU.is_equal, ALU.mult)
                ins.then_inc(mask_steps, 1)
                pool.wait_ge(mask_steps, r * 3 + 2)
                hold(pool)
                for s in range(STREAMS):
                    own = slice(s * P, s * P + P)
                    ins = nc.gpsimd.tensor_scalar(below[:, own], C["key"], seg_lo[:, s:s + 1], MASKED, ALU.is_lt, ALU.mult)
                ins.then_inc(mask_steps, 1)
                for s in range(STREAMS):
                    nc.gpsimd.tensor_tensor(mask3[s][:, :], mask3[s][:, :], causal_b, ALU.add)
                pool.wait_ge(mask_steps, r * 3 + 3)
                for s in range(STREAMS):
                    own = slice(s * P, s * P + P)
                    ins = nc.gpsimd.tensor_tensor(mask1[s][:, :], above[:, own], below[:, own], ALU.add)
                ins.then_inc(masks_ready, 1)
                add_bias(r, "0", x_in, R["b_v"])
                if "0f" in tags:
                    power(r, "0f")
                if "1" in tags:
                    power(r, "1")
                if "1f" in tags:
                    power(r, "1f")
                    power(r, "1f rms")
                    power(r, "1f h")
                    for s in range(STREAMS):
                        moved(pool, general, r, "1f out", s)
                        nc.gpsimd.tensor_tensor(x[s][:, :], x[s][:, :], hres[s][:, :], ALU.add).then_inc(x_biased, 1)
                if "2" in tags:
                    power(r, "2")
                if "2f" in tags:
                    power(r, "2f")
                    add_bias(r, "2f", x, R["bias2"])
                if "3" in tags:
                    power(r, "3")
                    add_bias(r, "3", x, R["b_o"])
                if "3f" in tags:
                    power(r, "3f")

        @block.scalar
        def _(act):
            for name in ("const", "w0"):
                act.wait_ge(loaded[name], 16)
            act.wait_ge(prep_done, 3)

            def copy_out(r, ring, job, out, source=lambda bank: bank[:, :]):
                bank = filled(act, ring, r, *job)
                nc.scalar.activation(out, source(bank), ACT.Copy).then_inc(emptied(ring, *job), 1)

            def turned(r, name):
                for s in range(STREAMS):
                    copy_out(r, general, (name, s), zT[s][:, :], lambda bank: bank[:, 0:WIDTH])

            def biased_blocks(r, name, out, func, bias):
                for s in range(STREAMS):
                    bank = filled(act, general, r, name, s)
                    for b in range(KB):
                        ins = nc.scalar.activation(out[s][:, b * P:b * P + P], bank[:, b * P:b * P + P], func,
                                                   bias=bias[:, b:b + 1], scale=1.0)
                    ins.then_inc(emptied(general, name, s), 1)

            def copy_narrow(r, tag, u, unit):
                at = u % 2 * GROUP * SLOT
                copy_out(r, general, (f"{tag} av",) + unit, narrow_out[:, at:at + GROUP * SLOT], lambda bank: bank[:, 0:GROUP * SLOT])

            def exponentials(r, tag, groups, scale, turns=2, per_turn=4, narrow=True):
                order = units(groups)
                for u, (s, g) in enumerate(order):
                    for a in range(turns):
                        job = (f"{tag} t", s, g, a)
                        n = prob_jobs.index((tag, s, g, a))
                        if n >= 4:
                            before = prob_jobs[n - 4]
                            filled(act, general, r, f"{before[0]} av", before[1], before[2], *([before[3]] if before[0] in "12" else []))
                        bank = filled(act, turn, r, *job)
                        at = (n % 4) * 512
                        nc.scalar.activation(probs[:, at:at + per_turn * P], bank[:, 0:per_turn * P], ACT.Exp,
                                             scale=scale).then_inc(emptied(turn, *job), 1)
                    if narrow and u:
                        copy_narrow(r, tag, u - 1, order[u - 1])
                if narrow:
                    copy_narrow(r, tag, len(order) - 1, order[-1])

            with act.Fori(0, ROUNDS) as r:
                biased_blocks(r, "0 sup", tB, ACT.Relu, W0["b_fc"])
                turned(r, "0 zT")
                biased_blocks(r, "0 ref", tA, ACT.Relu, W0["b_fc"])
                for s in range(STREAMS):
                    copy_out(r, general, ("0 v", s), heads(values[s][:, :], H0)[:, :, 0:HD0],
                             lambda bank: heads(bank[:, 0:WIDTH], H0))
                biased_blocks(r, "0 q", zT, ACT.Identity, W0["b_q"])
                exponentials(r, "0", 2, HD0 ** -0.5)
                if "0f" in tags:
                    for s in range(STREAMS):
                        act.wait_ge(z_ready, count(r, normalised, "0f", s))
                        nc.scalar.activation(tB[s][:, :], z[s][:, :], ACT.Square,
                                             accum_out=small[s][:, 106:107]).then_inc(z_squared, 1)
                    turned(r, "0f zT")
                    for s in range(STREAMS):
                        act.wait_ge(gates_in, nth(r, s))
                        nc.scalar.activation(small[s][:, 88:96], small[s][:, 80:88], ACT.Exp, scale=-1.0).then_inc(gates_exp, 1)
                    for s in range(STREAMS):
                        copy_out(r, turn, ("0f onehot", s), onehotT[s][:, :], lambda bank: bank[:, 0:P])
                if "1" in tags:
                    for s in range(STREAMS):
                        copy_out(r, general, ("1 kv", s), values1[s][:, 0:KVC], lambda bank: bank[:, 0:KVC])
                    turned(r, "1 zT")
                    for s in range(STREAMS):
                        copy_out(r, general, ("1 qc", s), qcT[s][0:QC, :], lambda bank: bank[0:QC, 0:P])
                    order = units(2)
                    for t in range(len(order) + 1):
                        if t < len(order):
                            s, g = order[t]
                            slot = score.place[("1 q", s, g)][0]
                            if t >= 2:
                                filled(act, turn, r, "1 q", *order[t - 2], 1)
                            bank = filled(act, score, r, "1 q", s, g)
                            nc.scalar.activation(heads(q_rows[:, slot * 1024:(slot + 1) * 1024], GROUP)[:, :, 0:KVC],
                                                 heads(bank[:, :], GROUP)[:, :, 0:KVC], ACT.Copy).then_inc(act_read, 1)
                        if t >= 1:
                            s, g = order[t - 1]
                            for a in range(2):
                                at = (g * GROUP + a * 4) * P
                                copy_out(r, turn, ("1 q", s, g, a), big[s][:, at:at + 512])
                    exponentials(r, "1", 2, float((HD1 + ROPE) ** -0.5), narrow=False)
                    for s in range(STREAMS):
                        for a in range(2):
                            copy_out(r, turn, ("1 o", s, a), big[s][:, a * 1024 + 512:(a + 1) * 1024])
                if "1f" in tags:
                    turned(r, "1f zT")
                    for s in range(STREAMS):
                        copy_out(r, general, ("1f kq", s), qcT[s][:, :], lambda bank: bank[:, 0:P])
                    for s in range(STREAMS):
                        bank = filled(act, score, r, "1f rows", s)
                        nc.scalar.activation(heads(heads_out[s][:, 0:512], 2 * LF)[:, :, 0:RD],
                                             heads(bank[:, 0:2 * P], 2 * LF), ACT.Copy)
                        nc.scalar.activation(heads(values[s][:, :], LF)[:, :, 0:2 * RD],
                                             heads(bank[:, 512:512 + WIDTH], LF), ACT.Copy).then_inc(act_read, 1)
                    exponentials(r, "1f", 2, (2 * RD) ** -0.5)
                    for s in range(STREAMS):
                        copy_out(r, turn, ("1f o", s), headsT[s][:, :], lambda bank: bank[:, 0:WIDTH])
                    for s in range(STREAMS):
                        moved(act, general, r, "1f out", s)
                        nc.scalar.activation(tB[s][:, :], hres[s][:, :], ACT.Square,
                                             accum_out=small[s][:, 106:107]).then_inc(h_squared, 1)
                    for s in range(STREAMS):
                        copy_out(r, turn, ("1f h", s), zT[s][:, :], lambda bank: bank[:, 0:WIDTH])
                    for s in range(STREAMS):
                        moved(act, general, r, "1f router", s)
                        nc.scalar.activation(small[s][:, 8:16], small[s][:, 0:8], ACT.Exp, scale=-1.0).then_inc(router_exp, 1)
                    order = units(2)
                    for t in range(len(order) + 1):
                        if t < len(order):
                            s, g = order[t]
                            slot = score.place[("1f gu", s, g)][0]
                            bank = filled(act, score, r, "1f gu", s, g)
                            gate = bank[:, :].rearrange("p (e u n) -> p e u n", e=4, u=2)[:, :, 0, :]
                            nc.scalar.activation(heads(q_rows[:, slot * 1024:slot * 1024 + 512], 4), gate, ACT.Tanh,
                                                 scale=0.5).then_inc(tanh_done, 1)
                        if t >= 1:
                            s, g = order[t - 1]
                            copy_out(r, turn, ("1f m", s, g), big[s][:, 1024 + g * 512:1536 + g * 512])
                if "2" in tags:
                    turned(r, "2 zT")
                    exponentials(r, "2", 1, WIDTH ** -0.5, turns=1, per_turn=1, narrow=False)
                if "2f" in tags:
                    turned(r, "2f zT")
                if "3" in tags:
                    for s in range(STREAMS):
                        copy_out(r, general, ("3 v", s), heads(values[s][:, 0:G3 * SLOT], G3)[:, :, 0:HD3],
                                 lambda bank: heads(bank[:, 0:G3 * HD3], G3))
                    turned(r, "3 zT")
                    for s in range(STREAMS):
                        copy_out(r, general, ("3 q", s), zT[s][:, :], lambda bank: bank[:, 0:WIDTH])
                    exponentials(r, "3", 4, HD3 ** -0.5)
                    for s in range(STREAMS):
                        copy_out(r, turn, ("3 o", s), headsT[s][:, :], lambda bank: bank[:, 0:WIDTH])
                if "3f" in tags:
                    turned(r, "3f zT")
                    for s in range(STREAMS):
                        bank = filled(act, score, r, "3f h", s)
                        nc.scalar.activation(big[s][:, 0:FF3], bank[:, 0:FF3], ACT.Relu).then_inc(emptied(score, "3f h", s), 1)

        @block.vector
        def _(vec):
            steps, marks = [0], {}

            def prep(ins):
                steps[0] += 1
                ins.then_inc(prep_steps, 1)
                vec.wait_ge(prep_steps, steps[0])

            V = nc.vector
            for name in ("const", "w0f", "w1", "w2f", "w3f"):
                vec.wait_ge(loaded[name], 16)
            vec.wait_ge(loaded["prep"], 16 * len(W1P))
            for b in range(KB):
                w = W0F["sel"][:, b * SELW:(b + 1) * SELW]
                mean = w[:, P:P + N_SEL]
                out = sel_prod[:, b * SELW:(b + 1) * SELW]
                V.tensor_tensor(heads(out[:, 0:64], N_SEL), heads(w[:, 0:64], N_SEL), spread(mean, SEL), ALU.mult)
                V.tensor_tensor(heads(out[:, 64:128], N_SEL), heads(w[:, 64:128], N_SEL),
                                spread(W0F["debias"][:, b * N_SEL:(b + 1) * N_SEL], LORA), ALU.mult)
                prep(V.tensor_tensor(out[:, P:P + N_SEL], mean, mean, ALU.mult))
            V.tensor_copy(heads(w_query[0:QC, :], H1)[:, :, KVC:P], heads(W1P["qr"][0:QC, :], H1))
            V.tensor_copy(heads(w_kv[:, :], KB)[:, :, 0:KVC], heads(W1["kvc"], KB))
            tmp = probs[:, 0:KB * WIDTH]
            w = w2f_rows[:, :]
            prep(V.scalar_tensor_tensor(out=tmp, in0=w, scalar=-1.0, in1=w, op0=ALU.mult, op1=ALU.max))
            prep(V.tensor_reduce(alpha, heads(tmp, KB), X_AXIS, ALU.add))
            prep(V.tensor_scalar(alpha, alpha, 1.0 / WIDTH, None, ALU.mult))
            prep(V.tensor_scalar(tmp, w, 0.0, 2.0, ALU.is_ge, ALU.mult))
            for b in range(KB):
                own = slice(b * WIDTH, (b + 1) * WIDTH)
                ins = V.tensor_scalar(tmp[:, own], tmp[:, own], -1.0, alpha[:, b:b + 1], ALU.add, ALU.mult)
            prep(ins)
            prep(V.tensor_tensor(tmp, tmp, w, ALU.subtract))
            prep(V.tensor_tensor(w, tmp, w, ALU.add))
            for i, (w, tmp) in enumerate(((W3F["fc"], probs[:, 0:KB * FF3]), (W3F["proj"], probs[:, 0:FB3 * WIDTH]))):
                prep(V.scalar_tensor_tensor(out=tmp, in0=w, scalar=-1.0, in1=w, op0=ALU.mult, op1=ALU.max))
                prep(V.tensor_reduce(total[:, i:i + 1], tmp, X_AXIS, ALU.add))
            V.memset(tiny[:, 0:1], 0.0).then_inc(prep_done, 1)
            vec.wait_ge(prep_filled, 1)
            V.tensor_copy(sel_const[:, :], general_psum[0][:, 0:SELW])
            scale, thr, low = (ternary[:, i:i + 2] for i in (0, 2, 4))
            prep(V.tensor_scalar(scale, general_psum[0][:, SELW:SELW + 2], 1.0 / (FF3 * WIDTH), 1e-5, ALU.mult, ALU.max))
            V.tensor_scalar(thr, scale, 0.7, None, ALU.mult)
            prep(V.tensor_scalar(low, scale, -0.7, None, ALU.mult))
            for i, w in enumerate((W3F["fc"], W3F["proj"])):
                tmp = probs[:, 0:FB3 * WIDTH]
                prep(V.tensor_scalar(tmp, w, low[:, i:i + 1], None, ALU.is_lt))
                prep(V.scalar_tensor_tensor(out=tmp, in0=w, scalar=thr[:, i:i + 1], in1=tmp, op0=ALU.is_gt, op1=ALU.subtract))
                prep(V.scalar_tensor_tensor(out=tmp, in0=tmp, scalar=scale[:, i:i + 1], in1=w, op0=ALU.mult, op1=ALU.subtract))
                prep(V.tensor_tensor(w, w, tmp, ALU.add))
            vec.wait_ge(prep_filled, 2)
            V.tensor_copy(w2f[:, :], turn_psum[0][:, :])
            vec.wait_ge(prep_filled, 3)
            kr = turn_psum[1][:, 0:KB * P].rearrange("p (b n) -> p b n", b=KB)
            V.tensor_copy(heads(w_kv[:, :], KB)[:, :, KVC:P], kr[:, :, 0:ROPE])
            V.tensor_copy(heads(w_kv_swap[:, :], KB), kr[:, :, ROPE:P])
            vec.wait_ge(prep_filled, 4)
            for i in range(2):
                bank = (general_psum[1], score_psum[0])[i]
                V.tensor_copy(heads(w_query[0:QC, :], H1)[:, GROUP * i:GROUP * (i + 1), 0:KVC], heads(bank[0:QC, 0:512], GROUP))
            V.memset(tiny[:, 1:2], 0.0).then_inc(prep_done, 1)
            vec.wait_ge(prep_filled, 5)
            for i in range(2):
                V.tensor_copy(w_out[:, 1024 * i:1024 * (i + 1)], score_psum[i][:, :])
            V.memset(tiny[:, 2:3], 0.0).then_inc(prep_done, 1)
            for i, s in enumerate(general.emptied + score.emptied + turn.emptied):
                V.memset(tiny[:, 3 + i:4 + i], 0.0).then_inc(s, 1)
            vec.wait_ge(loaded["w0"], 16)
            vec.wait_ge(loaded["rows"], 16)

            def step(key, ins):
                steps[0] += 1
                marks[key] = steps[0]
                ins.then_inc(vec_steps, 1)

            def after(r, *key):
                vec.wait_ge(vec_steps, r * STEPS + marks[key])

            def staggered(*stages):
                for t in range(STREAMS + len(stages) - 1):
                    for k, stage in reversed(list(enumerate(stages))):
                        if 0 <= t - k < STREAMS:
                            stage(t - k)

            def norm_stages(r, tag, source):
                def stats_of(s):
                    if ("x", tag, s) in marks:
                        after(r, "x", tag, s)
                    step(("stats", tag, s), V.bn_stats(stats[s][:, :], source[s][:, :]))

                def mean_of(s):
                    after(r, "stats", tag, s)
                    hold(vec)
                    step(("mean", tag, s), V.bn_aggr(mean_var[s][:, :], stats[s][:, :]))

                def ask(s):
                    after(r, "mean", tag, s)
                    V.tensor_scalar(var_eps[s][:, :], mean_var[s][:, 1:2], EPS, None, ALU.add).then_inc(power_in, 1)

                def scale_rows(s):
                    vec.wait_ge(power_out, count(r, powers, tag, s))
                    V.tensor_scalar(z[s][:, :], source[s][:, :], mean_var[s][:, 0:1], rstd[s][:, :],
                                    ALU.subtract, ALU.mult).then_inc(z_ready, 1)

                return [stats_of, mean_of, ask, scale_rows]

            def update(r, job, bias=None):
                def stage(s):
                    bank = filled(vec, general, r, job, s)
                    if bias is not None:
                        vec.wait_ge(x_biased, count(r, biased, bias, s))
                    V.tensor_tensor(x[s][:, :], x[s][:, :], bank[:, 0:WIDTH], ALU.add).then_inc(emptied(general, job, s), 1)
                return stage

            def next_norm(r, tag, job):
                if tag not in tags:
                    return []
                stages = norm_stages(r, tag, x)

                def first(s):
                    moved(vec, general, r, job, s)
                    stages[0](s)
                return [first] + stages[1:]

            def soften(r, tag, s, g, n):
                job = (f"{tag} s", s, g)
                slot = score.place[job][0]
                bank = filled(vec, score, r, *job)
                top = peak[:, slot * GROUP:slot * GROUP + n]
                step(("peak", tag, s, g), V.tensor_reduce(top, heads(bank[:, 0:n * P], n), X_AXIS, ALU.max))
                before = same_slot_before(tag, s, g)
                if before:
                    filled(vec, turn, r, *last_turn(*before))
                after(r, "peak", tag, s, g)
                V.tensor_tensor(heads(shifted[:, slot * 1024:slot * 1024 + n * P], n), heads(bank[:, 0:n * P], n),
                                spread(top, P), ALU.subtract).then_inc(emptied(score, *job), 1)

            def divide(r, tag, s, g, a, n, cols, out):
                job = (f"{tag} av", s, g, a)
                slot = general.place[job][0]
                bank = filled(vec, general, r, *job)
                result = heads(bank[:, 0:n * (cols + 1)], n)
                inv = inverse[:, slot * GROUP:slot * GROUP + n]
                step(("inverse", tag, s, g, a), V.reciprocal(inv, result[:, :, cols]))
                after(r, "inverse", tag, s, g, a)
                out(result[:, :, 0:cols], inv).then_inc(emptied(general, *job), 1)

            def divide_narrow(r, tag, s, g, out):
                job = (f"{tag} ao", s, g)
                slot = general.place[job][0]
                bank = filled(vec, general, r, *job)
                result = heads(bank[:, 0:GROUP * SLOT], GROUP)
                inv = inverse[:, slot * GROUP:(slot + 1) * GROUP]
                step(("inverse", tag, s, g), V.reciprocal(inv, result[:, :, HD0]))
                after(r, "inverse", tag, s, g)
                cols = out.shape[3]
                V.tensor_tensor(out, result[:, :, 0:cols].rearrange("p (c h) j -> p c h j", c=2),
                                spread(inv, cols).rearrange("p (c h) j -> p c h j", c=2), ALU.mult).then_inc(emptied(general, *job), 1)

            def attend(r, tag, groups, n, normal):
                order = units(groups)
                for t in range(len(order) + 3):
                    if t < len(order):
                        soften(r, tag, *order[t], n)
                    if t >= 3:
                        normal(*order[t - 3])

            def rotate(r, target, turning, cosine, sine, n, width, tmp, slot_free):
                half = width // 2
                V.tensor_tensor(target, turning, repeat(cosine, n), ALU.mult)
                V.tensor_tensor(tmp[:, :, 0:half], turning[:, :, half:width], repeat(sine[:, 0:half], n), ALU.mult)
                V.tensor_tensor(tmp[:, :, half:width], turning[:, :, 0:half], repeat(sine[:, half:width], n), ALU.mult)\
                    .then_inc(slot_free, 1)

            with vec.Fori(0, ROUNDS) as r:
                steps[0] = 0
                for s in range(STREAMS):
                    vec.wait_ge(x_loaded[s], r * 16 + 16)
                staggered(*norm_stages(r, "0", x_in))
                vec.wait_ge(masks_loaded, r * 48 + 48)
                V.tensor_reduce(valid[:, :], heads(keep_i[:, :], STREAMS), X_AXIS, ALU.max)
                for s in range(STREAMS):
                    bank = filled(vec, general, r, "0 k", s)
                    out = big[s][:, 0:4 * P].rearrange("p (b e k) -> p b e k", b=KB, e=2)
                    for b in range(KB):
                        for e, mask in enumerate(("even", "odd")):
                            ins = V.tensor_scalar(out[:, b, e, :], bank[:, b * P:b * P + P], W0["b_k"][:, b:b + 1], C[mask],
                                                  ALU.add, ALU.mult)
                    ins.then_inc(emptied(general, "0 k", s), 1)

                def divide_small(tag):
                    return lambda s, g: divide_narrow(r, tag, s, g, heads_out[s][:, 0:WIDTH].rearrange(
                        "p (c h j) -> p c h j", c=KB, h=GROUP)[:, :, 4 * g:4 * g + 4, :])

                attend(r, "0", 2, GROUP, divide_small("0"))

                def plus_attention(s):
                    moved(vec, general, r, "0 ao", s, 1)
                    vec.wait_ge(x_biased, count(r, biased, "0", s))
                    step(("half x", s), V.tensor_tensor(x[s][:, :], x_in[s][:, :], heads_out[s][:, 0:WIDTH], ALU.add))

                def plus_ref(s):
                    bank = filled(vec, general, r, "0 ref rows", s)
                    after(r, "half x", s)
                    V.tensor_tensor(x[s][:, :], x[s][:, :], bank[:, 0:WIDTH], ALU.add).then_inc(emptied(general, "0 ref rows", s), 1)

                staggered(plus_attention, plus_ref, *next_norm(r, "0f", "0 ref rows"))

                if "0f" in tags:
                    def cols(s, a, n):
                        return small[s][:, a:a + n]

                    def chain(name, previous, op, extra=None):
                        def stage(s):
                            if previous:
                                after(r, previous, s)
                            if extra:
                                extra(s)
                            step((name, s), op(s))
                        return stage

                    def diff(s):
                        bank = filled(vec, general, r, "0f sel", s)
                        step(("diff", s), V.tensor_tensor(sel[s][:, 0:P], bank[:, 0:P], sel_const[:, 0:P], ALU.subtract))
                        V.scalar_tensor_tensor(out=sel[s][:, P:P + N_SEL], in0=bank[:, P:P + N_SEL], scalar=-2.0,
                                               in1=sel_const[:, P:P + N_SEL], op0=ALU.mult,
                                               op1=ALU.add).then_inc(emptied(general, "0f sel", s), 1)

                    def square_length(s):
                        moved(vec, general, r, "0f sel", s)
                        vec.wait_ge(z_squared, nth(r, s))

                    def gates(s):
                        after(r, "score", s)
                        V.tensor_tensor(cols(s, 80, 8), cols(s, 72, 8), R["slope"], ALU.mult).then_inc(gates_in, 1)

                    def exp_given(s):
                        vec.wait_ge(gates_exp, nth(r, s))

                    def pick(s):
                        after(r, "which", s)
                        V.tensor_tensor(heads(onehot[s][:, 0:64], N_SEL), heads(sel[s][:, 64:P], N_SEL),
                                        spread(onehot[s][:, 64:72], LORA), ALU.mult).then_inc(onehot_ready, 1)

                    staggered(
                        diff,
                        chain("square", "diff", lambda s: V.tensor_tensor(cols(s, 0, 64), sel[s][:, 0:64], sel[s][:, 0:64], ALU.mult)),
                        chain("length", None, lambda s: V.tensor_scalar(sel[s][:, P:P + 8], sel[s][:, P:P + 8], cols(s, 106, 1),
                                                                        None, ALU.add), square_length),
                        chain("content", "square", lambda s: V.tensor_reduce(cols(s, 64, 8), heads(cols(s, 0, 64), N_SEL), X_AXIS, ALU.add)),
                        chain("1/length", "length", lambda s: V.reciprocal(cols(s, 72, 8), sel[s][:, P:P + 8])),
                        chain("ratio", "1/length", lambda s: V.tensor_tensor(cols(s, 72, 8), cols(s, 64, 8), cols(s, 72, 8), ALU.mult)),
                        chain("score", "ratio", lambda s: V.tensor_tensor(cols(s, 72, 8), cols(s, 72, 8), R["center"], ALU.subtract)),
                        gates,
                        chain("1+exp", None, lambda s: V.tensor_scalar(cols(s, 96, 8), cols(s, 88, 8), 1.0, None, ALU.add), exp_given),
                        chain("gate", "1+exp", lambda s: V.reciprocal(cols(s, 96, 8), cols(s, 96, 8))),
                        chain("largest", "gate", lambda s: V.tensor_reduce(cols(s, 104, 1), cols(s, 96, 8), X_AXIS, ALU.max)),
                        chain("candidates", "largest", lambda s: V.scalar_tensor_tensor(
                            out=cols(s, 72, 8), in0=cols(s, 96, 8), scalar=cols(s, 104, 1), in1=C["falling"],
                            op0=ALU.is_ge, op1=ALU.mult)),
                        chain("first", "candidates", lambda s: V.tensor_reduce(cols(s, 105, 1), cols(s, 72, 8), X_AXIS, ALU.max)),
                        chain("which", "first", lambda s: V.tensor_scalar(onehot[s][:, 64:72], cols(s, 72, 8), cols(s, 105, 1),
                                                                          None, ALU.is_equal)),
                        pick)

                    def gated(s):
                        bank = filled(vec, general, r, "0f mod", s)
                        after(r, "x+(1-gate)z", s)
                        V.scalar_tensor_tensor(out=x[s][:, :], in0=bank[:, 0:WIDTH], scalar=cols(s, 104, 1), in1=x[s][:, :],
                                               op0=ALU.mult, op1=ALU.add).then_inc(emptied(general, "0f mod", s), 1)

                    staggered(
                        chain("gate z", None, lambda s: V.tensor_scalar(tA[s][:, :], z[s][:, :], cols(s, 104, 1), None, ALU.mult)),
                        chain("x+z", None, lambda s: V.tensor_tensor(x[s][:, :], x[s][:, :], z[s][:, :], ALU.add)),
                        chain("x+(1-gate)z", "x+z", lambda s: V.tensor_tensor(x[s][:, :], x[s][:, :], tA[s][:, :], ALU.subtract)),
                        gated, *next_norm(r, "1", "0f mod"))

                if "1" in tags:
                    for s in range(STREAMS):
                        bank = filled(vec, general, r, "1 k", s)
                        V.tensor_copy(kcT[s][0:KVC, :], bank[0:KVC, 0:P])
                        V.tensor_tensor(tA[s][KVC:P, 0:P], bank[KVC:P, 0:P], C["cos_kT"][KVC:P, :], ALU.mult)
                        V.tensor_tensor(tA[s][KVC:P, P:2 * P], bank[KVC:P, P:2 * P], C["sin_kT"][KVC:P, :],
                                        ALU.mult).then_inc(emptied(general, "1 k", s), 1)
                        moved(vec, general, r, "1 k", s)
                        step(("keys", s), V.tensor_tensor(kcT[s][KVC:P, :], tA[s][KVC:P, 0:P], tA[s][KVC:P, P:2 * P], ALU.add))
                    for i, (s, g) in enumerate(units(2)):
                        slot = score.place[("1 q", s, g)][0]
                        bank = filled(vec, score, r, "1 q", s, g)
                        vec.wait_ge(act_read, count(r, act_reads, "1 q", s, g))
                        rope = heads(q_rows[:, slot * 1024:(slot + 1) * 1024], GROUP)[:, :, KVC:P]
                        tmp = heads(q_swap[:, slot * 512:(slot + 1) * 512], GROUP)
                        rotate(r, rope, heads(bank[:, :], GROUP)[:, :, KVC:P], C["cos_q"], C["sin_q"], GROUP, ROPE, tmp,
                               emptied(score, "1 q", s, g))
                        moved(vec, score, r, "1 q", s, g)
                        V.tensor_tensor(rope, rope, tmp, ALU.add).then_inc(q_rotated, 1)

                    def divide1(s, g):
                        for a in range(2):
                            at = g * 1024 + a * 4 * KVC
                            out = heads(big[s][:, at:at + 4 * KVC], 4)
                            divide(r, "1", s, g, a, 4, KVC, lambda result, inv: V.tensor_tensor(out, result, spread(inv, KVC), ALU.mult))

                    attend(r, "1", 2, GROUP, divide1)
                    staggered(update(r, "1 out"), *next_norm(r, "1f", "1 out"))

                if "1f" in tags:
                    def mean_square(s):
                        step(("var/root", s), V.tensor_tensor(small[s][:, 0:1], mean_var[s][:, 1:2], rstd[s][:, :], ALU.mult))

                    def ask_rms(s):
                        after(r, "var/root", s)
                        V.tensor_scalar(var_eps[s][:, :], small[s][:, 0:1], rstd[s][:, :], EPS, ALU.mult, ALU.add)\
                            .then_inc(power_in, 1)

                    def rms_rows(name, power, source, weight):
                        def stage(s):
                            vec.wait_ge(power_out, count(r, powers, power, s))
                            V.scalar_tensor_tensor(out=hrow[s][:, :], in0=source[s][:, :], scalar=rstd[s][:, :], in1=weight,
                                                   op0=ALU.mult, op1=ALU.mult).then_inc(rows_ready, 1)
                        return stage

                    def z_done(s):
                        vec.wait_ge(z_ready, count(r, normalised, "1f", s))
                        mean_square(s)

                    staggered(z_done, ask_rms, rms_rows("1f z", "1f rms", z, R["ln1"]))
                    for s in range(STREAMS):
                        bank = filled(vec, score, r, "1f rows", s)
                        vec.wait_ge(act_read, count(r, act_reads, "1f rows", s))
                        rope = heads(heads_out[s][:, 0:512], 2 * LF)[:, :, RD:2 * RD]
                        tmp = heads(tA[s][:, :], 2 * LF)
                        rotate(r, rope, heads(bank[:, 2 * P:4 * P], 2 * LF), C["cos_f"], C["sin_f"], 2 * LF, RD, tmp,
                               emptied(score, "1f rows", s))
                        moved(vec, score, r, "1f rows", s)
                        V.tensor_tensor(rope, rope, tmp, ALU.add).then_inc(qk_ready, 1)
                    for s in range(STREAMS):
                        bank = filled(vec, turn, r, "1f qk", s)
                        V.tensor_copy(tB[s][:, :], bank[:, 0:WIDTH])
                        out = big[s][:, 0:4 * P].rearrange("p (b e k) -> p b e k", b=KB, e=2)
                        for e, mask in enumerate(("even", "odd")):
                            ins = V.tensor_scalar(out[:, :, e, :], heads(bank[:, WIDTH:2 * WIDTH], KB), C[mask], None, ALU.mult)
                        ins.then_inc(emptied(turn, "1f qk", s), 1)
                    attend(r, "1f", 2, GROUP, divide_small("1f"))

                    def residual(s):
                        bank = filled(vec, general, r, "1f out", s)
                        V.tensor_tensor(hres[s][:, :], z[s][:, :], bank[:, 0:WIDTH], ALU.add).then_inc(emptied(general, "1f out", s), 1)

                    def ask_h(s):
                        vec.wait_ge(h_squared, nth(r, s))
                        V.tensor_scalar(var_eps[s][:, :], small[s][:, 106:107], 1.0 / WIDTH, EPS, ALU.mult, ALU.add)\
                            .then_inc(power_in, 1)

                    staggered(residual, ask_h, rms_rows("1f h", "1f h", hres, R["ln2"]))

                    N = EXPERTS - 1

                    def logits(s):
                        bank = filled(vec, general, r, "1f router", s)
                        V.tensor_tensor(cols(s, 0, 8), bank[:, 0:8], R["router_b"], ALU.add).then_inc(emptied(general, "1f router", s), 1)

                    def router_given(s):
                        vec.wait_ge(router_exp, nth(r, s))

                    def take(name, source, best, previous, at):
                        return [
                            chain(name + " best", previous, lambda s: V.tensor_reduce(cols(s, best, 1), cols(s, source, N), X_AXIS, ALU.max)),
                            chain(name + " candidates", name + " best", lambda s: V.scalar_tensor_tensor(
                                out=cols(s, 24, N), in0=cols(s, source, N), scalar=cols(s, best, 1), in1=C["falling"][:, 0:N],
                                op0=ALU.is_ge, op1=ALU.mult)),
                            chain(name + " first", name + " candidates", lambda s: V.tensor_reduce(cols(s, 65, 1), cols(s, 24, N), X_AXIS, ALU.max)),
                            chain(name, name + " first", lambda s: V.tensor_scalar(cols(s, at, N), cols(s, 24, N), cols(s, 65, 1), None, ALU.is_equal))]

                    staggered(
                        logits,
                        chain("1+exp r", None, lambda s: V.tensor_scalar(cols(s, 16, 8), cols(s, 8, 8), 1.0, None, ALU.add), router_given),
                        chain("probability", "1+exp r", lambda s: V.reciprocal(cols(s, 16, 8), cols(s, 16, 8))),
                        *take("one", 16, 64, "probability", 32),
                        chain("without one", "one", lambda s: V.scalar_tensor_tensor(
                            out=cols(s, 40, N), in0=cols(s, 32, N), scalar=-2.0, in1=cols(s, 16, N), op0=ALU.mult, op1=ALU.add)),
                        *take("two", 40, 66, "without one", 56),
                        chain("both", "two", lambda s: V.tensor_tensor(cols(s, 56, N), cols(s, 56, N), cols(s, 32, N), ALU.add)),
                        chain("sum", "both", lambda s: V.tensor_tensor(cols(s, 68, 1), cols(s, 64, 1), cols(s, 66, 1), ALU.add)),
                        chain("1/sum", "sum", lambda s: V.reciprocal(cols(s, 68, 1), cols(s, 68, 1))),
                        chain("chosen", "both", lambda s: V.tensor_tensor(cols(s, 56, N), cols(s, 56, N), cols(s, 16, N), ALU.mult)),
                        chain("expert weights", "1/sum", lambda s: V.tensor_scalar(
                            expert_w[s][:, 1:8], cols(s, 56, N), cols(s, 68, 1), 0.5 / EXPERT_SCALE, ALU.mult, ALU.mult),
                            lambda s: after(r, "chosen", s)))

                    for s, g in units(2):
                        job = ("1f gu", s, g)
                        slot = score.place[job][0]
                        bank = filled(vec, score, r, *job)
                        vec.wait_ge(tanh_done, count(r, units(2), s, g))
                        gu = bank[:, :].rearrange("p (e u n) -> p e u n", e=4, u=2)
                        th = heads(q_rows[:, slot * 1024:slot * 1024 + 512], 4)
                        ga = heads(q_rows[:, slot * 1024 + 512:slot * 1024 + 1024], 4)
                        step(("silu", s, g), V.scalar_tensor_tensor(out=ga, in0=th, scalar=1.0, in1=gu[:, :, 0, :],
                                                                    op0=ALU.add, op1=ALU.mult))
                        after(r, "expert weights", s)
                        after(r, "silu", s, g)
                        for e in range(4):
                            ins = V.scalar_tensor_tensor(
                                out=big[s][:, (4 * g + e) * INNER:(4 * g + e + 1) * INNER], in0=ga[:, e, :],
                                scalar=expert_w[s][:, 4 * g + e:4 * g + e + 1], in1=gu[:, e, 1, :], op0=ALU.mult, op1=ALU.mult)
                        ins.then_inc(emptied(score, *job), 1)
                    staggered(update(r, "1f moe", "1f"), *next_norm(r, "2", "1f moe"))

                if "2" in tags:
                    def divide2(s, g):
                        def out(result, inv):
                            step(("kept inverse", s), V.tensor_tensor(inv, inv, valid[:, s:s + 1], ALU.mult))
                            after(r, "kept inverse", s)
                            return V.scalar_tensor_tensor(out=x[s][:, :], in0=result[:, 0, :], scalar=inv, in1=x[s][:, :],
                                                          op0=ALU.mult, op1=ALU.add)
                        divide(r, "2", s, g, 0, 1, WIDTH, out)

                    attend(r, "2", 1, 1, divide2)
                    if "2f" in tags:
                        stages = norm_stages(r, "2f", x)

                        def first(s):
                            moved(vec, general, r, "2 av", s, 0, 0)
                            stages[0](s)
                        staggered(first, *stages[1:])
                if "2f" in tags:
                    staggered(update(r, "2f out", "2f"), *next_norm(r, "3", "2f out"))

                if "3" in tags:
                    for s in range(STREAMS):
                        bank = filled(vec, general, r, "3 k", s)
                        out = big[s][:, 0:KB * HPG * P].rearrange("p (b h k) -> p b h k", b=KB, h=HPG)
                        for h in range(HPG):
                            ins = V.tensor_scalar(out[:, :, h, :], heads(bank[:, 0:WIDTH], KB), C["quarter"][:, h:h + 1], None, ALU.mult)
                        ins.then_inc(emptied(general, "3 k", s), 1)

                    def divide3(s, g):
                        divide_narrow(r, "3", s, g, heads_out[s][:, g * GROUP * HD3:(g + 1) * GROUP * HD3].rearrange(
                            "p (c h j) -> p c h j", c=2, h=HPG))

                    attend(r, "3", 4, GROUP, divide3)
                    staggered(update(r, "3 out", "3"), *next_norm(r, "3f", "3 out"))

                if "3f" in tags:
                    for s in range(STREAMS):
                        moved(vec, score, r, "3f h", s)
                        V.tensor_tensor(big[s][:, 1024:1024 + FF3], big[s][:, 0:FF3], big[s][:, 0:FF3], ALU.mult).then_inc(relu_squared, 1)
                    staggered(update(r, "3f out"))
                assert steps[0] < STEPS, steps[0]
                vec.sem_inc(vec_steps, STEPS - steps[0])

        @block.tensor
        def _(pe):
            T = nc.tensor
            ident = C["ident"]

            for name in ("const", "prep", "w1"):
                pe.wait_ge(loaded[name], 16 * (len(W1P) if name == "prep" else 1))
            pe.wait_ge(ones_ready, 1)
            pe.wait_ge(prep_done, 1)
            for b in range(KB):
                T.matmul(general_psum[0][:, 0:SELW], ones[:, :], sel_prod[:, b * SELW:(b + 1) * SELW], start=(b == 0), stop=(b == KB - 1))
            T.matmul(general_psum[0][:, SELW:SELW + 2], ones[:, :], total, start=True, stop=True).then_inc(prep_filled, 1)
            for i in range(KB):
                for b in range(KB):
                    ins = T.transpose(turn_psum[0][:, i * WIDTH + b * P:i * WIDTH + b * P + P],
                                      w2f_rows[:, b * WIDTH + i * P:b * WIDTH + i * P + P], ident)
            ins.then_inc(prep_filled, 1)
            for b in range(KB):
                ins = T.matmul(turn_psum[1][:, b * P:b * P + P], W1P["kvcT"][0:KVC, b * P:b * P + P], W1P["kr"][0:KVC, :],
                               start=True, stop=True)
            ins.then_inc(prep_filled, 1)
            for h in range(H1):
                bank = (general_psum[1], score_psum[0])[h // GROUP]
                at = h % GROUP * KVC
                ins = T.matmul(bank[0:QC, at:at + KVC], W1P["uqT"][:, h * QC:(h + 1) * QC], W1P["ukT"][:, h * KVC:(h + 1) * KVC],
                               start=True, stop=True)
            ins.then_inc(prep_filled, 1)
            pe.wait_ge(prep_done, 2)
            for h in range(H1):
                pair, row = h // 2, h % 2 * KVC
                out = score_psum[pair // 4][row:row + KVC, pair % 4 * WIDTH:(pair % 4 + 1) * WIDTH]
                ins = T.matmul(out, W1P["uvT"][:, h * KVC:(h + 1) * KVC], W1P[f"o{h // GROUP}"][:, h % GROUP * WIDTH:(h % GROUP + 1) * WIDTH],
                               start=True, stop=True)
            ins.then_inc(prep_filled, 1)
            pe.wait_ge(loaded["w0"], 16)
            pe.wait_ge(loaded["constb"], 16)

            def turn_rows(bank, source, n=KB):
                for b in range(n):
                    ins = T.transpose(bank[:, b * P:b * P + P], source[:, b * P:b * P + P], ident)
                return ins

            def blocks_out(bank, w, cols, actT, n=KB):
                for m in range(n):
                    for b in range(KB):
                        ins = T.matmul(bank[:, m * P:m * P + P], w[:, b * cols + m * P:b * cols + m * P + P], actT[:, b * P:b * P + P],
                                       start=(b == 0), stop=(b == KB - 1))
                return ins

            def rows_out(out, actT, w, cols, n=KB, at=0):
                wide = out.shape[1]
                for b in range(n):
                    ins = T.matmul(out, actT[:, b * P:b * P + P], w[:, b * cols + at:b * cols + at + wide], start=(b == 0), stop=(b == n - 1))
                return ins

            def job(ring, r, *key):
                return free(pe, ring, r, *key)

            def done(ins, ring, *key):
                ins.then_inc(fill(ring, *key), 1)

            def turn_z(r, name, tag):
                for s in range(STREAMS):
                    pe.wait_ge(z_ready, count(r, normalised, tag, s))
                    done(turn_rows(job(general, r, name, s), z[s]), general, name, s)

            def masked(bank, mask, n, last=False):
                return T.matmul(bank, ident_b, repeat(mask[:, :], n), start=True, stop=last)

            def scores_and_turns(r, tag, t, order, per, turns, scores):
                if t < len(order):
                    s, g = order[t]
                    bank = job(score, r, f"{tag} s", s, g)
                    done(scores(s, g, bank), score, f"{tag} s", s, g)
                if 1 <= t <= len(order):
                    s, g = order[t - 1]
                    slot = score.place[(f"{tag} s", s, g)][0]
                    for a in range(turns):
                        bank = job(turn, r, f"{tag} t", s, g, a)
                        if a == 0:
                            moved(pe, score, r, f"{tag} s", s, g)
                        done(turn_rows(bank, shifted[:, slot * 1024 + a * 512:slot * 1024 + a * 512 + per * P], per),
                             turn, f"{tag} t", s, g, a)

            def attend(r, tag, groups, n, scores, value, wide, turns=2):
                order = units(groups)
                per = n // turns
                for t in range(len(order) + 2):
                    scores_and_turns(r, tag, t, order, per, turns, scores)
                    if t >= 2:
                        s, g = order[t - 2]
                        for a in range(turns):
                            key = (f"{tag} av", s, g, a)
                            bank = job(general, r, *key)
                            moved(pe, turn, r, f"{tag} t", s, g, a)
                            at = (prob_jobs.index((tag, s, g, a)) % 4) * 512
                            for i in range(per):
                                ins = T.matmul(bank[:, i * wide:(i + 1) * wide], probs[:, at + i * P:at + i * P + P], value(s),
                                               start=True, stop=True)
                            done(ins, general, *key)

            def attend_narrow(r, tag, groups, scores, place):
                order = units(groups)
                for t in range(len(order) + 3):
                    scores_and_turns(r, tag, t, order, 4, 2, scores)
                    if 2 <= t < len(order) + 2:
                        s, g = order[t - 2]
                        bank = job(general, r, f"{tag} av", s, g)
                        for a in range(2):
                            moved(pe, turn, r, f"{tag} t", s, g, a)
                            at = (prob_jobs.index((tag, s, g, a)) % 4) * 512
                            for i in range(4):
                                v, block, row = place(g, a * 4 + i)
                                ins = T.matmul(bank[SLOT * row:SLOT * (row + 1), block * P:(block + 1) * P],
                                               values[s][:, v * SLOT:(v + 1) * SLOT], probs[:, at + i * P:at + i * P + P],
                                               start=True, stop=True)
                        done(ins, general, f"{tag} av", s, g)
                    if t >= 3:
                        s, g = order[t - 3]
                        bank = job(general, r, f"{tag} ao", s, g)
                        moved(pe, general, r, f"{tag} av", s, g)
                        at = (t - 3) % 2 * GROUP * SLOT
                        done(turn_rows(bank, narrow_out[:, at:at + GROUP * SLOT]), general, f"{tag} ao", s, g)

            with pe.Fori(0, ROUNDS) as r:
                for s in range(STREAMS):
                    pe.wait_ge(cxT_loaded[s], r * 16 + 16)
                    done(blocks_out(job(general, r, "0 sup", s), W0["fc"], WIDTH, cxT[s]), general, "0 sup", s)
                turn_z(r, "0 zT", "0")
                for s in range(STREAMS):
                    bank = job(general, r, "0 ref", s)
                    moved(pe, general, r, "0 zT", s)
                    done(blocks_out(bank, W0["fc"], WIDTH, zT[s]), general, "0 ref", s)
                for s in range(STREAMS):
                    bank = job(general, r, "0 k", s)
                    moved(pe, general, r, "0 sup", s)
                    done(blocks_out(bank, W0["k"], WIDTH, tB[s]), general, "0 k", s)
                for s in range(STREAMS):
                    done(rows_out(job(general, r, "0 v", s)[:, 0:WIDTH], tB[s], W0["v"], WIDTH), general, "0 v", s)
                for s in range(STREAMS):
                    bank = job(general, r, "0 q", s)
                    moved(pe, general, r, "0 ref", s)
                    done(blocks_out(bank, W0["q"], WIDTH, tA[s]), general, "0 q", s)

                def small_scores(tag, queries, mask=None):
                    def scores(s, g, bank):
                        if g == 0:
                            if tag == "0":
                                moved(pe, general, r, "0 k", s)
                                moved(pe, general, r, "0 q", s)
                                moved(pe, general, r, "0 v", s)
                            else:
                                moved(pe, turn, r, "1f qk", s)
                        keys = big[s][:, 0:4 * P].rearrange("p (b e k) -> p b (e k)", b=KB, e=2)
                        for q in range(2):
                            row = 32 * (2 * g + q)
                            if mask is not None:
                                masked(bank[:, q * 512:(q + 1) * 512], mask, 4)
                            for b in range(KB):
                                at = q * 512 + b * 256
                                ins = T.matmul(bank[:, at:at + 256], queries[s][row:row + 32, b * P:b * P + P], keys[row:row + 32, b, :],
                                               start=(mask is None), stop=(mask is None or b == KB - 1))
                        return ins
                    return scores

                def small_place(g, i):
                    return small_head(g, i), i % 4 // 2, i // 4 * 2 + i % 2

                attend_narrow(r, "0", 2, small_scores("0", zT), small_place)
                for s in range(STREAMS):
                    done(turn_rows(job(general, r, "0 ref rows", s), tA[s]), general, "0 ref rows", s)

                if "0f" in tags:
                    turn_z(r, "0f zT", "0f")
                    for s in range(STREAMS):
                        bank = job(general, r, "0f sel", s)
                        moved(pe, general, r, "0f zT", s)
                        done(rows_out(bank[:, 0:SELW], zT[s], W0F["sel"], SELW), general, "0f sel", s)
                    for s in range(STREAMS):
                        bank = job(turn, r, "0f onehot", s)
                        pe.wait_ge(onehot_ready, nth(r, s))
                        done(turn_rows(bank, onehot[s], 1), turn, "0f onehot", s)
                    for s in range(STREAMS):
                        bank = job(general, r, "0f mod", s)
                        moved(pe, turn, r, "0f onehot", s)
                        done(T.matmul(bank[:, 0:WIDTH], onehotT[s][:, :], W0F["lift"], start=True, stop=True), general, "0f mod", s)

                if "1" in tags:
                    for s in range(STREAMS):
                        bank = job(general, r, "1 k", s)
                        blocks_out(bank, w_kv, P, cxT[s], 1)
                        for b in range(KB):
                            ins = T.matmul(bank[KVC:P, P:2 * P], w_kv_swap[:, b * ROPE:(b + 1) * ROPE], cxT[s][:, b * P:b * P + P],
                                           start=(b == 0), stop=(b == KB - 1))
                        done(ins, general, "1 k", s)
                    for s in range(STREAMS):
                        done(rows_out(job(general, r, "1 kv", s)[:, 0:KVC], cxT[s], W1["kvc"], KVC), general, "1 kv", s)
                    turn_z(r, "1 zT", "1")
                    for s in range(STREAMS):
                        bank = job(general, r, "1 qc", s)
                        moved(pe, general, r, "1 zT", s)
                        for b in range(KB):
                            ins = T.matmul(bank[0:QC, 0:P], W1["dq"][:, b * QC:(b + 1) * QC], zT[s][:, b * P:b * P + P],
                                           start=(b == 0), stop=(b == KB - 1))
                        done(ins, general, "1 qc", s)
                    order = units(2)
                    for t in range(len(order) + 1):
                        if t < len(order):
                            s, g = order[t]
                            bank = job(score, r, "1 q", s, g)
                            moved(pe, general, r, "1 qc", s)
                            for q in range(2):
                                at = g * 1024 + q * 512
                                ins = T.matmul(bank[:, q * 512:(q + 1) * 512], qcT[s][0:QC, :], w_query[0:QC, at:at + 512], start=True, stop=True)
                            done(ins, score, "1 q", s, g)
                        if t >= 1:
                            s, g = order[t - 1]
                            slot = score.place[("1 q", s, g)][0]
                            for a in range(2):
                                bank = job(turn, r, "1 q", s, g, a)
                                pe.wait_ge(q_rotated, r * len(order) + t)
                                done(turn_rows(bank, q_rows[:, slot * 1024 + a * 512:slot * 1024 + (a + 1) * 512], 4), turn, "1 q", s, g, a)

                    def scores1(s, g, bank):
                        if g == 0:
                            moved(pe, turn, r, "1 q", s, 1, 1)
                            pe.wait_ge(q_rotated, r * len(order) + 1)
                            pe.wait_ge(masks_ready, r + 1)
                        for q in range(2):
                            masked(bank[:, q * 512:(q + 1) * 512], mask1[s], 4)
                            for i in range(4):
                                at = (q * 4 + i) * P
                                h = g * GROUP + q * 4 + i
                                ins = T.matmul(bank[:, at:at + P], big[s][:, h * P:h * P + P], kcT[s][:, :], start=False, stop=(i == 3))
                        return ins

                    attend(r, "1", 2, GROUP, scores1, lambda s: values1[s][:, 0:KVC + 1], KVC + 1)
                    for s in range(STREAMS):
                        for a in range(2):
                            bank = job(turn, r, "1 o", s, a)
                            for i in range(2):
                                moved(pe, general, r, "1 av", s, a, i)
                            done(turn_rows(bank, big[s][:, a * 1024:a * 1024 + 512], 4), turn, "1 o", s, a)
                    for s in range(STREAMS):
                        bank = job(general, r, "1 out", s)
                        for a in range(2):
                            moved(pe, turn, r, "1 o", s, a)
                        for pair in range(H1 // 2):
                            at = pair // 4 * 1024 + 512 + pair % 4 * P
                            ins = T.matmul(bank[:, 0:WIDTH], big[s][:, at:at + P], w_out[:, pair * WIDTH:(pair + 1) * WIDTH],
                                           start=(pair == 0), stop=(pair == H1 // 2 - 1))
                        done(ins, general, "1 out", s)

                if "1f" in tags:
                    pe.wait_ge(loaded["w1f"], 16)
                    for s in range(STREAMS):
                        bank = job(general, r, "1f zT", s)
                        pe.wait_ge(rows_ready, count(r, weighted_rows, "1f z", s))
                        done(turn_rows(bank, hrow[s]), general, "1f zT", s)
                    for s in range(STREAMS):
                        bank = job(general, r, "1f kq", s)
                        moved(pe, general, r, "1f zT", s)
                        done(blocks_out(bank, W1F["down_kq"], P, zT[s], 1), general, "1f kq", s)
                    for s in range(STREAMS):
                        bank = job(score, r, "1f rows", s)
                        moved(pe, general, r, "1f kq", s)
                        T.matmul(bank[:, 0:3 * P], qcT[s][:, :], W1F["up"][:, 0:3 * P], start=True, stop=True)
                        rows_out(bank[:, 3 * P:4 * P], zT[s], W1F["rope_k"], P)
                        done(T.matmul(bank[:, 512:512 + WIDTH], qcT[s][:, :], W1F["up"][:, 3 * P:3 * P + WIDTH], start=True, stop=True),
                             score, "1f rows", s)
                    for s in range(STREAMS):
                        bank = job(turn, r, "1f qk", s)
                        pe.wait_ge(qk_ready, nth(r, s))
                        done(turn_rows(bank, heads_out[s][:, 0:512], 4), turn, "1f qk", s)
                    causal = causal_b
                    attend_narrow(r, "1f", 2, small_scores("1f", tB, causal), small_place)
                    for s in range(STREAMS):
                        bank = job(turn, r, "1f o", s)
                        moved(pe, general, r, "1f ao", s, 1)
                        done(turn_rows(bank, heads_out[s]), turn, "1f o", s)
                    for s in range(STREAMS):
                        bank = job(general, r, "1f out", s)
                        moved(pe, turn, r, "1f o", s)
                        done(rows_out(bank[:, 0:WIDTH], headsT[s], W1F["o"], WIDTH), general, "1f out", s)
                    for s in range(STREAMS):
                        bank = job(turn, r, "1f h", s)
                        pe.wait_ge(rows_ready, count(r, weighted_rows, "1f h", s))
                        done(turn_rows(bank, hrow[s]), turn, "1f h", s)
                    for s in range(STREAMS):
                        bank = job(general, r, "1f router", s)
                        moved(pe, turn, r, "1f h", s)
                        done(rows_out(bank[:, 0:EXPERTS], zT[s], W1F["router"], EXPERTS), general, "1f router", s)
                    pe.wait_ge(loaded["wm"], 16)
                    order = units(2)
                    for t in range(len(order) + 2):
                        if t < len(order):
                            s, g = order[t]
                            bank = job(score, r, "1f gu", s, g)
                            for q in range(2):
                                ins = rows_out(bank[:, q * 512:(q + 1) * 512], zT[s], WM["gate_up"], EXPERTS * 2 * INNER,
                                               at=g * 1024 + q * 512)
                            done(ins, score, "1f gu", s, g)
                        if 1 <= t <= len(order):
                            s, g = order[t - 1]
                            bank = job(turn, r, "1f m", s, g)
                            moved(pe, score, r, "1f gu", s, g)
                            done(turn_rows(bank, big[s][:, g * 512:(g + 1) * 512], 4), turn, "1f m", s, g)
                        if t >= 2:
                            s, g = order[t - 2]
                            if g == 1:
                                bank = job(general, r, "1f moe", s)
                                for half in range(2):
                                    moved(pe, turn, r, "1f m", s, half)
                                done(rows_out(bank[:, 0:WIDTH], big[s][:, 1024:2048], WM["down"], WIDTH, EXPERTS), general, "1f moe", s)

                if "2" in tags:
                    turn_z(r, "2 zT", "2")

                    def scores2(s, g, bank):
                        moved(pe, general, r, "2 zT", s)
                        pe.wait_ge(cx_loaded[s], r * 16 + 16)
                        masked(bank[:, 0:P], mask2[s], 1)
                        for b in range(KB):
                            ins = T.matmul(bank[:, 0:P], zT[s][:, b * P:b * P + P], cxT[s][:, b * P:b * P + P], start=False, stop=(b == KB - 1))
                        return ins

                    attend(r, "2", 1, 1, scores2, lambda s: cx[s][:, 0:WIDTH + 1], WIDTH + 1, turns=1)
                if "2f" in tags:
                    turn_z(r, "2f zT", "2f")
                    for s in range(STREAMS):
                        bank = job(general, r, "2f out", s)
                        moved(pe, general, r, "2f zT", s)
                        done(rows_out(bank[:, 0:WIDTH], zT[s], w2f, WIDTH), general, "2f out", s)

                if "3" in tags:
                    pe.wait_ge(loaded["w3"], 16)
                    for s in range(STREAMS):
                        done(blocks_out(job(general, r, "3 k", s), W3["k"], WIDTH, cxT[s]), general, "3 k", s)
                    for s in range(STREAMS):
                        done(rows_out(job(general, r, "3 v", s)[:, 0:G3 * HD3], cxT[s], W3["v"], G3 * HD3), general, "3 v", s)
                    turn_z(r, "3 zT", "3")
                    for s in range(STREAMS):
                        bank = job(general, r, "3 q", s)
                        moved(pe, general, r, "3 zT", s)
                        done(blocks_out(bank, W3["q"], WIDTH, zT[s]), general, "3 q", s)

                    def scores3(s, g, bank):
                        if g == 0:
                            for name in ("3 k", "3 v", "3 q"):
                                moved(pe, general, r, name, s)
                        for q in range(2):
                            b, row = (2 * g + q) // 4, 32 * ((2 * g + q) % 4)
                            masked(bank[:, q * 512:(q + 1) * 512], mask3[s], 4)
                            ins = T.matmul(bank[:, q * 512:(q + 1) * 512], zT[s][row:row + 32, b * P:b * P + P],
                                           big[s][row:row + 32, b * 512:(b + 1) * 512], start=False, stop=True)
                        return ins

                    attend_narrow(r, "3", 4, scores3, lambda g, i: (2 * g + i // HPG, i // HPG, i % HPG))
                    for s in range(STREAMS):
                        bank = job(turn, r, "3 o", s)
                        all_moved(pe, general, r, [("3 ao", s, g) for g in range(4)])
                        done(turn_rows(bank, heads_out[s]), turn, "3 o", s)
                    for s in range(STREAMS):
                        bank = job(general, r, "3 out", s)
                        moved(pe, turn, r, "3 o", s)
                        done(rows_out(bank[:, 0:WIDTH], headsT[s], W3["o"], WIDTH), general, "3 out", s)

                if "3f" in tags:
                    turn_z(r, "3f zT", "3f")
                    for s in range(STREAMS):
                        bank = job(score, r, "3f h", s)
                        moved(pe, general, r, "3f zT", s)
                        done(blocks_out(bank, W3F["fc"], FF3, zT[s], FB3), score, "3f h", s)
                    for s in range(STREAMS):
                        bank = job(general, r, "3f out", s)
                        pe.wait_ge(relu_squared, nth(r, s))
                        done(rows_out(bank[:, 0:WIDTH], big[s][:, 1024:1024 + FF3], W3F["proj"], WIDTH, FB3), general, "3f out", s)


INPUT_SHAPES = [("x", (SEQUENCES, P, WIDTH), F32), ("ctx", (SEQUENCES, P, WIDTH), F32), ("ctxT", (SEQUENCES, P, WIDTH), F32),
                ("seg", (ROUNDS, P, STREAMS), I32), ("keep", (ROUNDS, STREAMS * P), U8), ("pad", (ROUNDS, STREAMS * P), I32),
                ("const", (P, width(CONST_NAMES)), F32), ("constb", (P, 2 * P), BF16), ("rows", (width(ROW_NAMES),), F32),
                ("w0", (P, width(W0_NAMES)), F32), ("w0f", (P, width(W0F_NAMES)), F32), ("w1", (P, width(W1_NAMES)), F32),
                ("w1p", (P, width(W1P_NAMES)), F32), ("w1f", (P, width(W1F_NAMES)), F32), ("wm", (P, width(WM_NAMES)), F32),
                ("w2f", (P, KB * WIDTH), F32), ("w3", (P, width(W3_NAMES)), F32), ("w3f", (P, width(W3F_NAMES)), F32)]


def by_block(w):
    n = w.shape[1]
    return w.reshape(-1, P, n).transpose(1, 0, 2).reshape(P, -1)


def pad_rows(w, at=0):
    out = np.zeros((P, w.shape[1]), w.dtype)
    out[at:at + w.shape[0]] = w
    return out


def constants():
    part = np.arange(P)
    t = np.arange(P, dtype=np.float32)

    def angles(half):
        inv = (1.0 / np.float32(10000.0) ** (np.arange(half, dtype=np.float32) / np.float32(half))).astype(np.float32)
        return (t[:, None] * inv).astype(np.float32)
    a, f = angles(ROPE // 2), angles(RD // 2)
    cos_q = np.concatenate([np.cos(a), np.cos(a)], 1)
    sin_q = np.concatenate([-np.sin(a), np.sin(a)], 1)
    parts = {
        "ident": np.eye(P), "even": (part // HD0 % 2 == 0)[:, None], "odd": (part // HD0 % 2 == 1)[:, None],
        "quarter": part[:, None] // HD3 % HPG == np.arange(HPG)[None, :], "key": np.tile(t, (P, 1)),
        "falling": np.tile(np.arange(EXPERTS, 0, -1), (P, 1)), "cos_q": cos_q, "sin_q": sin_q,
        "cos_kT": pad_rows(cos_q.T, KVC), "sin_kT": pad_rows(sin_q.T, KVC),
        "cos_f": np.concatenate([np.cos(f), np.cos(f)], 1), "sin_f": np.concatenate([-np.sin(f), np.sin(f)], 1)}
    return np.concatenate([np.asarray(parts[n], np.float32) for n, _ in CONST_NAMES], 1)


def kernel(**inputs):
    import concourse.bacc as bacc
    import ml_dtypes
    from concourse.bass_utils import run_bass_kernel_spmd

    I = {k: np.asarray(v) for k, v in inputs.items()}

    def pack(names, parts):
        for n, cols in names:
            assert parts[n].shape == (P, cols), (n, parts[n].shape, cols)
        return np.ascontiguousarray(np.concatenate([parts[n] for n, _ in names], 1))

    def of(prefix):
        return {k[len(prefix):]: v for k, v in I.items() if k.startswith(prefix)}
    x0, f0, x1, f1 = of("L0_xattn_"), of("L0_ffn_"), of("L1_xattn_"), of("L1_ffn_")
    x3, f3 = of("L3_xattn_"), of("L3_ffn_")

    def features_first(w):
        return w.transpose(1, 0, 2).reshape(w.shape[1], -1)

    def swapped(w):
        half = w.shape[1] // 2
        return np.concatenate([w[:, half:], w[:, :half]], 1)

    causal = np.where(np.tril(np.ones((P, P), bool)), 0.0, MASKED)
    tail = np.zeros((WIDTH, 1), np.float32)
    gate_up = np.stack([np.concatenate([f1["sh_gate"][None], f1["r_gate"]]),
                        np.concatenate([f1["sh_up"][None], f1["r_up"]])], 1)
    k_repeated = np.repeat(x3["w_k"].reshape(G3, 1, HD3, WIDTH), HPG, 1).reshape(WIDTH, WIDTH)
    none = np.zeros((LATENT, P), np.float32)
    up = np.concatenate([np.concatenate([none, f1["k_u_w"], none, f1["v_u_w"]], 1),
                         np.concatenate([f1["q_u_w"], none, f1["rope_q_w"], none, none], 1)], 0)
    arrays = {
        "x": I["x"], "ctx": I["ctx_2048"],
        "ctxT": I["ctx_2048"].transpose(0, 2, 1).reshape(SEQUENCES, KB, P, P).transpose(0, 2, 1, 3).reshape(SEQUENCES, P, WIDTH),
        "seg": I["itok_BxS_0_1023"].reshape(ROUNDS, STREAMS, P).transpose(0, 2, 1),
        "keep": I["mask_BxS2_bk0"].reshape(ROUNDS, STREAMS * P),
        "pad": I["mask_BxS2_if1"].reshape(ROUNDS, STREAMS * P),
        "const": constants(), "constb": np.concatenate([np.eye(P), causal], 1).astype(ml_dtypes.bfloat16),
        "rows": np.concatenate([x0["b_v"], f1["ln1_w"], f1["ln2_w"], I["L2_ffn_bias"], x3["b_o"], f1["router_b"],
                                np.zeros(1, np.float32), f0["imp_center"], f0["imp_slope"]]),
        "w0": pack(W0_NAMES, {"fc": by_block(x0["W_fc"].T), "q": by_block(x0["W_q"].T), "k": by_block(x0["W_k"].T),
                              "v": by_block(x0["W_v"].reshape(WIDTH, WIDTH).T), "b_fc": x0["b_fc"].reshape(KB, P).T,
                              "b_q": x0["b_q"].reshape(KB, P).T, "b_k": x0["b_k"].reshape(KB, P).T}),
        "w0f": pack(W0F_NAMES, {
            "sel": by_block(np.concatenate([features_first(f0["select_weight"]), features_first(f0["lora_update"]),
                                            f0["select_mean_diff"].T], 1)),
            "debias": by_block(f0["debias_w"].T),
            "lift": pad_rows(np.concatenate([f0["lora_degen"].transpose(0, 2, 1).reshape(-1, WIDTH), f0["bias_w"]]))}),
        "w1": pack(W1_NAMES, {"kvc": by_block(x1["W_kvc"]), "dq": by_block(x1["W_dq"])}),
        "w1p": pack(W1P_NAMES, {"uqT": x1["W_uq"].reshape(QC, H1, P).transpose(2, 1, 0).reshape(P, -1),
                                "ukT": x1["W_uk"].reshape(KVC, H1, P).transpose(2, 1, 0).reshape(P, -1),
                                "uvT": x1["W_uv"].reshape(KVC, H1, P).transpose(2, 1, 0).reshape(P, -1),
                                "o": by_block(x1["W_o"]), "kvcT": pad_rows(x1["W_kvc"].T), "qr": pad_rows(x1["W_qr"]),
                                "kr": pad_rows(np.concatenate([x1["W_kr"], swapped(x1["W_kr"])], 1))}),
        "w1f": pack(W1F_NAMES, {"down_kq": by_block(np.concatenate([f1["kv_d_w"], f1["q_d_w"]], 1)), "up": up,
                                "rope_k": by_block(f1["rope_k_w"]), "o": by_block(f1["o_w"]),
                                "router": by_block(np.concatenate([f1["router_w"], tail], 1))}),
        "wm": pack(WM_NAMES, {"gate_up": by_block(gate_up.transpose(2, 0, 1, 3).reshape(WIDTH, -1)),
                              "down": by_block(np.concatenate([f1["sh_down"][None], f1["r_down"]]).reshape(-1, WIDTH))}),
        "w2f": by_block(I["L2_ffn_weight"]),
        "w3": pack(W3_NAMES, {"q": by_block(x3["w_q"].T), "k": by_block(k_repeated.T), "v": by_block(x3["w_v"].T),
                              "o": by_block(x3["w_o"].T)}),
        "w3f": pack(W3F_NAMES, {"fc": by_block(f3["w_fc"].T), "proj": by_block(f3["w_proj"].T)}),
    }
    nc = bacc.Bacc("TRN2", target_bir_lowering=False, num_devices=1)
    A = {n: nc.dram_tensor(f"in_{n}", shape, dt, kind="ExternalInput").ap() for n, shape, dt in INPUT_SHAPES}
    A["out"] = nc.dram_tensor("out", (SEQUENCES, P, WIDTH), F32, kind="ExternalOutput").ap()
    program(nc, A)
    data = {f"in_{n}": np.ascontiguousarray(arrays[n]) for n, _, _ in INPUT_SHAPES}
    for n, shape, _ in INPUT_SHAPES:
        assert data[f"in_{n}"].shape == shape, (n, data[f"in_{n}"].shape)
    return run_bass_kernel_spmd(nc, [data], core_ids=[0]).results[0]["out"]
```

```python
from contextlib import ExitStack

import numpy as np

import concourse.bass as bass
from concourse import mybir

F32 = mybir.dt.float32
BF16 = mybir.dt.bfloat16
I32 = mybir.dt.int32
U8 = mybir.dt.uint8
ALU = mybir.AluOpType
ACT = mybir.ActivationFunctionType
X_AXIS = mybir.AxisListType.X

P = 128
SEQUENCES, TOKENS, WIDTH = 16, 128, 256
KB = WIDTH // P
STREAMS = 4
ROUNDS = SEQUENCES // STREAMS
PAIRS = STREAMS // 2
BOTH = [(2 * p, 2 * p + 1) for p in range(PAIRS)]
EPS = 1e-5
MASKED = -1e30
LAYERS = 8
WARM_Z, WARM_T, WARM_O, WARM_R, WARM_Q = (16, 4, 2, 2), 6, 10, (0, 0, 0, 0), 0
STEPS = 1024

H0, HD0 = 16, 16
N_SEL, SEL, LORA = 8, 8, 8
H1, HD1, KVC, QC, ROPE = 16, 128, 64, 96, 64
LOOKBACK = 8
LF, RD, LATENT = 16, 8, 64
EXPERTS, INNER, EXPERT_SCALE = 8, 128, 8.0
H3, HD3, G3 = 32, 8, 8
HPG = H3 // G3
FF3 = 640
FB3 = FF3 // P
SLOT = 32
GROUP = 8

ROW_NAMES = [("b_v", WIDTH), ("ln1", WIDTH), ("ln2", WIDTH), ("bias2", WIDTH), ("b_o", WIDTH),
             ("router_b", EXPERTS), ("center", N_SEL), ("slope", N_SEL)]
CONST_NAMES = [("ident", P), ("even", 1), ("odd", 1), ("quarter", HPG), ("key", P), ("falling", EXPERTS),
               ("cos_q", ROPE), ("sin_q", ROPE), ("cos_kT", P), ("sin_kT", P), ("cos_f", RD), ("sin_f", RD)]
W0_NAMES = [("fc", KB * WIDTH), ("q", KB * WIDTH), ("k", KB * WIDTH), ("v", KB * WIDTH),
            ("b_fc", KB), ("b_q", KB), ("b_k", KB)]
SELW = N_SEL * SEL + N_SEL * LORA + N_SEL
W0F_NAMES = [("sel", KB * SELW), ("debias", KB * N_SEL), ("lift", WIDTH)]
W1_NAMES = [("kvc", KB * KVC), ("dq", KB * QC)]
W1P_NAMES = [("uqT", H1 * QC), ("ukT", H1 * KVC), ("uvT", H1 * KVC), ("o", H1 * WIDTH),
             ("kvcT", KB * P), ("qr", H1 * ROPE), ("kr", 2 * ROPE)]
W1F_NAMES = [("down_kq", KB * P), ("up", 3 * P + WIDTH), ("rope_k", KB * P), ("o", KB * WIDTH),
             ("router", KB * EXPERTS)]
WM_NAMES = [("gate_up", KB * EXPERTS * 2 * INNER), ("down", EXPERTS * WIDTH)]
W3_NAMES = [("q", KB * WIDTH), ("k", KB * WIDTH), ("v", KB * G3 * HD3), ("o", KB * WIDTH)]
W3F_NAMES = [("fc", KB * FF3), ("proj", FB3 * WIDTH)]


def width(names):
    return sum(n for _, n in names)


def columns(tile, names):
    out, at = {}, 0
    for name, n in names:
        out[name] = tile[:, at:at + n]
        at += n
    return out


def blocks(ap, n):
    return ap.rearrange("p (b n) -> p b n", b=n)


class Ring:

    def __init__(self, jobs, slots):
        self.place, self.uses = {}, [0] * slots
        for n, job in enumerate(jobs):
            assert job not in self.place, job
            self.uses[n % slots] += 1
            self.place[job] = (n % slots, self.uses[n % slots])


def each(*names):
    return [(name, s) for name in names for s in range(STREAMS)]


def pairwise(*names):
    return [(name, s) for pair in BOTH for name in names for s in pair]


def units(groups):
    return [(s, g) for s in range(STREAMS) for g in range(groups)]


TAGS = ["0", "0f", "1", "1f", "2", "2f", "3", "3f"]


def program(nc, A, layers=LAYERS):
    tags = TAGS[:layers]
    FINAL = {"0": "0 ref rows", "0f": "0f mod", "1": "1 out", "1f": "1f moe", "2": "2 av", "2f": "2f out", "3": "3 out", "3f": "3f out"}[tags[-1]]

    def attn(layer, groups, per=1):
        return [(f"{layer} av", s, g, a) for s, g in units(groups) for a in range(per)]

    def narrow_attn(layer, groups):
        order = units(groups)
        return [job for t in range(len(order) + 1)
                for job in ([(f"{layer} av",) + order[t]] if t < len(order) else [])
                + ([(f"{layer} ao",) + order[t - 1]] if t else [])]

    moe_jobs = each("1f moe")[:-1] + each("3 v") + each("1f moe")[-1:]
    keys3 = each("3 k")

    general_jobs = (
        each("0 sup", "0 k", "0 v", "0 zT", "0 ref", "0 q") + narrow_attn("0", 2) + each("0 ref rows")
        + pairwise("0f zT", "0f sel") + each("1 k", "1 kv", "0f mod")
        + pairwise("1 zT", "1 qc") + attn("1", 2, 2) + each("1 out")
        + pairwise("1f zT", "1f kq") + narrow_attn("1f", 2) + each("1f out", "1f router") + moe_jobs
        + each("2 zT") + attn("2", 1) + keys3[:2] + pairwise("2f zT", "2f out") + keys3[2:]
        + pairwise("3 zT", "3 q") + narrow_attn("3", 4) + each("3 out")
        + each("3f zT", "3f out"))
    score_jobs = (
        [("0 s",) + u for u in units(2)] + [("1 q",) + u for u in units(2)] + [("1 s",) + u for u in units(2)]
        + each("1f rows") + [("1f s",) + u for u in units(2)] + [("1f gu",) + u for u in units(2)]
        + [("2 s",) + u for u in units(1)] + [("3 s",) + u for u in units(4)] + each("3f h"))
    turn_jobs = (
        [("0 t",) + u + (a,) for u in units(2) for a in range(2)] + each("0f onehot")
        + [("1 q",) + u + (a,) for u in units(2) for a in range(2)]
        + [("1 t",) + u + (a,) for u in units(2) for a in range(2)]
        + [("1 o", s, a) for s in range(STREAMS) for a in range(2)]
        + each("1f qk") + [("1f t",) + u + (a,) for u in units(2) for a in range(2)] + each("1f o", "1f h")
        + [("1f m",) + u for u in units(2)]
        + [("2 t",) + u + (0,) for u in units(1)] + [("3 t",) + u + (a,) for u in units(4) for a in range(2)]
        + each("3 o"))
    def kept(jobs):
        return [j for j in jobs if (j if isinstance(j, str) else j[0]).split()[0] in tags]

    general, score, turn = (Ring(kept(jobs), 2) for jobs in (general_jobs, score_jobs, turn_jobs))
    powers = [(n, p) for n in kept(["0", "0f", "1", "1f", "1f h", "2", "2f", "3", "3f"]) for p in range(PAIRS)]
    normalised = [(n, s) for n in tags for s in range(STREAMS)]
    biased = [(n, s) for n in kept(["0", "1f", "2f", "3"]) for s in range(STREAMS)]
    weighted_rows = [(n, s) for n in kept(["1f z", "1f h"]) for s in range(STREAMS)]
    act_reads = kept([("1 q",) + u for u in units(2)] + each("1f rows"))
    attention = [(tag, s, g) for tag, groups in (("0", 2), ("1", 2), ("1f", 2), ("2", 1), ("3", 4)) if tag in tags
                 for s, g in units(groups)]
    prob_jobs = [(tag, s, g, a) for tag, s, g in attention for a in range(1 if tag == "2" else 2)]

    with ExitStack() as ctx:
        def sb(name, cols, dt=F32):
            return ctx.enter_context(nc.sbuf_tensor(name, [P, cols], dt))

        def sem(name):
            return ctx.enter_context(nc.semaphore(name))

        const = sb("const", width(CONST_NAMES))
        C = columns(const, CONST_NAMES)
        at_kT = width(CONST_NAMES[:[n for n, _ in CONST_NAMES].index("cos_kT")])
        cos_sin_kT = const[:, at_kT:at_kT + 2 * P]
        constb = sb("constb", 2 * P, BF16)
        ident_b, causal_b = constb[:, 0:P], constb[:, P:2 * P]
        rows = sb("rows", width(ROW_NAMES))
        R = columns(rows, ROW_NAMES)
        w0, w0f, w1 = sb("w0", width(W0_NAMES)), sb("w0f", width(W0F_NAMES)), sb("w1", width(W1_NAMES))
        w1f, wm = sb("w1f", width(W1F_NAMES)), sb("wm", width(WM_NAMES))
        w2f = sb("w2f", KB * WIDTH)
        w3, w3f = sb("w3", width(W3_NAMES)), sb("w3f", width(W3F_NAMES))
        W0, W0F, W1, W1F = columns(w0, W0_NAMES), columns(w0f, W0F_NAMES), columns(w1, W1_NAMES), columns(w1f, W1F_NAMES)
        WM, W3, W3F = columns(wm, WM_NAMES), columns(w3, W3_NAMES), columns(w3f, W3F_NAMES)
        w_query = sb("w_query", H1 * P)
        w_kv = sb("w_kv", KB * P)
        w_kv_swap = sb("w_kv_swap", KB * ROPE)
        w_out = sb("w_out", H1 // 2 * WIDTH)
        sel_const = sb("sel_const", P + N_SEL)
        ones = sb("ones", P)
        minus_half = sb("minus_half", 4)
        bias_k = sb("bias_k", 2 * KB)

        def per_stream(name, cols, dt=F32):
            return [sb(f"{name}{s}", cols, dt) for s in range(STREAMS)]
        x_in, x, z = (per_stream(n, WIDTH) for n in ("x_in", "x", "z"))
        zT = per_stream("zT", WIDTH)
        cx, cxT = per_stream("cx", WIDTH + 2), per_stream("cxT", WIDTH)
        tA, tB = (per_stream(n, WIDTH) for n in ("tA", "tB"))
        hres, headsT, hrow = tA, tA, tB
        big = per_stream("big", 2048)
        heads_out = [b[:, 1024:2048] for b in big]
        values = per_stream("values", H0 * SLOT)
        values1 = per_stream("values1", KVC + 1)
        qcT, kcT = per_stream("qcT", P), per_stream("kcT", P)
        sel, onehot = sb("sel", STREAMS * P), sb("onehot", STREAMS * P)
        onehotT = per_stream("onehotT", P)
        stats = per_stream("stats", 6)
        mean_var = sb("mean_var", 2 * STREAMS)
        var_eps, rstd = sb("var_eps", 4 * PAIRS), sb("rstd", 4 * PAIRS)
        square_sum = sb("square_sum", STREAMS)
        small = sb("small", (6 * 8 + 3) * STREAMS)
        largest, less_gate = sb("largest", STREAMS), sb("less_gate", STREAMS)
        squares = sb("squares", 64 * STREAMS)
        expert_w = sb("expert_w", EXPERTS * STREAMS)
        seg_i, keep_i, pad_i = sb("seg_i", STREAMS, I32), sb("keep_i", STREAMS * P, U8), sb("pad_i", STREAMS * P, I32)
        seg_f, seg_lo = sb("seg_f", STREAMS), sb("seg_lo", STREAMS)
        valid = sb("valid", STREAMS)
        above, below = sb("above", STREAMS * P), sb("below", STREAMS * P)
        mask1, mask2, mask3 = (per_stream(n, P, BF16) for n in ("mask1", "mask2", "mask3"))
        shifted = sb("shifted", 2 * GROUP * P)
        probs = sb("probs", 4 * 4 * P)
        narrow_out = sb("narrow_out", 2 * GROUP * SLOT)
        peak = sb("peak", 2 * GROUP)
        inverse = sb("inverse", 2 * GROUP)
        q_rows, q_swap = shifted, probs
        tiny = sb("tiny", 10)

        score_psum = [ctx.enter_context(nc.psum_tensor(f"score_psum{i}", [P, 1024], F32)) for i in range(2)]
        turn_psum = [ctx.enter_context(nc.psum_tensor(f"turn_psum{i}", [P, 512], F32)) for i in range(2)]
        general_psum = [ctx.enter_context(nc.psum_tensor(f"general_psum{i}", [P, 512], F32)) for i in range(2)]

        for ring, name, banks in ((score, "score", score_psum), (turn, "turn", turn_psum), (general, "general", general_psum)):
            ring.banks = banks
            ring.filled = [sem(f"{name}_filled{i}") for i in range(2)]
            ring.emptied = [sem(f"{name}_emptied{i}") for i in range(2)]

        loaded = {n: sem(f"{n}_loaded") for n in
                  ["w0", "w0f", "w1", "w1f", "wm", "w2f", "w3", "w3f", "const", "constb", "rows", "prep"]}
        x_loaded, cx_loaded, cxT_loaded = ([sem(f"{n}_loaded{s}") for s in range(STREAMS)] for n in ("x", "cx", "cxT"))
        masks_loaded, x_stored = sem("masks_loaded"), sem("x_stored")
        prep_filled, prep_steps, prep_done = sem("prep_filled"), sem("prep_steps"), sem("prep_done")
        vec_steps = sem("vec_steps")
        power_in, power_out = sem("power_in"), sem("power_out")
        z_ready = sem("z_ready")
        x_biased = sem("x_biased")
        act_read = sem("act_read")
        q_rotated, qk_ready = sem("q_rotated"), sem("qk_ready")
        gates_in, gates_exp = sem("gates_in"), sem("gates_exp")
        z_squared, h_squared = sem("z_squared"), sem("h_squared")
        onehot_ready = sem("onehot_ready")
        rows_ready = sem("rows_ready")
        router_exp = sem("router_exp")
        tanh_done = sem("tanh_done")
        x_free = sem("x_free")
        keys_copied, keys_turned = sem("keys_copied"), sem("keys_turned")
        keys_ready = sem("keys_ready")
        relu_squared = sem("relu_squared")
        mask_steps, masks_ready = sem("mask_steps"), sem("masks_ready")
        ones_ready, holds = sem("ones_ready"), sem("holds")

        def count(r, events, *event):
            return r * len(events) + events.index(event) + 1

        def nth(r, s):
            return r * STREAMS + s + 1

        waited = {}

        def wait_slot(eng, semaphore, r, uses, k):
            if waited.get((eng, semaphore.name), 0) < k:
                waited[eng, semaphore.name] = k
                eng.wait_ge(semaphore, r * uses + k)

        def filled(eng, ring, r, *job):
            slot, k = ring.place[job]
            wait_slot(eng, ring.filled[slot], r, ring.uses[slot], k)
            return ring.banks[slot]

        def hold(eng):
            eng.sem_inc(holds, 1)

        def free(eng, ring, r, *job):
            slot, k = ring.place[job]
            wait_slot(eng, ring.emptied[slot], r, ring.uses[slot], k)
            return ring.banks[slot]

        def moved(eng, ring, r, *job):
            slot, k = ring.place[job]
            wait_slot(eng, ring.emptied[slot], r, ring.uses[slot], k + 1)

        def all_moved(eng, ring, r, jobs):
            for job in sorted(jobs, key=lambda job: -ring.place[job][1]):
                moved(eng, ring, r, *job)

        def emptied(ring, *job):
            return ring.emptied[ring.place[job][0]]

        def fill(ring, *job):
            return ring.filled[ring.place[job][0]]

        def cell(i):
            return small[:, 8 * STREAMS * i:8 * STREAMS * (i + 1)]

        def of_each(i, n=8):
            return cell(i).rearrange("p (s n) -> p s n", s=STREAMS)[:, :, 0:n]

        def lone(i):
            at = (6 * 8 + i) * STREAMS
            return small[:, at:at + STREAMS]

        def heads(ap, n):
            return ap.rearrange("p (h n) -> p h n", h=n)

        def spread(ap, n):
            return ap.unsqueeze(2).to_broadcast([P, ap.shape[1], n])

        def repeat(ap, n):
            return ap.unsqueeze(1).to_broadcast([P, n, ap.shape[1]])

        def same_slot_before(tag, s, g):
            at = attention.index((tag, s, g))
            slot = score.place[(f"{tag} s", s, g)][0]
            for u in reversed(attention[:at]):
                if score.place[(f"{u[0]} s", u[1], u[2])][0] == slot:
                    return u
            return None

        def last_turn(tag, s, g):
            return (f"{tag} t", s, g, 0 if tag == "2" else 1)

        def small_head(g, i):
            q, c, e = i // 4, (i % 4) // 2, i % 2
            return c * 8 + 4 * g + 2 * q + e

        W1P = {"uqT": big[0][:, 0:H1 * QC], "ukT": big[1][:, 0:H1 * KVC], "uvT": big[1][:, 1024:1024 + H1 * KVC],
               "o0": big[2][:, :], "o1": big[3][:, :],
               "kvcT": shifted[:, 0:KB * P], "qr": shifted[:, 256:256 + H1 * ROPE], "kr": shifted[:, 1280:1280 + 2 * ROPE]}
        w2f_rows = shifted[:, 1408:1408 + KB * WIDTH]
        sel_prod = big[0][:, H1 * QC:H1 * QC + KB * SELW]
        alpha, total, ternary = inverse[:, 0:KB], inverse[:, 2:4], inverse[:, 4:10]

        block = ctx.enter_context(nc.Block())

        @block.sync
        def _(sp):
            sp.dma_start(w0f[:, :], A["w0f"]).then_inc(loaded["w0f"], 16)
            sp.dma_start(w3f[:, :], A["w3f"]).then_inc(loaded["w3f"], 16)
            sp.dma_start(w2f_rows[:, :], A["w2f"]).then_inc(loaded["w2f"], 16)
            sp.dma_start(const[:, :], A["const"]).then_inc(loaded["const"], 16)
            sp.dma_start(w1[:, :], A["w1"]).then_inc(loaded["w1"], 16)
            at = 0
            for part in W1P.values():
                cols = part.shape[1]
                sp.dma_start(part, A["w1p"][:, at:at + cols]).then_inc(loaded["prep"], 16)
                at += cols
            sp.dma_start(constb[:, :], A["constb"]).then_inc(loaded["constb"], 16)
            sp.dma_start(rows[:, :], A["rows"].partition_broadcast(P)).then_inc(loaded["rows"], 16)
            sp.dma_start(w0[:, :], A["w0"]).then_inc(loaded["w0"], 16)
            for s in range(STREAMS):
                sp.dma_start(cxT[s][:, :], A["ctxT"][bass.ds(s, 1)].squeeze(0)).then_inc(cxT_loaded[s], 16)

            def load_context(s, sequence):
                sp.dma_start(cxT[s][:, :], A["ctxT"][sequence].squeeze(0)).then_inc(cxT_loaded[s], 16)

            def load_rows(s, sequence):
                sp.dma_start(cx[s][:, 0:WIDTH], A["ctx"][sequence].squeeze(0)).then_inc(cx_loaded[s], 16)

            def load_x(s, sequence):
                sp.dma_start(x_in[s][:, :], A["x"][sequence].squeeze(0)).then_inc(x_loaded[s], 16)

            def load_masks(now):
                sp.dma_start(seg_i[:, :], A["seg"][now].squeeze(0)).then_inc(masks_loaded, 16)
                sp.dma_start(keep_i[:, :], A["keep"][now].to_broadcast([P, STREAMS * P])).then_inc(masks_loaded, 16)
                sp.dma_start(pad_i[:, :], A["pad"][now].to_broadcast([P, STREAMS * P])).then_inc(masks_loaded, 16)

            def store(r):
                for s in range(STREAMS):
                    moved(sp, general, r, FINAL, s)
                    hold(sp)
                    sp.dma_start(A["out"][bass.ds(r * STREAMS + s, 1)].squeeze(0), x[s][:, :]).then_inc(x_stored, 16)
                sp.wait_ge(x_stored, r * (16 * STREAMS) + 16 * STREAMS)
                sp.sem_inc(x_free, 1)

            sp.sem_inc(x_free, 1)
            load_masks(bass.ds(0, 1))
            for load in (load_x, load_rows):
                for s in range(STREAMS):
                    load(s, bass.ds(s, 1))
            with sp.Fori(0, ROUNDS - 1) as r:
                sp.wait_ge(masks_ready, r + 1)
                hold(sp)
                for s in (STREAMS - 1, STREAMS - 2):
                    moved(sp, general, r, "0 ref rows", s)
                    hold(sp)
                load_masks(bass.ds(r + 1, 1))
                for s in range(STREAMS):
                    load_x(s, bass.ds(r * STREAMS + (STREAMS + s), 1))
                for s in (STREAMS - 1, STREAMS - 2):
                    filled(sp, general, r, "2 av", s, 0, 0)
                    hold(sp)
                for s in range(STREAMS):
                    load_rows(s, bass.ds(r * STREAMS + (STREAMS + s), 1))
                for s in range(STREAMS):
                    filled(sp, general, r, "3 k", s)
                    hold(sp)
                    load_context(s, bass.ds(r * STREAMS + (STREAMS + s), 1))
                store(r)
            waited.clear()
            store(ROUNDS - 1)

        @block.gpsimd
        def _(pool):
            nc.gpsimd.memset(minus_half[:, :], -0.5)
            for s in range(STREAMS):
                for tile in (values[s], values1[s]):
                    nc.gpsimd.memset(tile[:, :], 1.0)
                nc.gpsimd.memset(cx[s][:, WIDTH:WIDTH + 2], 1.0)
            nc.gpsimd.memset(onehot[:, :], 0.0)
            nc.gpsimd.memset(expert_w[:, :], 0.5 / EXPERT_SCALE)
            nc.gpsimd.memset(ones[:, :], 1.0).then_inc(ones_ready, 1)
            pool.wait_ge(ones_ready, 1)
            pool.wait_ge(loaded["w0"], 16)
            for name, tile in (("w1f", w1f), ("wm", wm), ("w3", w3)):
                pool.dma_start(tile[:, :], A[name]).then_inc(loaded[name], 16)
            for name in ("const", "constb", "rows"):
                pool.wait_ge(loaded[name], 16)

            def power(r, name, n=2):
                for p in range(PAIRS):
                    pool.wait_ge(power_in, count(r, powers, name, p))
                    nc.gpsimd.tensor_tensor(rstd[:, 4 * p:4 * p + n], var_eps[:, 4 * p:4 * p + n], minus_half[:, 0:n],
                                            ALU.pow).then_inc(power_out, 1)

            def add_bias(r, tag, tile, bias):
                for s in range(STREAMS):
                    pool.wait_ge(z_ready, count(r, normalised, tag, s))
                    nc.gpsimd.tensor_tensor(tile[s][:, :], tile[s][:, :], bias, ALU.add).then_inc(x_biased, 1)

            with pool.Fori(0, ROUNDS) as r:
                power(r, "0")
                pool.wait_ge(masks_loaded, r * 48 + 48)
                hold(pool)
                nc.gpsimd.tensor_copy(seg_f[:, :], seg_i[:, :]).then_inc(mask_steps, 1)
                pool.wait_ge(mask_steps, r * 3 + 1)
                hold(pool)
                nc.gpsimd.tensor_scalar(seg_lo[:, :], seg_f[:, :], float(LOOKBACK), None, ALU.subtract)
                for s in range(STREAMS):
                    own = slice(s * P, s * P + P)
                    nc.gpsimd.tensor_scalar(above[:, own], C["key"], seg_f[:, s:s + 1], MASKED, ALU.is_gt, ALU.mult)
                    nc.gpsimd.tensor_scalar(mask2[s][:, :], keep_i[:, own], 1.0, -MASKED, ALU.subtract, ALU.mult)
                    ins = nc.gpsimd.tensor_scalar(mask3[s][:, :], pad_i[:, own], 0.0, MASKED, ALU.is_equal, ALU.mult)
                ins.then_inc(mask_steps, 1)
                pool.wait_ge(mask_steps, r * 3 + 2)
                hold(pool)
                for s in range(STREAMS):
                    own = slice(s * P, s * P + P)
                    ins = nc.gpsimd.tensor_scalar(below[:, own], C["key"], seg_lo[:, s:s + 1], MASKED, ALU.is_lt, ALU.mult)
                ins.then_inc(mask_steps, 1)
                for s in range(STREAMS):
                    nc.gpsimd.tensor_tensor(mask3[s][:, :], mask3[s][:, :], causal_b, ALU.add)
                pool.wait_ge(mask_steps, r * 3 + 3)
                for s in range(STREAMS):
                    own = slice(s * P, s * P + P)
                    ins = nc.gpsimd.tensor_tensor(mask1[s][:, :], above[:, own], below[:, own], ALU.add)
                ins.then_inc(masks_ready, 1)
                add_bias(r, "0", x_in, R["b_v"])
                if "0f" in tags:
                    power(r, "0f")
                if "1" in tags:
                    for s in range(STREAMS):
                        pool.wait_ge(keys_copied, nth(r, s))
                        both = tB[s][KVC:P, :]
                        nc.gpsimd.tensor_tensor(both, both, cos_sin_kT[KVC:P, :], ALU.mult).then_inc(keys_turned, 1)
                        pool.wait_ge(keys_turned, nth(r, s))
                        nc.gpsimd.tensor_tensor(kcT[s][KVC:P, :], both[:, 0:P], both[:, P:2 * P], ALU.add).then_inc(keys_ready, 1)
                    pool.wait_ge(keys_ready, nth(r, STREAMS - 1))
                    hold(pool)
                    power(r, "1")
                if "1f" in tags:
                    power(r, "1f", 4)
                    power(r, "1f h")
                    for s in range(STREAMS):
                        moved(pool, general, r, "1f out", s)
                        nc.gpsimd.tensor_tensor(x[s][:, :], x[s][:, :], hres[s][:, :], ALU.add).then_inc(x_biased, 1)
                if "2" in tags:
                    power(r, "2")
                if "2f" in tags:
                    power(r, "2f")
                    add_bias(r, "2f", x, R["bias2"])
                if "3" in tags:
                    power(r, "3")
                    add_bias(r, "3", x, R["b_o"])
                if "3f" in tags:
                    power(r, "3f")

        @block.scalar
        def _(act):
            for name in ("const", "w0"):
                act.wait_ge(loaded[name], 16)
            act.wait_ge(prep_done, 4)

            def copy_out(r, ring, job, out, source=lambda bank: bank[:, :]):
                bank = filled(act, ring, r, *job)
                nc.scalar.activation(out, source(bank), ACT.Copy).then_inc(emptied(ring, *job), 1)

            def turned(r, name, streams=range(STREAMS)):
                for s in streams:
                    copy_out(r, general, (name, s), zT[s][:, :], lambda bank: bank[:, 0:WIDTH])

            def biased_blocks(r, name, out, func, bias):
                for s in range(STREAMS):
                    bank = filled(act, general, r, name, s)
                    for b in range(KB):
                        ins = nc.scalar.activation(out[s][:, b * P:b * P + P], bank[:, b * P:b * P + P], func,
                                                   bias=bias[:, b:b + 1], scale=1.0)
                    ins.then_inc(emptied(general, name, s), 1)

            def copy_narrow(r, tag, u, unit):
                at = u % 2 * GROUP * SLOT
                copy_out(r, general, (f"{tag} av",) + unit, narrow_out[:, at:at + GROUP * SLOT], lambda bank: bank[:, 0:GROUP * SLOT])

            def exponentials(r, tag, groups, scale, turns=2, per_turn=4, narrow=True):
                order = units(groups)
                for u, (s, g) in enumerate(order):
                    for a in range(turns):
                        job = (f"{tag} t", s, g, a)
                        n = prob_jobs.index((tag, s, g, a))
                        if n >= 4:
                            before = prob_jobs[n - 4]
                            filled(act, general, r, f"{before[0]} av", before[1], before[2], *([before[3]] if before[0] in "12" else []))
                        bank = filled(act, turn, r, *job)
                        at = (n % 4) * 512
                        nc.scalar.activation(probs[:, at:at + per_turn * P], bank[:, 0:per_turn * P], ACT.Exp,
                                             scale=scale).then_inc(emptied(turn, *job), 1)
                    if narrow and u:
                        copy_narrow(r, tag, u - 1, order[u - 1])
                if narrow:
                    copy_narrow(r, tag, len(order) - 1, order[-1])

            def keys3_out(r, streams):
                for s in streams:
                    bank = filled(act, general, r, "3 k", s)
                    out = big[s][:, 0:KB * HPG * P].rearrange("p (b h k) -> p b h k", b=KB, h=HPG)
                    for h in range(HPG):
                        ins = nc.scalar.activation(out[:, :, h, :], heads(bank[:, 0:WIDTH], KB), ACT.Copy, scale=C["quarter"][:, h:h + 1])
                    ins.then_inc(emptied(general, "3 k", s), 1)

            with act.Fori(0, ROUNDS) as r:
                biased_blocks(r, "0 sup", tB, ACT.Relu, W0["b_fc"])
                for s in range(STREAMS):
                    bank = filled(act, general, r, "0 k", s)
                    for b in range(KB):
                        for e, mask in enumerate(("even", "odd")):
                            at = (2 * b + e) * P
                            ins = nc.scalar.activation(big[s][:, at:at + P], bank[:, b * P:b * P + P], ACT.Identity,
                                                       bias=bias_k[:, 2 * b + e:2 * b + e + 1], scale=C[mask])
                    ins.then_inc(emptied(general, "0 k", s), 1)
                for s in range(STREAMS):
                    copy_out(r, general, ("0 v", s), heads(values[s][:, :], H0)[:, :, 0:HD0],
                             lambda bank: heads(bank[:, 0:WIDTH], H0))
                turned(r, "0 zT")
                biased_blocks(r, "0 ref", tA, ACT.Relu, W0["b_fc"])
                biased_blocks(r, "0 q", zT, ACT.Identity, W0["b_q"])
                exponentials(r, "0", 2, HD0 ** -0.5)
                if "0f" in tags:
                    turned(r, "0f zT")
                    for s in range(STREAMS):
                        act.wait_ge(z_ready, count(r, normalised, "0f", s))
                        nc.scalar.activation(big[s][:, 1536:1792], z[s][:, :], ACT.Square,
                                             accum_out=square_sum[:, s:s + 1]).then_inc(z_squared, 1)
                    if "1" in tags:
                        for s in range(STREAMS):
                            bank = filled(act, general, r, "1 k", s)
                            nc.scalar.activation(tB[s][KVC:P, :], bank[KVC:P, 0:2 * P], ACT.Copy).then_inc(keys_copied, 1)
                            nc.scalar.activation(kcT[s][0:KVC, :], bank[0:KVC, 0:P], ACT.Copy).then_inc(emptied(general, "1 k", s), 1)
                        for s in range(STREAMS):
                            copy_out(r, general, ("1 kv", s), values1[s][:, 0:KVC], lambda bank: bank[:, 0:KVC])
                    act.wait_ge(gates_in, r + 1)
                    nc.scalar.activation(cell(3), cell(2), ACT.Exp, scale=-1.0).then_inc(gates_exp, 1)
                    for s in range(STREAMS):
                        copy_out(r, turn, ("0f onehot", s), onehotT[s][:, :], lambda bank: bank[:, 0:P])
                if "1" in tags:
                    for pair in BOTH:
                        turned(r, "1 zT", pair)
                        for s in pair:
                            copy_out(r, general, ("1 qc", s), qcT[s][0:QC, :], lambda bank: bank[0:QC, 0:P])
                    order = units(2)
                    for t in range(len(order) + 1):
                        if t < len(order):
                            s, g = order[t]
                            slot = score.place[("1 q", s, g)][0]
                            if t >= 2:
                                filled(act, turn, r, "1 q", *order[t - 2], 1)
                            bank = filled(act, score, r, "1 q", s, g)
                            nc.scalar.activation(heads(q_rows[:, slot * 1024:(slot + 1) * 1024], GROUP)[:, :, 0:KVC],
                                                 heads(bank[:, :], GROUP)[:, :, 0:KVC], ACT.Copy).then_inc(act_read, 1)
                        if t >= 1:
                            s, g = order[t - 1]
                            for a in range(2):
                                at = (g * GROUP + a * 4) * P
                                copy_out(r, turn, ("1 q", s, g, a), big[s][:, at:at + 512])
                    exponentials(r, "1", 2, float((HD1 + ROPE) ** -0.5), narrow=False)
                    for s in range(STREAMS):
                        for a in range(2):
                            copy_out(r, turn, ("1 o", s, a), big[s][:, a * 1024 + 512:(a + 1) * 1024])
                if "1f" in tags:
                    for pair in BOTH:
                        turned(r, "1f zT", pair)
                        for s in pair:
                            copy_out(r, general, ("1f kq", s), qcT[s][:, :], lambda bank: bank[:, 0:P])
                        for s in pair:
                            bank = filled(act, score, r, "1f rows", s)
                            nc.scalar.activation(heads(heads_out[s][:, 0:512], 2 * LF)[:, :, 0:RD],
                                                 heads(bank[:, 0:2 * P], 2 * LF), ACT.Copy)
                            nc.scalar.activation(heads(values[s][:, :], LF)[:, :, 0:2 * RD],
                                                 heads(bank[:, 512:512 + WIDTH], LF), ACT.Copy).then_inc(act_read, 1)
                    for s in range(STREAMS):
                        bank = filled(act, turn, r, "1f qk", s)
                        nc.scalar.activation(tB[s][:, :], bank[:, 0:WIDTH], ACT.Copy)
                        out = big[s][:, 0:4 * P].rearrange("p (b e k) -> p b e k", b=KB, e=2)
                        for e, mask in enumerate(("even", "odd")):
                            ins = nc.scalar.activation(out[:, :, e, :], heads(bank[:, WIDTH:2 * WIDTH], KB), ACT.Copy, scale=C[mask])
                        ins.then_inc(emptied(turn, "1f qk", s), 1)
                    exponentials(r, "1f", 2, (2 * RD) ** -0.5)
                    for s in range(STREAMS):
                        copy_out(r, turn, ("1f o", s), headsT[s][:, :], lambda bank: bank[:, 0:WIDTH])
                    for s in range(STREAMS):
                        moved(act, general, r, "1f out", s)
                        nc.scalar.activation(tB[s][:, :], hres[s][:, :], ACT.Square,
                                             accum_out=square_sum[:, s:s + 1]).then_inc(h_squared, 1)
                    for s in range(STREAMS):
                        copy_out(r, turn, ("1f h", s), zT[s][:, :], lambda bank: bank[:, 0:WIDTH])
                    all_moved(act, general, r, [("1f router", s) for s in range(STREAMS)])
                    nc.scalar.activation(cell(1), cell(0), ACT.Exp, scale=-1.0).then_inc(router_exp, 1)
                    order = units(2)
                    for t in range(len(order) + 1):
                        if t < len(order):
                            s, g = order[t]
                            slot = score.place[("1f gu", s, g)][0]
                            bank = filled(act, score, r, "1f gu", s, g)
                            gate = bank[:, :].rearrange("p (e u n) -> p e u n", e=4, u=2)[:, :, 0, :]
                            nc.scalar.activation(heads(q_rows[:, slot * 1024:slot * 1024 + 512], 4), gate, ACT.Tanh,
                                                 scale=0.5).then_inc(tanh_done, 1)
                        if t >= 1:
                            s, g = order[t - 1]
                            copy_out(r, turn, ("1f m", s, g), big[s][:, 1024 + g * 512:1536 + g * 512])
                    if "3" in tags:
                        for s in range(STREAMS):
                            copy_out(r, general, ("3 v", s), heads(values[s][:, 0:G3 * SLOT], G3)[:, :, 0:HD3],
                                     lambda bank: heads(bank[:, 0:G3 * HD3], G3))
                if "2" in tags:
                    turned(r, "2 zT")
                    exponentials(r, "2", 1, WIDTH ** -0.5, turns=1, per_turn=1, narrow=False)
                    if "3" in tags:
                        keys3_out(r, (0, 1))
                if "2f" in tags:
                    turned(r, "2f zT")
                    if "3" in tags:
                        keys3_out(r, (2, 3))
                if "3" in tags:
                    for pair in BOTH:
                        turned(r, "3 zT", pair)
                        for s in pair:
                            copy_out(r, general, ("3 q", s), zT[s][:, :], lambda bank: bank[:, 0:WIDTH])
                    exponentials(r, "3", 4, HD3 ** -0.5)
                    for s in range(STREAMS):
                        copy_out(r, turn, ("3 o", s), headsT[s][:, :], lambda bank: bank[:, 0:WIDTH])
                if "3f" in tags:
                    for pair in BOTH:
                        turned(r, "3f zT", pair)
                        for s in pair:
                            bank = filled(act, score, r, "3f h", s)
                            nc.scalar.activation(big[s][:, 0:FF3], bank[:, 0:FF3], ACT.Relu).then_inc(emptied(score, "3f h", s), 1)

        @block.vector
        def _(vec):
            steps, marks = [0], {}

            def prep(ins):
                steps[0] += 1
                ins.then_inc(prep_steps, 1)
                vec.wait_ge(prep_steps, steps[0])

            V = nc.vector
            for name in ("w0f", "w3f"):
                vec.wait_ge(loaded[name], 16)
            for b in range(KB):
                w = W0F["sel"][:, b * SELW:(b + 1) * SELW]
                mean = w[:, P:P + N_SEL]
                out = sel_prod[:, b * SELW:(b + 1) * SELW]
                V.tensor_tensor(heads(out[:, 0:64], N_SEL), heads(w[:, 0:64], N_SEL), spread(mean, SEL), ALU.mult)
                V.tensor_tensor(heads(out[:, 64:128], N_SEL), heads(w[:, 64:128], N_SEL),
                                spread(W0F["debias"][:, b * N_SEL:(b + 1) * N_SEL], LORA), ALU.mult)
                prep(V.tensor_tensor(out[:, P:P + N_SEL], mean, mean, ALU.mult))
            for i, (w, tmp) in enumerate(((W3F["fc"], probs[:, 0:KB * FF3]), (W3F["proj"], probs[:, 0:FB3 * WIDTH]))):
                prep(V.scalar_tensor_tensor(out=tmp, in0=w, scalar=-1.0, in1=w, op0=ALU.mult, op1=ALU.max))
                prep(V.tensor_reduce(total[:, i:i + 1], tmp, X_AXIS, ALU.add))
            V.memset(tiny[:, 0:1], 0.0).then_inc(prep_done, 1)
            vec.wait_ge(loaded["w2f"], 16)
            tmp = probs[:, 0:KB * WIDTH]
            w = w2f_rows[:, :]
            prep(V.scalar_tensor_tensor(out=tmp, in0=w, scalar=-1.0, in1=w, op0=ALU.mult, op1=ALU.max))
            prep(V.tensor_reduce(alpha, heads(tmp, KB), X_AXIS, ALU.add))
            prep(V.tensor_scalar(alpha, alpha, 1.0 / WIDTH, None, ALU.mult))
            prep(V.tensor_scalar(tmp, w, 0.0, 2.0, ALU.is_ge, ALU.mult))
            for b in range(KB):
                own = slice(b * WIDTH, (b + 1) * WIDTH)
                ins = V.tensor_scalar(tmp[:, own], tmp[:, own], -1.0, alpha[:, b:b + 1], ALU.add, ALU.mult)
            prep(ins)
            prep(V.tensor_tensor(tmp, tmp, w, ALU.subtract))
            prep(V.tensor_tensor(w, tmp, w, ALU.add))
            V.memset(tiny[:, 9:10], 0.0).then_inc(prep_done, 1)
            vec.wait_ge(prep_filled, 1)
            V.tensor_copy(sel_const[:, :], general_psum[0][:, 0:SELW])
            scale, thr, low = (ternary[:, i:i + 2] for i in (0, 2, 4))
            prep(V.tensor_scalar(scale, general_psum[0][:, SELW:SELW + 2], 1.0 / (FF3 * WIDTH), 1e-5, ALU.mult, ALU.max))
            V.tensor_scalar(thr, scale, 0.7, None, ALU.mult)
            prep(V.tensor_scalar(low, scale, -0.7, None, ALU.mult))
            for i, w in enumerate((W3F["fc"], W3F["proj"])):
                tmp = probs[:, 0:FB3 * WIDTH]
                prep(V.tensor_scalar(tmp, w, low[:, i:i + 1], None, ALU.is_lt))
                prep(V.scalar_tensor_tensor(out=tmp, in0=w, scalar=thr[:, i:i + 1], in1=tmp, op0=ALU.is_gt, op1=ALU.subtract))
                prep(V.scalar_tensor_tensor(out=tmp, in0=tmp, scalar=scale[:, i:i + 1], in1=w, op0=ALU.mult, op1=ALU.subtract))
                prep(V.tensor_tensor(w, w, tmp, ALU.add))
            vec.wait_ge(loaded["prep"], 16 * len(W1P))
            vec.wait_ge(loaded["w1"], 16)
            V.tensor_copy(heads(w_query[0:QC, :], H1)[:, :, KVC:P], heads(W1P["qr"][0:QC, :], H1))
            V.tensor_copy(heads(w_kv[:, :], KB)[:, :, 0:KVC], heads(W1["kvc"], KB))
            vec.wait_ge(prep_filled, 2)
            V.tensor_copy(w2f[:, :], turn_psum[0][:, :])
            vec.wait_ge(prep_filled, 3)
            kr = turn_psum[1][:, 0:KB * P].rearrange("p (b n) -> p b n", b=KB)
            V.tensor_copy(heads(w_kv[:, :], KB)[:, :, KVC:P], kr[:, :, 0:ROPE])
            V.tensor_copy(heads(w_kv_swap[:, :], KB), kr[:, :, ROPE:P])
            vec.wait_ge(prep_filled, 4)
            for i in range(2):
                bank = (general_psum[1], score_psum[0])[i]
                V.tensor_copy(heads(w_query[0:QC, :], H1)[:, GROUP * i:GROUP * (i + 1), 0:KVC], heads(bank[0:QC, 0:512], GROUP))
            V.memset(tiny[:, 1:2], 0.0).then_inc(prep_done, 1)
            vec.wait_ge(prep_filled, 5)
            for i in range(2):
                V.tensor_copy(w_out[:, 1024 * i:1024 * (i + 1)], score_psum[i][:, :])
            vec.wait_ge(loaded["w0"], 16)
            vec.wait_ge(loaded["const"], 16)
            for b in range(KB):
                for e, mask in enumerate(("even", "odd")):
                    ins = V.tensor_tensor(bias_k[:, 2 * b + e:2 * b + e + 1], W0["b_k"][:, b:b + 1], C[mask], ALU.mult)
            prep(ins)
            V.memset(tiny[:, 2:3], 0.0).then_inc(prep_done, 1)
            for i, s in enumerate(general.emptied + score.emptied + turn.emptied):
                V.memset(tiny[:, 3 + i:4 + i], 0.0).then_inc(s, 1)
            vec.wait_ge(loaded["rows"], 16)

            def step(key, ins):
                steps[0] += 1
                marks[key if isinstance(key, tuple) else (key,)] = steps[0]
                ins.then_inc(vec_steps, 1)

            def after(r, *key):
                vec.wait_ge(vec_steps, r * STEPS + marks[key])

            def staggered(*stages):
                for t in range(STREAMS + len(stages) - 1):
                    for k, stage in reversed(list(enumerate(stages))):
                        if 0 <= t - k < STREAMS:
                            stage(t - k)

            def root(s, kind=0):
                at = 4 * (s // 2) + 2 * kind + s % 2
                return rstd[:, at:at + 1]

            def z_of(r, tag, source, s):
                vec.wait_ge(power_out, count(r, powers, tag, s // 2))
                V.tensor_scalar(z[s][:, :], source[s][:, :], mean_var[:, 2 * s:2 * s + 1], root(s), ALU.subtract, ALU.mult)\
                    .then_inc(z_ready, 1)

            def by_pairs(*stages, last=None):
                for p in range(PAIRS + 1):
                    pair = (2 * p, 2 * p + 1)
                    if p < PAIRS:
                        for s in pair:
                            stages[0](s)
                    if p and last:
                        for s in (2 * p - 2, 2 * p - 1):
                            last(s)
                    if p < PAIRS:
                        for stage in stages[1:]:
                            for s in pair:
                                stage(s)

            def normalise(r, tag, source, job=None, before=(), also=None, finish=None, while_asked=None):
                def stats_of(s):
                    if job:
                        moved(vec, general, r, *job(s))
                    step(("stats", tag, s), V.bn_stats(stats[s][:, :], source[s][:, :]))

                def mean_of(s):
                    after(r, "stats", tag, s)
                    hold(vec)
                    step(("mean", tag, s), V.bn_aggr(mean_var[:, 2 * s:2 * s + 2], stats[s][:, :]))

                def ask(s):
                    if s % 2:
                        after(r, "mean", tag, s)
                        at = 2 * s - 2
                        variances = mean_var[:, at:at + 4].rearrange("p (s k) -> p k s", k=2)[:, 1, :]
                        if also:
                            also(s // 2, variances)
                        V.tensor_scalar(var_eps[:, at:at + 2], variances, EPS, None, ALU.add).then_inc(power_in, 1)

                by_pairs(*before, stats_of, mean_of, ask, *([while_asked] if while_asked else []), last=finish or (lambda s: z_of(r, tag, source, s)))

            def update(r, job, bias=None):
                def stage(s):
                    bank = filled(vec, general, r, job, s)
                    if bias is not None:
                        vec.wait_ge(x_biased, count(r, biased, bias, s))
                    V.tensor_tensor(x[s][:, :], x[s][:, :], bank[:, 0:WIDTH], ALU.add).then_inc(emptied(general, job, s), 1)
                return stage

            def update_and_norm(r, job, bias, tag):
                if tag in tags:
                    normalise(r, tag, x, lambda s: (job, s), [update(r, job, bias)])
                else:
                    by_pairs(update(r, job, bias))

            def soften(r, tag, s, g, n):
                job = (f"{tag} s", s, g)
                slot = score.place[job][0]
                bank = filled(vec, score, r, *job)
                top = peak[:, slot * GROUP:slot * GROUP + n]
                step(("peak", tag, s, g), V.tensor_reduce(top, heads(bank[:, 0:n * P], n), X_AXIS, ALU.max))
                before = same_slot_before(tag, s, g)
                if before:
                    filled(vec, turn, r, *last_turn(*before))
                after(r, "peak", tag, s, g)
                V.tensor_tensor(heads(shifted[:, slot * 1024:slot * 1024 + n * P], n), heads(bank[:, 0:n * P], n),
                                spread(top, P), ALU.subtract).then_inc(emptied(score, *job), 1)

            def divide(r, tag, s, g, a, n, cols, out):
                job = (f"{tag} av", s, g, a)
                slot = general.place[job][0]
                bank = filled(vec, general, r, *job)
                result = heads(bank[:, 0:n * (cols + 1)], n)
                inv = inverse[:, slot * GROUP:slot * GROUP + n]
                step(("inverse", tag, s, g, a), V.reciprocal(inv, result[:, :, cols]))
                after(r, "inverse", tag, s, g, a)
                out(result[:, :, 0:cols], inv).then_inc(emptied(general, *job), 1)

            def divide_narrow(r, tag, s, g, out):
                job = (f"{tag} ao", s, g)
                slot = general.place[job][0]
                bank = filled(vec, general, r, *job)
                result = heads(bank[:, 0:GROUP * SLOT], GROUP)
                inv = inverse[:, slot * GROUP:(slot + 1) * GROUP]
                step(("inverse", tag, s, g), V.reciprocal(inv, result[:, :, HD0]))
                after(r, "inverse", tag, s, g)
                cols = out.shape[3]
                V.tensor_tensor(out, result[:, :, 0:cols].rearrange("p (c h) j -> p c h j", c=2),
                                spread(inv, cols).rearrange("p (c h) j -> p c h j", c=2), ALU.mult).then_inc(emptied(general, *job), 1)

            def attend(r, tag, groups, n, normal, behind=3):
                order = units(groups)
                for t in range(len(order) + behind):
                    if t < len(order):
                        soften(r, tag, *order[t], n)
                    if t >= behind:
                        normal(*order[t - behind])

            def rotate(r, target, turning, cosine, sine, n, width, tmp, slot_free):
                half = width // 2
                V.tensor_tensor(target, turning, repeat(cosine, n), ALU.mult)
                V.tensor_tensor(tmp[:, :, 0:half], turning[:, :, half:width], repeat(sine[:, 0:half], n), ALU.mult)
                V.tensor_tensor(tmp[:, :, half:width], turning[:, :, 0:half], repeat(sine[:, half:width], n), ALU.mult)\
                    .then_inc(slot_free, 1)

            with vec.Fori(0, ROUNDS) as r:
                steps[0] = 0
                for s in range(STREAMS):
                    vec.wait_ge(x_loaded[s], r * 16 + 16)
                normalise(r, "0", x_in)
                vec.wait_ge(masks_loaded, r * 48 + 48)
                V.tensor_reduce(valid[:, :], heads(keep_i[:, :], STREAMS), X_AXIS, ALU.max)
                def divide_small(tag):
                    return lambda s, g: divide_narrow(r, tag, s, g, heads_out[s][:, 0:WIDTH].rearrange(
                        "p (c h j) -> p c h j", c=KB, h=GROUP)[:, :, 4 * g:4 * g + 4, :])

                attend(r, "0", 2, GROUP, divide_small("0"))

                def plus_attention(s):
                    if s == 0:
                        vec.wait_ge(x_free, r + 1)
                    moved(vec, general, r, "0 ao", s, 1)
                    vec.wait_ge(x_biased, count(r, biased, "0", s))
                    step(("half x", s), V.tensor_tensor(x[s][:, :], x_in[s][:, :], heads_out[s][:, 0:WIDTH], ALU.add))

                def plus_ref(s):
                    bank = filled(vec, general, r, "0 ref rows", s)
                    after(r, "half x", s)
                    V.tensor_tensor(x[s][:, :], x[s][:, :], bank[:, 0:WIDTH], ALU.add).then_inc(emptied(general, "0 ref rows", s), 1)

                normalise(r, "0f", x, lambda s: ("0 ref rows", s), [plus_attention, plus_ref])

                if "0f" in tags:
                    for s in range(STREAMS):
                        vec.wait_ge(z_ready, count(r, normalised, "0f", s))
                        step(("x+z", s), V.tensor_tensor(x[s][:, :], x[s][:, :], z[s][:, :], ALU.add))
                    for s in range(STREAMS):
                        bank = filled(vec, general, r, "0f sel", s)
                        ins = V.tensor_tensor(sel[:, s * P:(s + 1) * P], bank[:, 0:P], sel_const[:, 0:P], ALU.subtract)
                        if s == STREAMS - 1:
                            step("diff", ins)
                        ins = V.scalar_tensor_tensor(out=cell(0)[:, s * 8:s * 8 + 8], in0=bank[:, P:P + N_SEL], scalar=-2.0,
                                                     in1=sel_const[:, P:P + N_SEL], op0=ALU.mult, op1=ALU.add)
                        ins.then_inc(emptied(general, "0f sel", s), 1)
                    after(r, "diff")
                    chosen, lora = heads(sel[:, :], STREAMS)[:, :, 0:64], heads(sel[:, :], STREAMS)[:, :, 64:P]
                    step("square", V.tensor_tensor(heads(squares[:, :], STREAMS), chosen, chosen, ALU.mult))
                    all_moved(vec, general, r, [("0f sel", s) for s in range(STREAMS)])
                    vec.wait_ge(z_squared, nth(r, STREAMS - 1))
                    step("length", V.tensor_tensor(of_each(0), of_each(0), spread(square_sum[:, :], N_SEL), ALU.add))
                    after(r, "square")
                    step("content", V.tensor_reduce(cell(1), heads(squares[:, :], STREAMS * N_SEL), X_AXIS, ALU.add))
                    after(r, "length")
                    step("1/length", V.reciprocal(cell(0), cell(0)))
                    after(r, "1/length")
                    step("ratio", V.tensor_tensor(cell(1), cell(1), cell(0), ALU.mult))
                    after(r, "ratio")
                    step("score", V.tensor_tensor(of_each(1), of_each(1), repeat(R["center"], STREAMS), ALU.subtract))
                    after(r, "score")
                    V.tensor_tensor(of_each(2), of_each(1), repeat(R["slope"], STREAMS), ALU.mult).then_inc(gates_in, 1)
                    vec.wait_ge(gates_exp, r + 1)
                    step("1+exp", V.tensor_scalar(cell(3), cell(3), 1.0, None, ALU.add))
                    after(r, "1+exp")
                    step("gate", V.reciprocal(cell(3), cell(3)))
                    after(r, "gate")
                    step("largest", V.tensor_reduce(largest[:, :], of_each(3), X_AXIS, ALU.max))
                    after(r, "largest")
                    step("-gate", V.tensor_scalar(less_gate[:, :], largest[:, :], -1.0, None, ALU.mult))
                    step("are largest", V.tensor_tensor(of_each(4), of_each(3), spread(largest[:, :], N_SEL), ALU.is_ge))
                    after(r, "are largest")
                    step("candidates", V.tensor_tensor(of_each(4), of_each(4), repeat(C["falling"], STREAMS), ALU.mult))
                    after(r, "candidates")
                    step("first", V.tensor_reduce(lone(0), of_each(4), X_AXIS, ALU.max))
                    after(r, "first")
                    step("which", V.tensor_tensor(heads(onehot[:, :], STREAMS)[:, :, 64:72], of_each(4), spread(lone(0), N_SEL), ALU.is_equal))
                    after(r, "which")
                    for s in range(STREAMS):
                        V.tensor_tensor(heads(onehot[:, s * P:s * P + 64], N_SEL), heads(lora[:, s, :], N_SEL),
                                        spread(onehot[:, s * P + 64:s * P + 72], LORA), ALU.mult).then_inc(onehot_ready, 1)

                    after(r, "-gate")
                    def gated(s):
                        bank = filled(vec, general, r, "0f mod", s)
                        after(r, "x+(1-gate)z", s)
                        V.scalar_tensor_tensor(out=x[s][:, :], in0=bank[:, 0:WIDTH], scalar=largest[:, s:s + 1], in1=x[s][:, :],
                                               op0=ALU.mult, op1=ALU.add).then_inc(emptied(general, "0f mod", s), 1)

                    for s in range(STREAMS):
                        after(r, "x+z", s)
                        step(("x+(1-gate)z", s), V.scalar_tensor_tensor(out=x[s][:, :], in0=z[s][:, :], scalar=less_gate[:, s:s + 1],
                                                                        in1=x[s][:, :], op0=ALU.mult, op1=ALU.add))
                    normalise(r, "1", x, lambda s: ("0f mod", s), [gated])

                if "1" in tags:
                    for i, (s, g) in enumerate(units(2)):
                        slot = score.place[("1 q", s, g)][0]
                        bank = filled(vec, score, r, "1 q", s, g)
                        vec.wait_ge(act_read, count(r, act_reads, "1 q", s, g))
                        rope = heads(q_rows[:, slot * 1024:(slot + 1) * 1024], GROUP)[:, :, KVC:P]
                        tmp = heads(q_swap[:, slot * 512:(slot + 1) * 512], GROUP)
                        rotate(r, rope, heads(bank[:, :], GROUP)[:, :, KVC:P], C["cos_q"], C["sin_q"], GROUP, ROPE, tmp,
                               emptied(score, "1 q", s, g))
                        moved(vec, score, r, "1 q", s, g)
                        V.tensor_tensor(rope, rope, tmp, ALU.add).then_inc(q_rotated, 1)

                    def divide1(s, g):
                        for a in range(2):
                            at = g * 1024 + a * 4 * KVC
                            out = heads(big[s][:, at:at + 4 * KVC], 4)
                            divide(r, "1", s, g, a, 4, KVC, lambda result, inv: V.tensor_tensor(out, result, spread(inv, KVC), ALU.mult))

                    attend(r, "1", 2, GROUP, divide1, behind=2)

                    def second_root(p, variances):
                        V.tensor_scalar(var_eps[:, 4 * p + 2:4 * p + 4], variances, 1.0 + EPS, EPS * EPS, ALU.mult, ALU.add)

                    def weighted(s):
                        after(r, "mean", "1f", s)
                        step(("weighted", s), V.scalar_tensor_tensor(out=hrow[s][:, :], in0=x[s][:, :], scalar=mean_var[:, 2 * s:2 * s + 1],
                                                                     in1=R["ln1"], op0=ALU.subtract, op1=ALU.mult))

                    def both_rows(s):
                        vec.wait_ge(power_out, count(r, powers, "1f", s // 2))
                        after(r, "weighted", s)
                        V.tensor_scalar(hrow[s][:, :], hrow[s][:, :], root(s, 1), None, ALU.mult).then_inc(rows_ready, 1)
                        z_of(r, "1f", x, s)

                    normalise(r, "1f", x, lambda s: ("1 out", s), [update(r, "1 out")], second_root, both_rows, weighted)

                if "1f" in tags:
                    for s in range(STREAMS):
                        bank = filled(vec, score, r, "1f rows", s)
                        vec.wait_ge(act_read, count(r, act_reads, "1f rows", s))
                        rope = heads(heads_out[s][:, 0:512], 2 * LF)[:, :, RD:2 * RD]
                        tmp = heads(tA[s][:, :], 2 * LF)
                        rotate(r, rope, heads(bank[:, 2 * P:4 * P], 2 * LF), C["cos_f"], C["sin_f"], 2 * LF, RD, tmp,
                               emptied(score, "1f rows", s))
                        moved(vec, score, r, "1f rows", s)
                        V.tensor_tensor(rope, rope, tmp, ALU.add).then_inc(qk_ready, 1)
                    attend(r, "1f", 2, GROUP, divide_small("1f"))

                    def residual(s):
                        bank = filled(vec, general, r, "1f out", s)
                        V.tensor_tensor(hres[s][:, :], z[s][:, :], bank[:, 0:WIDTH], ALU.add).then_inc(emptied(general, "1f out", s), 1)

                    def ask_h(s):
                        if s % 2:
                            vec.wait_ge(h_squared, nth(r, s))
                            V.tensor_scalar(var_eps[:, 2 * s - 2:2 * s], square_sum[:, s - 1:s + 1], 1.0 / WIDTH, EPS, ALU.mult, ALU.add)\
                                .then_inc(power_in, 1)

                    def h_rows(s):
                        vec.wait_ge(power_out, count(r, powers, "1f h", s // 2))
                        V.scalar_tensor_tensor(out=hrow[s][:, :], in0=hres[s][:, :], scalar=root(s), in1=R["ln2"],
                                               op0=ALU.mult, op1=ALU.mult).then_inc(rows_ready, 1)

                    by_pairs(residual, ask_h, last=h_rows)

                    N = EXPERTS - 1

                    for s in range(STREAMS):
                        bank = filled(vec, general, r, "1f router", s)
                        V.tensor_tensor(cell(0)[:, s * 8:s * 8 + 8], bank[:, 0:8], R["router_b"], ALU.add).then_inc(emptied(general, "1f router", s), 1)
                    vec.wait_ge(router_exp, r + 1)
                    step("1+exp r", V.tensor_scalar(cell(1), cell(1), 1.0, None, ALU.add))
                    after(r, "1+exp r")
                    step("probability", V.reciprocal(cell(1), cell(1)))
                    after(r, "probability")

                    def take(name, source, best, target):
                        step(name + " best", V.tensor_reduce(best, source, X_AXIS, ALU.max))
                        after(r, name + " best")
                        step(name + " are", V.tensor_tensor(of_each(2, N), source, spread(best, N), ALU.is_ge))
                        after(r, name + " are")
                        step(name + " candidates", V.tensor_tensor(of_each(2, N), of_each(2, N), repeat(C["falling"][:, 0:N], STREAMS), ALU.mult))
                        after(r, name + " candidates")
                        step(name + " first", V.tensor_reduce(lone(0), of_each(2, N), X_AXIS, ALU.max))
                        after(r, name + " first")
                        step(name, V.tensor_tensor(target, of_each(2, N), spread(lone(0), N), ALU.is_equal))
                        after(r, name)

                    take("one", of_each(1, N), lone(1), of_each(3, N))
                    step("without one", V.scalar_tensor_tensor(out=of_each(4, N), in0=of_each(3, N), scalar=-2.0, in1=of_each(1, N),
                                                               op0=ALU.mult, op1=ALU.add))
                    after(r, "without one")
                    take("two", of_each(4, N), lone(2), of_each(5, N))
                    step("both", V.tensor_tensor(of_each(5, N), of_each(5, N), of_each(3, N), ALU.add))
                    step("sum", V.tensor_tensor(lone(1), lone(1), lone(2), ALU.add))
                    after(r, "sum")
                    step("1/sum", V.reciprocal(lone(1), lone(1)))
                    after(r, "1/sum")
                    step("scaled", V.tensor_scalar(lone(1), lone(1), 0.5 / EXPERT_SCALE, None, ALU.mult))
                    step("chosen", V.tensor_tensor(of_each(5, N), of_each(5, N), of_each(1, N), ALU.mult))
                    after(r, "chosen")
                    step("expert weights", V.tensor_tensor(heads(expert_w[:, :], STREAMS)[:, :, 1:8], of_each(5, N), spread(lone(1), N), ALU.mult))

                    for s, g in units(2):
                        job = ("1f gu", s, g)
                        slot = score.place[job][0]
                        bank = filled(vec, score, r, *job)
                        vec.wait_ge(tanh_done, count(r, units(2), s, g))
                        gu = bank[:, :].rearrange("p (e u n) -> p e u n", e=4, u=2)
                        th = heads(q_rows[:, slot * 1024:slot * 1024 + 512], 4)
                        ga = heads(q_rows[:, slot * 1024 + 512:slot * 1024 + 1024], 4)
                        step(("silu", s, g), V.scalar_tensor_tensor(out=ga, in0=th, scalar=1.0, in1=gu[:, :, 0, :],
                                                                    op0=ALU.add, op1=ALU.mult))
                        after(r, "expert weights")
                        after(r, "silu", s, g)
                        for e in range(4):
                            ins = V.scalar_tensor_tensor(
                                out=big[s][:, (4 * g + e) * INNER:(4 * g + e + 1) * INNER], in0=ga[:, e, :],
                                scalar=expert_w[:, s * EXPERTS + 4 * g + e:s * EXPERTS + 4 * g + e + 1], in1=gu[:, e, 1, :], op0=ALU.mult, op1=ALU.mult)
                        ins.then_inc(emptied(score, *job), 1)
                    update_and_norm(r, "1f moe", "1f", "2")

                if "2" in tags:
                    def divide2(s, g):
                        def out(result, inv):
                            step(("kept inverse", s), V.tensor_tensor(inv, inv, valid[:, s:s + 1], ALU.mult))
                            after(r, "kept inverse", s)
                            return V.scalar_tensor_tensor(out=x[s][:, :], in0=result[:, 0, :], scalar=inv, in1=x[s][:, :],
                                                          op0=ALU.mult, op1=ALU.add)
                        divide(r, "2", s, g, 0, 1, WIDTH, out)

                    attend(r, "2", 1, 1, divide2, behind=2)
                    if "2f" in tags:
                        normalise(r, "2f", x, lambda s: ("2 av", s, 0, 0))
                if "2f" in tags:
                    update_and_norm(r, "2f out", "2f", "3")

                if "3" in tags:
                    def divide3(s, g):
                        divide_narrow(r, "3", s, g, heads_out[s][:, g * GROUP * HD3:(g + 1) * GROUP * HD3].rearrange(
                            "p (c h j) -> p c h j", c=2, h=HPG))

                    attend(r, "3", 4, GROUP, divide3)
                    update_and_norm(r, "3 out", "3", "3f")

                if "3f" in tags:
                    for s in range(STREAMS):
                        moved(vec, score, r, "3f h", s)
                        V.tensor_tensor(big[s][:, 1024:1024 + FF3], big[s][:, 0:FF3], big[s][:, 0:FF3], ALU.mult).then_inc(relu_squared, 1)
                    by_pairs(update(r, "3f out"))
                assert steps[0] < STEPS, steps[0]
                vec.sem_inc(vec_steps, STEPS - steps[0])

        @block.tensor
        def _(pe):
            T = nc.tensor
            ident = C["ident"]

            pe.wait_ge(ones_ready, 1)
            pe.wait_ge(prep_done, 1)
            for b in range(KB):
                T.matmul(general_psum[0][:, 0:SELW], ones[:, :], sel_prod[:, b * SELW:(b + 1) * SELW], start=(b == 0), stop=(b == KB - 1))
            T.matmul(general_psum[0][:, SELW:SELW + 2], ones[:, :], total, start=True, stop=True).then_inc(prep_filled, 1)
            pe.wait_ge(loaded["const"], 16)
            pe.wait_ge(prep_done, 2)
            for i in range(KB):
                for b in range(KB):
                    ins = T.transpose(turn_psum[0][:, i * WIDTH + b * P:i * WIDTH + b * P + P],
                                      w2f_rows[:, b * WIDTH + i * P:b * WIDTH + i * P + P], ident)
            ins.then_inc(prep_filled, 1)
            pe.wait_ge(loaded["prep"], 16 * len(W1P))
            pe.wait_ge(loaded["w1"], 16)
            for b in range(KB):
                ins = T.matmul(turn_psum[1][:, b * P:b * P + P], W1P["kvcT"][0:KVC, b * P:b * P + P], W1P["kr"][0:KVC, :],
                               start=True, stop=True)
            ins.then_inc(prep_filled, 1)
            for h in range(H1):
                bank = (general_psum[1], score_psum[0])[h // GROUP]
                at = h % GROUP * KVC
                ins = T.matmul(bank[0:QC, at:at + KVC], W1P["uqT"][:, h * QC:(h + 1) * QC], W1P["ukT"][:, h * KVC:(h + 1) * KVC],
                               start=True, stop=True)
            ins.then_inc(prep_filled, 1)
            pe.wait_ge(prep_done, 3)
            for h in range(H1):
                pair, row = h // 2, h % 2 * KVC
                out = score_psum[pair // 4][row:row + KVC, pair % 4 * WIDTH:(pair % 4 + 1) * WIDTH]
                ins = T.matmul(out, W1P["uvT"][:, h * KVC:(h + 1) * KVC], W1P[f"o{h // GROUP}"][:, h % GROUP * WIDTH:(h % GROUP + 1) * WIDTH],
                               start=True, stop=True)
            ins.then_inc(prep_filled, 1)
            pe.wait_ge(loaded["w0"], 16)
            pe.wait_ge(loaded["constb"], 16)

            def turn_rows(bank, source, n=KB):
                for b in range(n):
                    ins = T.transpose(bank[:, b * P:b * P + P], source[:, b * P:b * P + P], ident)
                return ins

            def blocks_out(bank, w, cols, actT, n=KB):
                for m in range(n):
                    for b in range(KB):
                        ins = T.matmul(bank[:, m * P:m * P + P], w[:, b * cols + m * P:b * cols + m * P + P], actT[:, b * P:b * P + P],
                                       start=(b == 0), stop=(b == KB - 1))
                return ins

            def rows_out(out, actT, w, cols, n=KB, at=0):
                wide = out.shape[1]
                for b in range(n):
                    ins = T.matmul(out, actT[:, b * P:b * P + P], w[:, b * cols + at:b * cols + at + wide], start=(b == 0), stop=(b == n - 1))
                return ins

            def job(ring, r, *key):
                return free(pe, ring, r, *key)

            def done(ins, ring, *key):
                ins.then_inc(fill(ring, *key), 1)

            def stay_warm(bank, n):
                for _ in range(n):
                    T.matmul(bank[:, 0:2 * P], ident_b, constb[:, :], start=True, stop=True)

            def turn_z(r, name, tag, streams=range(STREAMS), warm=WARM_Z):
                for s in streams:
                    bank = job(general, r, name, s)
                    stay_warm(bank, warm[s])
                    pe.wait_ge(z_ready, count(r, normalised, tag, s))
                    done(turn_rows(bank, z[s]), general, name, s)

            def masked(bank, mask, n, last=False):
                return T.matmul(bank, ident_b, repeat(mask[:, :], n), start=True, stop=last)

            def scores_and_turns(r, tag, t, order, per, turns, scores):
                if t < len(order):
                    s, g = order[t]
                    bank = job(score, r, f"{tag} s", s, g)
                    done(scores(s, g, bank), score, f"{tag} s", s, g)
                if 1 <= t <= len(order):
                    s, g = order[t - 1]
                    slot = score.place[(f"{tag} s", s, g)][0]
                    for a in range(turns):
                        bank = job(turn, r, f"{tag} t", s, g, a)
                        if a == 0:
                            if t == 1:
                                stay_warm(bank, WARM_T)
                            moved(pe, score, r, f"{tag} s", s, g)
                        done(turn_rows(bank, shifted[:, slot * 1024 + a * 512:slot * 1024 + a * 512 + per * P], per),
                             turn, f"{tag} t", s, g, a)

            def attend(r, tag, groups, n, scores, value, wide, turns=2):
                order = units(groups)
                per = n // turns
                for t in range(len(order) + 2):
                    scores_and_turns(r, tag, t, order, per, turns, scores)
                    if t >= 2:
                        s, g = order[t - 2]
                        for a in range(turns):
                            key = (f"{tag} av", s, g, a)
                            bank = job(general, r, *key)
                            moved(pe, turn, r, f"{tag} t", s, g, a)
                            at = (prob_jobs.index((tag, s, g, a)) % 4) * 512
                            for i in range(per):
                                ins = T.matmul(bank[:, i * wide:(i + 1) * wide], probs[:, at + i * P:at + i * P + P], value(s),
                                               start=True, stop=True)
                            done(ins, general, *key)

            def attend_narrow(r, tag, groups, scores, place):
                order = units(groups)
                for t in range(len(order) + 3):
                    scores_and_turns(r, tag, t, order, 4, 2, scores)
                    if 2 <= t < len(order) + 2:
                        s, g = order[t - 2]
                        bank = job(general, r, f"{tag} av", s, g)
                        for a in range(2):
                            moved(pe, turn, r, f"{tag} t", s, g, a)
                            at = (prob_jobs.index((tag, s, g, a)) % 4) * 512
                            for i in range(4):
                                v, block, row = place(g, a * 4 + i)
                                ins = T.matmul(bank[SLOT * row:SLOT * (row + 1), block * P:(block + 1) * P],
                                               values[s][:, v * SLOT:(v + 1) * SLOT], probs[:, at + i * P:at + i * P + P],
                                               start=True, stop=True)
                        done(ins, general, f"{tag} av", s, g)
                    if t >= 3:
                        s, g = order[t - 3]
                        bank = job(general, r, f"{tag} ao", s, g)
                        moved(pe, general, r, f"{tag} av", s, g)
                        at = (t - 3) % 2 * GROUP * SLOT
                        done(turn_rows(bank, narrow_out[:, at:at + GROUP * SLOT]), general, f"{tag} ao", s, g)

            def keys3_in(r, streams):
                for s in streams:
                    done(blocks_out(job(general, r, "3 k", s), W3["k"], WIDTH, cxT[s]), general, "3 k", s)

            with pe.Fori(0, ROUNDS) as r:
                for s in range(STREAMS):
                    pe.wait_ge(cxT_loaded[s], r * 16 + 16)
                    done(blocks_out(job(general, r, "0 sup", s), W0["fc"], WIDTH, cxT[s]), general, "0 sup", s)
                for s in range(STREAMS):
                    bank = job(general, r, "0 k", s)
                    moved(pe, general, r, "0 sup", s)
                    done(blocks_out(bank, W0["k"], WIDTH, tB[s]), general, "0 k", s)
                for s in range(STREAMS):
                    done(rows_out(job(general, r, "0 v", s)[:, 0:WIDTH], tB[s], W0["v"], WIDTH), general, "0 v", s)
                turn_z(r, "0 zT", "0", warm=(0, 0, 0, 0))
                for s in range(STREAMS):
                    bank = job(general, r, "0 ref", s)
                    moved(pe, general, r, "0 zT", s)
                    done(blocks_out(bank, W0["fc"], WIDTH, zT[s]), general, "0 ref", s)
                for s in range(STREAMS):
                    bank = job(general, r, "0 q", s)
                    moved(pe, general, r, "0 ref", s)
                    done(blocks_out(bank, W0["q"], WIDTH, tA[s]), general, "0 q", s)

                def small_scores(tag, queries, mask=None):
                    def scores(s, g, bank):
                        if g == 0:
                            if tag == "0":
                                moved(pe, general, r, "0 k", s)
                                moved(pe, general, r, "0 q", s)
                                moved(pe, general, r, "0 v", s)
                            else:
                                moved(pe, turn, r, "1f qk", s)
                        keys = big[s][:, 0:4 * P].rearrange("p (b e k) -> p b (e k)", b=KB, e=2)
                        for q in range(2):
                            row = 32 * (2 * g + q)
                            if mask is not None:
                                masked(bank[:, q * 512:(q + 1) * 512], mask, 4)
                            for b in range(KB):
                                at = q * 512 + b * 256
                                ins = T.matmul(bank[:, at:at + 256], queries[s][row:row + 32, b * P:b * P + P], keys[row:row + 32, b, :],
                                               start=(mask is None), stop=(mask is None or b == KB - 1))
                        return ins
                    return scores

                def small_place(g, i):
                    return small_head(g, i), i % 4 // 2, i // 4 * 2 + i % 2

                attend_narrow(r, "0", 2, small_scores("0", zT), small_place)
                for s in range(STREAMS):
                    done(turn_rows(job(general, r, "0 ref rows", s), tA[s]), general, "0 ref rows", s)

                if "0f" in tags:
                    for pair in BOTH:
                        turn_z(r, "0f zT", "0f", pair)
                        for s in pair:
                            bank = job(general, r, "0f sel", s)
                            moved(pe, general, r, "0f zT", s)
                            done(rows_out(bank[:, 0:SELW], zT[s], W0F["sel"], SELW), general, "0f sel", s)
                    if "1" in tags:
                        for s in range(STREAMS):
                            bank = job(general, r, "1 k", s)
                            blocks_out(bank, w_kv, P, cxT[s], 1)
                            for b in range(KB):
                                ins = T.matmul(bank[KVC:P, P:2 * P], w_kv_swap[:, b * ROPE:(b + 1) * ROPE], cxT[s][:, b * P:b * P + P],
                                               start=(b == 0), stop=(b == KB - 1))
                            done(ins, general, "1 k", s)
                        for s in range(STREAMS):
                            done(rows_out(job(general, r, "1 kv", s)[:, 0:KVC], cxT[s], W1["kvc"], KVC), general, "1 kv", s)
                    for s in range(STREAMS):
                        bank = job(turn, r, "0f onehot", s)
                        if s == 0:
                            stay_warm(bank, WARM_O)
                        pe.wait_ge(onehot_ready, nth(r, s))
                        done(turn_rows(bank, onehot[:, s * P:(s + 1) * P], 1), turn, "0f onehot", s)
                    for s in range(STREAMS):
                        bank = job(general, r, "0f mod", s)
                        moved(pe, turn, r, "0f onehot", s)
                        done(T.matmul(bank[:, 0:WIDTH], onehotT[s][:, :], W0F["lift"], start=True, stop=True), general, "0f mod", s)

                if "1" in tags:
                    for pair in BOTH:
                        turn_z(r, "1 zT", "1", pair)
                        for s in pair:
                            bank = job(general, r, "1 qc", s)
                            moved(pe, general, r, "1 zT", s)
                            for b in range(KB):
                                ins = T.matmul(bank[0:QC, 0:P], W1["dq"][:, b * QC:(b + 1) * QC], zT[s][:, b * P:b * P + P],
                                               start=(b == 0), stop=(b == KB - 1))
                            done(ins, general, "1 qc", s)
                    order = units(2)
                    for t in range(len(order) + 1):
                        if t < len(order):
                            s, g = order[t]
                            bank = job(score, r, "1 q", s, g)
                            moved(pe, general, r, "1 qc", s)
                            for q in range(2):
                                at = g * 1024 + q * 512
                                ins = T.matmul(bank[:, q * 512:(q + 1) * 512], qcT[s][0:QC, :], w_query[0:QC, at:at + 512], start=True, stop=True)
                            done(ins, score, "1 q", s, g)
                        if t >= 1:
                            s, g = order[t - 1]
                            slot = score.place[("1 q", s, g)][0]
                            for a in range(2):
                                bank = job(turn, r, "1 q", s, g, a)
                                pe.wait_ge(q_rotated, r * len(order) + t)
                                done(turn_rows(bank, q_rows[:, slot * 1024 + a * 512:slot * 1024 + (a + 1) * 512], 4), turn, "1 q", s, g, a)

                    def scores1(s, g, bank):
                        if g == 0:
                            moved(pe, turn, r, "1 q", s, 1, 1)
                            pe.wait_ge(keys_ready, nth(r, s))
                            pe.wait_ge(masks_ready, r + 1)
                        for q in range(2):
                            masked(bank[:, q * 512:(q + 1) * 512], mask1[s], 4)
                            for i in range(4):
                                at = (q * 4 + i) * P
                                h = g * GROUP + q * 4 + i
                                ins = T.matmul(bank[:, at:at + P], big[s][:, h * P:h * P + P], kcT[s][:, :], start=False, stop=(i == 3))
                        return ins

                    attend(r, "1", 2, GROUP, scores1, lambda s: values1[s][:, 0:KVC + 1], KVC + 1)
                    for s in range(STREAMS):
                        for a in range(2):
                            bank = job(turn, r, "1 o", s, a)
                            for i in range(2):
                                moved(pe, general, r, "1 av", s, a, i)
                            done(turn_rows(bank, big[s][:, a * 1024:a * 1024 + 512], 4), turn, "1 o", s, a)
                    for s in range(STREAMS):
                        bank = job(general, r, "1 out", s)
                        for a in range(2):
                            moved(pe, turn, r, "1 o", s, a)
                        for pair in range(H1 // 2):
                            at = pair // 4 * 1024 + 512 + pair % 4 * P
                            ins = T.matmul(bank[:, 0:WIDTH], big[s][:, at:at + P], w_out[:, pair * WIDTH:(pair + 1) * WIDTH],
                                           start=(pair == 0), stop=(pair == H1 // 2 - 1))
                        done(ins, general, "1 out", s)

                if "1f" in tags:
                    pe.wait_ge(loaded["w1f"], 16)
                    for pair in BOTH:
                        for s in pair:
                            bank = job(general, r, "1f zT", s)
                            stay_warm(bank, WARM_R[s])
                            pe.wait_ge(rows_ready, count(r, weighted_rows, "1f z", s))
                            done(turn_rows(bank, hrow[s]), general, "1f zT", s)
                        for s in pair:
                            bank = job(general, r, "1f kq", s)
                            moved(pe, general, r, "1f zT", s)
                            done(blocks_out(bank, W1F["down_kq"], P, zT[s], 1), general, "1f kq", s)
                        for s in pair:
                            bank = job(score, r, "1f rows", s)
                            moved(pe, general, r, "1f kq", s)
                            T.matmul(bank[:, 0:3 * P], qcT[s][:, :], W1F["up"][:, 0:3 * P], start=True, stop=True)
                            rows_out(bank[:, 3 * P:4 * P], zT[s], W1F["rope_k"], P)
                            done(T.matmul(bank[:, 512:512 + WIDTH], qcT[s][:, :], W1F["up"][:, 3 * P:3 * P + WIDTH], start=True, stop=True),
                                 score, "1f rows", s)
                    for s in range(STREAMS):
                        bank = job(turn, r, "1f qk", s)
                        if s == 0:
                            stay_warm(bank, WARM_Q)
                        pe.wait_ge(qk_ready, nth(r, s))
                        done(turn_rows(bank, heads_out[s][:, 0:512], 4), turn, "1f qk", s)
                    causal = causal_b
                    attend_narrow(r, "1f", 2, small_scores("1f", tB, causal), small_place)
                    for s in range(STREAMS):
                        bank = job(turn, r, "1f o", s)
                        moved(pe, general, r, "1f ao", s, 1)
                        done(turn_rows(bank, heads_out[s]), turn, "1f o", s)
                    for s in range(STREAMS):
                        bank = job(general, r, "1f out", s)
                        moved(pe, turn, r, "1f o", s)
                        done(rows_out(bank[:, 0:WIDTH], headsT[s], W1F["o"], WIDTH), general, "1f out", s)
                    for s in range(STREAMS):
                        bank = job(turn, r, "1f h", s)
                        pe.wait_ge(rows_ready, count(r, weighted_rows, "1f h", s))
                        done(turn_rows(bank, hrow[s]), turn, "1f h", s)
                    for s in range(STREAMS):
                        bank = job(general, r, "1f router", s)
                        moved(pe, turn, r, "1f h", s)
                        done(rows_out(bank[:, 0:EXPERTS], zT[s], W1F["router"], EXPERTS), general, "1f router", s)
                    pe.wait_ge(loaded["wm"], 16)
                    order = units(2)
                    for t in range(len(order) + 2):
                        if t < len(order):
                            s, g = order[t]
                            bank = job(score, r, "1f gu", s, g)
                            for q in range(2):
                                ins = rows_out(bank[:, q * 512:(q + 1) * 512], zT[s], WM["gate_up"], EXPERTS * 2 * INNER,
                                               at=g * 1024 + q * 512)
                            done(ins, score, "1f gu", s, g)
                        if 1 <= t <= len(order):
                            s, g = order[t - 1]
                            bank = job(turn, r, "1f m", s, g)
                            moved(pe, score, r, "1f gu", s, g)
                            done(turn_rows(bank, big[s][:, g * 512:(g + 1) * 512], 4), turn, "1f m", s, g)
                        if t >= 2:
                            s, g = order[t - 2]
                            if g == 1:
                                if s == STREAMS - 1 and "3" in tags:
                                    pe.wait_ge(loaded["w3"], 16)
                                    for i in range(STREAMS):
                                        done(rows_out(job(general, r, "3 v", i)[:, 0:G3 * HD3], cxT[i], W3["v"], G3 * HD3), general, "3 v", i)
                                bank = job(general, r, "1f moe", s)
                                for half in range(2):
                                    moved(pe, turn, r, "1f m", s, half)
                                done(rows_out(bank[:, 0:WIDTH], big[s][:, 1024:2048], WM["down"], WIDTH, EXPERTS), general, "1f moe", s)

                if "2" in tags:
                    turn_z(r, "2 zT", "2")

                    def scores2(s, g, bank):
                        moved(pe, general, r, "2 zT", s)
                        pe.wait_ge(cx_loaded[s], r * 16 + 16)
                        masked(bank[:, 0:P], mask2[s], 1)
                        for b in range(KB):
                            ins = T.matmul(bank[:, 0:P], zT[s][:, b * P:b * P + P], cxT[s][:, b * P:b * P + P], start=False, stop=(b == KB - 1))
                        return ins

                    attend(r, "2", 1, 1, scores2, lambda s: cx[s][:, 0:WIDTH + 1], WIDTH + 1, turns=1)
                    if "3" in tags:
                        keys3_in(r, (0, 1))
                if "2f" in tags:
                    for pair in BOTH:
                        turn_z(r, "2f zT", "2f", pair)
                        for s in pair:
                            bank = job(general, r, "2f out", s)
                            moved(pe, general, r, "2f zT", s)
                            done(rows_out(bank[:, 0:WIDTH], zT[s], w2f, WIDTH), general, "2f out", s)
                    if "3" in tags:
                        keys3_in(r, (2, 3))

                if "3" in tags:
                    for pair in BOTH:
                        turn_z(r, "3 zT", "3", pair)
                        for s in pair:
                            bank = job(general, r, "3 q", s)
                            moved(pe, general, r, "3 zT", s)
                            done(blocks_out(bank, W3["q"], WIDTH, zT[s]), general, "3 q", s)

                    def scores3(s, g, bank):
                        if g == 0:
                            all_moved(pe, general, r, [("3 k", s), ("3 v", s), ("3 q", s)])
                        for q in range(2):
                            b, row = (2 * g + q) // 4, 32 * ((2 * g + q) % 4)
                            masked(bank[:, q * 512:(q + 1) * 512], mask3[s], 4)
                            ins = T.matmul(bank[:, q * 512:(q + 1) * 512], zT[s][row:row + 32, b * P:b * P + P],
                                           big[s][row:row + 32, b * 512:(b + 1) * 512], start=False, stop=True)
                        return ins

                    attend_narrow(r, "3", 4, scores3, lambda g, i: (2 * g + i // HPG, i // HPG, i % HPG))
                    for s in range(STREAMS):
                        bank = job(turn, r, "3 o", s)
                        all_moved(pe, general, r, [("3 ao", s, g) for g in range(4)])
                        done(turn_rows(bank, heads_out[s]), turn, "3 o", s)
                    for s in range(STREAMS):
                        bank = job(general, r, "3 out", s)
                        moved(pe, turn, r, "3 o", s)
                        done(rows_out(bank[:, 0:WIDTH], headsT[s], W3["o"], WIDTH), general, "3 out", s)

                if "3f" in tags:
                    for pair in BOTH:
                        turn_z(r, "3f zT", "3f", pair)
                        for s in pair:
                            bank = job(score, r, "3f h", s)
                            moved(pe, general, r, "3f zT", s)
                            done(blocks_out(bank, W3F["fc"], FF3, zT[s], FB3), score, "3f h", s)
                    for s in range(STREAMS):
                        bank = job(general, r, "3f out", s)
                        pe.wait_ge(relu_squared, nth(r, s))
                        done(rows_out(bank[:, 0:WIDTH], big[s][:, 1024:1024 + FF3], W3F["proj"], WIDTH, FB3), general, "3f out", s)


INPUT_SHAPES = [("x", (SEQUENCES, P, WIDTH), F32), ("ctx", (SEQUENCES, P, WIDTH), F32), ("ctxT", (SEQUENCES, P, WIDTH), F32),
                ("seg", (ROUNDS, P, STREAMS), I32), ("keep", (ROUNDS, STREAMS * P), U8), ("pad", (ROUNDS, STREAMS * P), I32),
                ("const", (P, width(CONST_NAMES)), F32), ("constb", (P, 2 * P), BF16), ("rows", (width(ROW_NAMES),), F32),
                ("w0", (P, width(W0_NAMES)), F32), ("w0f", (P, width(W0F_NAMES)), F32), ("w1", (P, width(W1_NAMES)), F32),
                ("w1p", (P, width(W1P_NAMES)), F32), ("w1f", (P, width(W1F_NAMES)), F32), ("wm", (P, width(WM_NAMES)), F32),
                ("w2f", (P, KB * WIDTH), F32), ("w3", (P, width(W3_NAMES)), F32), ("w3f", (P, width(W3F_NAMES)), F32)]


def by_block(w):
    n = w.shape[1]
    return w.reshape(-1, P, n).transpose(1, 0, 2).reshape(P, -1)


def pad_rows(w, at=0):
    out = np.zeros((P, w.shape[1]), w.dtype)
    out[at:at + w.shape[0]] = w
    return out


def constants():
    part = np.arange(P)
    t = np.arange(P, dtype=np.float32)

    def angles(half):
        inv = (1.0 / np.float32(10000.0) ** (np.arange(half, dtype=np.float32) / np.float32(half))).astype(np.float32)
        return (t[:, None] * inv).astype(np.float32)
    a, f = angles(ROPE // 2), angles(RD // 2)
    cos_q = np.concatenate([np.cos(a), np.cos(a)], 1)
    sin_q = np.concatenate([-np.sin(a), np.sin(a)], 1)
    parts = {
        "ident": np.eye(P), "even": (part // HD0 % 2 == 0)[:, None], "odd": (part // HD0 % 2 == 1)[:, None],
        "quarter": part[:, None] // HD3 % HPG == np.arange(HPG)[None, :], "key": np.tile(t, (P, 1)),
        "falling": np.tile(np.arange(EXPERTS, 0, -1), (P, 1)), "cos_q": cos_q, "sin_q": sin_q,
        "cos_kT": pad_rows(cos_q.T, KVC), "sin_kT": pad_rows(sin_q.T, KVC),
        "cos_f": np.concatenate([np.cos(f), np.cos(f)], 1), "sin_f": np.concatenate([-np.sin(f), np.sin(f)], 1)}
    return np.concatenate([np.asarray(parts[n], np.float32) for n, _ in CONST_NAMES], 1)


def kernel(**inputs):
    import concourse.bacc as bacc
    import ml_dtypes
    from concourse.bass_utils import run_bass_kernel_spmd

    I = {k: np.asarray(v) for k, v in inputs.items()}

    def pack(names, parts):
        for n, cols in names:
            assert parts[n].shape == (P, cols), (n, parts[n].shape, cols)
        return np.ascontiguousarray(np.concatenate([parts[n] for n, _ in names], 1))

    def of(prefix):
        return {k[len(prefix):]: v for k, v in I.items() if k.startswith(prefix)}
    x0, f0, x1, f1 = of("L0_xattn_"), of("L0_ffn_"), of("L1_xattn_"), of("L1_ffn_")
    x3, f3 = of("L3_xattn_"), of("L3_ffn_")

    def features_first(w):
        return w.transpose(1, 0, 2).reshape(w.shape[1], -1)

    def swapped(w):
        half = w.shape[1] // 2
        return np.concatenate([w[:, half:], w[:, :half]], 1)

    causal = np.where(np.tril(np.ones((P, P), bool)), 0.0, MASKED)
    tail = np.zeros((WIDTH, 1), np.float32)
    gate_up = np.stack([np.concatenate([f1["sh_gate"][None], f1["r_gate"]]),
                        np.concatenate([f1["sh_up"][None], f1["r_up"]])], 1)
    k_repeated = np.repeat(x3["w_k"].reshape(G3, 1, HD3, WIDTH), HPG, 1).reshape(WIDTH, WIDTH)
    none = np.zeros((LATENT, P), np.float32)
    up = np.concatenate([np.concatenate([none, f1["k_u_w"], none, f1["v_u_w"]], 1),
                         np.concatenate([f1["q_u_w"], none, f1["rope_q_w"], none, none], 1)], 0)
    arrays = {
        "x": I["x"], "ctx": I["ctx_2048"],
        "ctxT": I["ctx_2048"].transpose(0, 2, 1).reshape(SEQUENCES, KB, P, P).transpose(0, 2, 1, 3).reshape(SEQUENCES, P, WIDTH),
        "seg": I["itok_BxS_0_1023"].reshape(ROUNDS, STREAMS, P).transpose(0, 2, 1),
        "keep": I["mask_BxS2_bk0"].reshape(ROUNDS, STREAMS * P),
        "pad": I["mask_BxS2_if1"].reshape(ROUNDS, STREAMS * P),
        "const": constants(), "constb": np.concatenate([np.eye(P), causal], 1).astype(ml_dtypes.bfloat16),
        "rows": np.concatenate([x0["b_v"], f1["ln1_w"], f1["ln2_w"], I["L2_ffn_bias"], x3["b_o"], f1["router_b"],
                                np.zeros(1, np.float32), f0["imp_center"], f0["imp_slope"]]),
        "w0": pack(W0_NAMES, {"fc": by_block(x0["W_fc"].T), "q": by_block(x0["W_q"].T), "k": by_block(x0["W_k"].T),
                              "v": by_block(x0["W_v"].reshape(WIDTH, WIDTH).T), "b_fc": x0["b_fc"].reshape(KB, P).T,
                              "b_q": x0["b_q"].reshape(KB, P).T, "b_k": x0["b_k"].reshape(KB, P).T}),
        "w0f": pack(W0F_NAMES, {
            "sel": by_block(np.concatenate([features_first(f0["select_weight"]), features_first(f0["lora_update"]),
                                            f0["select_mean_diff"].T], 1)),
            "debias": by_block(f0["debias_w"].T),
            "lift": pad_rows(np.concatenate([f0["lora_degen"].transpose(0, 2, 1).reshape(-1, WIDTH), f0["bias_w"]]))}),
        "w1": pack(W1_NAMES, {"kvc": by_block(x1["W_kvc"]), "dq": by_block(x1["W_dq"])}),
        "w1p": pack(W1P_NAMES, {"uqT": x1["W_uq"].reshape(QC, H1, P).transpose(2, 1, 0).reshape(P, -1),
                                "ukT": x1["W_uk"].reshape(KVC, H1, P).transpose(2, 1, 0).reshape(P, -1),
                                "uvT": x1["W_uv"].reshape(KVC, H1, P).transpose(2, 1, 0).reshape(P, -1),
                                "o": by_block(x1["W_o"]), "kvcT": pad_rows(x1["W_kvc"].T), "qr": pad_rows(x1["W_qr"]),
                                "kr": pad_rows(np.concatenate([x1["W_kr"], swapped(x1["W_kr"])], 1))}),
        "w1f": pack(W1F_NAMES, {"down_kq": by_block(np.concatenate([f1["kv_d_w"], f1["q_d_w"]], 1)), "up": up,
                                "rope_k": by_block(f1["rope_k_w"]), "o": by_block(f1["o_w"]),
                                "router": by_block(np.concatenate([f1["router_w"], tail], 1))}),
        "wm": pack(WM_NAMES, {"gate_up": by_block(gate_up.transpose(2, 0, 1, 3).reshape(WIDTH, -1)),
                              "down": by_block(np.concatenate([f1["sh_down"][None], f1["r_down"]]).reshape(-1, WIDTH))}),
        "w2f": by_block(I["L2_ffn_weight"]),
        "w3": pack(W3_NAMES, {"q": by_block(x3["w_q"].T), "k": by_block(k_repeated.T), "v": by_block(x3["w_v"].T),
                              "o": by_block(x3["w_o"].T)}),
        "w3f": pack(W3F_NAMES, {"fc": by_block(f3["w_fc"].T), "proj": by_block(f3["w_proj"].T)}),
    }
    nc = bacc.Bacc("TRN2", target_bir_lowering=False, num_devices=1)
    A = {n: nc.dram_tensor(f"in_{n}", shape, dt, kind="ExternalInput").ap() for n, shape, dt in INPUT_SHAPES}
    A["out"] = nc.dram_tensor("out", (SEQUENCES, P, WIDTH), F32, kind="ExternalOutput").ap()
    program(nc, A)
    data = {f"in_{n}": np.ascontiguousarray(arrays[n]) for n, _, _ in INPUT_SHAPES}
    for n, shape, _ in INPUT_SHAPES:
        assert data[f"in_{n}"].shape == shape, (n, data[f"in_{n}"].shape)
    return run_bass_kernel_spmd(nc, [data], core_ids=[0]).results[0]["out"]
```

```python
from contextlib import ExitStack

import numpy as np

import concourse.bass as bass
from concourse import mybir

F32 = mybir.dt.float32
BF16 = mybir.dt.bfloat16
I32 = mybir.dt.int32
U8 = mybir.dt.uint8
ALU = mybir.AluOpType
ACT = mybir.ActivationFunctionType
X_AXIS = mybir.AxisListType.X

P = 128
SEQUENCES, TOKENS, WIDTH = 16, 128, 256
KB = WIDTH // P
STREAMS = 4
ROUNDS = SEQUENCES // STREAMS
PAIRS = STREAMS // 2
BOTH = [(2 * p, 2 * p + 1) for p in range(PAIRS)]
KEYS_BY_SCALAR, KEYS_BY_VECTOR = (0, 2), (1, 3)
EPS = 1e-5
MASKED = -1e30
WARM_Z, WARM_T, WARM_O, WARM_R = (4, 2, 2, 2), {"0": 14, "1": 6, "1f": 6, "2": 6, "3": 6}, 10, (0, 0, 4, 0)
STEPS = 1024

H0, HD0 = 16, 16
N_SEL, SEL, LORA = 8, 8, 8
H1, HD1, KVC, QC, ROPE = 16, 128, 64, 96, 64
LOOKBACK = 8
LF, RD, LATENT = 16, 8, 64
EXPERTS, INNER, EXPERT_SCALE = 8, 128, 8.0
H3, HD3, G3 = 32, 8, 8
HPG = H3 // G3
FF3 = 640
FB3 = FF3 // P
SLOT = 32
GROUP = 8

ROW_NAMES = [("b_v", WIDTH), ("ln1", WIDTH), ("ln2", WIDTH), ("bias2", WIDTH), ("b_o", WIDTH),
             ("router_b", EXPERTS), ("center", N_SEL), ("slope", N_SEL)]
CONST_NAMES = [("ident", P), ("even", 1), ("odd", 1), ("quarter", HPG), ("key", P), ("falling", EXPERTS),
               ("cos_q", ROPE), ("sin_q", ROPE), ("cos_kT", P), ("sin_kT", P), ("cos_f", RD), ("sin_f", RD)]
W0_NAMES = [("fc", KB * WIDTH), ("q", KB * WIDTH), ("k", KB * WIDTH), ("v", KB * WIDTH),
            ("b_fc", KB), ("b_q", KB), ("b_k", KB)]
SELW = N_SEL * SEL + N_SEL * LORA + N_SEL
W0F_NAMES = [("sel", KB * SELW), ("debias", KB * N_SEL), ("lift", WIDTH)]
W1_NAMES = [("kvc", KB * KVC), ("dq", KB * QC)]
W1P_NAMES = [("uqT", H1 * QC), ("ukT", H1 * KVC), ("uvT", H1 * KVC), ("o", H1 * WIDTH),
             ("kvcT", KB * P), ("qr", H1 * ROPE), ("kr", 2 * ROPE)]
W1F_NAMES = [("down_kq", KB * P), ("up", 3 * P + WIDTH), ("rope_k", KB * P), ("o", KB * WIDTH),
             ("router", KB * EXPERTS)]
WM_NAMES = [("gate_up", KB * EXPERTS * 2 * INNER), ("down", EXPERTS * WIDTH)]
W3_NAMES = [("q", KB * WIDTH), ("k", KB * WIDTH), ("v", KB * G3 * HD3), ("o", KB * WIDTH)]
W3F_NAMES = [("fc", KB * FF3), ("proj", FB3 * WIDTH)]


def width(names):
    return sum(n for _, n in names)


def columns(tile, names):
    out, at = {}, 0
    for name, n in names:
        out[name] = tile[:, at:at + n]
        at += n
    return out


def blocks(ap, n):
    return ap.rearrange("p (b n) -> p b n", b=n)


class Ring:

    def __init__(self, jobs, slots):
        self.place, self.uses = {}, [0] * slots
        for n, job in enumerate(jobs):
            assert job not in self.place, job
            self.uses[n % slots] += 1
            self.place[job] = (n % slots, self.uses[n % slots])


def each(*names):
    return [(name, s) for name in names for s in range(STREAMS)]


def pairwise(*names):
    return [(name, s) for pair in BOTH for name in names for s in pair]


def units(groups):
    return [(s, g) for s in range(STREAMS) for g in range(groups)]


TAGS = ["0", "0f", "1", "1f", "2", "2f", "3", "3f"]


def program(nc, A):
    BETWEEN = {"1": {7: [("1 out", 0)], 8: [("1 out", 1)]}, "1f": {8: [("1f out", 0)], 9: [("1f out", 1)]},
               "3": {12: [("3 out", 0)], 13: [("3 out", 1)]}}
    TURNED_BETWEEN = {"1": {6: [("1 o", s, a) for s in BOTH[0] for a in range(2)]}, "1f": {7: [("1f o", s) for s in BOTH[0]]},
                      "3": {11: [("3 o", s) for s in BOTH[0]]}}

    def attn(layer, groups, per=1):
        order = units(groups)
        return [job for t in range(2, len(order) + 2)
                for job in [(f"{layer} av",) + order[t - 2] + (a,) for a in range(per)] + BETWEEN.get(layer, {}).get(t, [])]

    def narrow_attn(layer, groups):
        order = units(groups)
        return [job for t in range(2, len(order) + 3)
                for job in ([(f"{layer} av",) + order[t - 2]] if t < len(order) + 2 else [])
                + ([(f"{layer} ao",) + order[t - 3]] if t >= 3 else []) + BETWEEN.get(layer, {}).get(t, [])]

    def turns_of(layer, groups):
        order = units(groups)
        return [job for t in range(1, len(order) + 1)
                for job in [(f"{layer} t",) + order[t - 1] + (a,) for a in range(2)] + TURNED_BETWEEN.get(layer, {}).get(t, [])]

    def later(name):
        return [(name, s) for s in BOTH[1]]

    moe_jobs = each("1f moe")[:-1] + each("3 v") + each("1f moe")[-1:]
    keys3 = each("3 k")

    general_jobs = (
        each("0 sup", "0 k", "0 v", "0 zT", "0 ref", "0 q", "0 ref rows") + narrow_attn("0", 2)
        + pairwise("0f zT", "0f sel") + each("1 k", "1 kv", "0f mod")
        + pairwise("1 zT", "1 qc") + attn("1", 2, 2) + later("1 out")
        + pairwise("1f zT", "1f kq") + narrow_attn("1f", 2) + later("1f out") + each("1f router") + moe_jobs
        + each("2 zT") + attn("2", 1) + keys3[:2] + pairwise("2f zT", "2f out") + keys3[2:]
        + pairwise("3 zT", "3 q") + narrow_attn("3", 4) + later("3 out")
        + each("3f zT", "3f out"))
    score_jobs = (
        [("0 s",) + u for u in units(2)] + [("1 q",) + u for u in units(2)] + [("1 s",) + u for u in units(2)]
        + each("1f rows") + [("1f s",) + u for u in units(2)] + [("1f gu",) + u for u in units(2)]
        + [("2 s",) + u for u in units(1)] + [("3 s",) + u for u in units(4)] + each("3f h"))
    turn_jobs = (
        turns_of("0", 2) + each("0f onehot")
        + [("1 q",) + u + (a,) for u in units(2) for a in range(2)]
        + turns_of("1", 2) + [("1 o", s, a) for s in BOTH[1] for a in range(2)]
        + each("1f qk") + turns_of("1f", 2) + later("1f o") + each("1f h")
        + [("1f m",) + u for u in units(2)]
        + [("2 t",) + u + (0,) for u in units(1)] + turns_of("3", 4) + later("3 o"))

    general, score, turn = (Ring(jobs, 2) for jobs in (general_jobs, score_jobs, turn_jobs))
    powers = [(n, p) for n in ["0", "0f", "1", "1f", "1f h", "2", "2f", "3", "3f"] for p in range(PAIRS)]
    normalised = [(n, s) for n in TAGS for s in range(STREAMS)]
    biased = [(n, s) for n in ["0", "1f", "2f", "3"] for s in range(STREAMS)]
    weighted_rows = [(n, s) for n in ["1f z", "1f h"] for s in range(STREAMS)]
    act_reads = [("1 q",) + u for u in units(2)] + each("1f rows")
    attention = [(tag, s, g) for tag, groups in (("0", 2), ("1", 2), ("1f", 2), ("2", 1), ("3", 4))
                 for s, g in units(groups)]
    prob_jobs = [(tag, s, g, a) for tag, s, g in attention for a in range(1 if tag == "2" else 2)]

    with ExitStack() as ctx:
        def sb(name, cols, dt=F32):
            return ctx.enter_context(nc.sbuf_tensor(name, [P, cols], dt))

        def sem(name):
            return ctx.enter_context(nc.semaphore(name))

        const = sb("const", width(CONST_NAMES))
        C = columns(const, CONST_NAMES)
        at_kT = width(CONST_NAMES[:[n for n, _ in CONST_NAMES].index("cos_kT")])
        cos_sin_kT = const[:, at_kT:at_kT + 2 * P]
        constb = sb("constb", 2 * P, BF16)
        ident_b, causal_b = constb[:, 0:P], constb[:, P:2 * P]
        rows = sb("rows", width(ROW_NAMES))
        R = columns(rows, ROW_NAMES)
        w0, w0f, w1 = sb("w0", width(W0_NAMES)), sb("w0f", width(W0F_NAMES)), sb("w1", width(W1_NAMES))
        w1f, wm = sb("w1f", width(W1F_NAMES)), sb("wm", width(WM_NAMES))
        w2f = sb("w2f", KB * WIDTH)
        w3, w3f = sb("w3", width(W3_NAMES)), sb("w3f", width(W3F_NAMES))
        W0, W0F, W1, W1F = columns(w0, W0_NAMES), columns(w0f, W0F_NAMES), columns(w1, W1_NAMES), columns(w1f, W1F_NAMES)
        WM, W3, W3F = columns(wm, WM_NAMES), columns(w3, W3_NAMES), columns(w3f, W3F_NAMES)
        w_query = sb("w_query", H1 * P)
        w_kv = sb("w_kv", KB * P)
        w_kv_swap = sb("w_kv_swap", KB * ROPE)
        w_out = sb("w_out", H1 // 2 * WIDTH)
        sel_const = sb("sel_const", P + N_SEL)
        ones = sb("ones", P)
        minus_half = sb("minus_half", 4)
        bias_k = sb("bias_k", 2 * KB)

        def per_stream(name, cols, dt=F32):
            return [sb(f"{name}{s}", cols, dt) for s in range(STREAMS)]
        x_in, x, z = (per_stream(n, WIDTH) for n in ("x_in", "x", "z"))
        zT = per_stream("zT", WIDTH)
        cx, cxT = per_stream("cx", WIDTH + 2), per_stream("cxT", WIDTH)
        tA, tB = (per_stream(n, WIDTH) for n in ("tA", "tB"))
        hres, headsT, hrow = tA, tA, tB
        big = per_stream("big", 2048)
        heads_out = [b[:, 1024:2048] for b in big]
        values = per_stream("values", H0 * SLOT)
        values1 = per_stream("values1", KVC + 1)
        qcT, kcT = per_stream("qcT", P), per_stream("kcT", P)
        sel, onehot = sb("sel", STREAMS * P), sb("onehot", STREAMS * P)
        onehotT = per_stream("onehotT", P)
        stats = per_stream("stats", 6)
        mean_var = sb("mean_var", 2 * STREAMS)
        var_eps, rstd = sb("var_eps", 4 * PAIRS), sb("rstd", 4 * PAIRS)
        square_sum = sb("square_sum", STREAMS)
        small = sb("small", (6 * 8 + 3) * STREAMS)
        largest, less_gate = sb("largest", STREAMS), sb("less_gate", STREAMS)
        squares = sb("squares", 64 * STREAMS)
        expert_w = sb("expert_w", EXPERTS * STREAMS)
        seg_i, keep_i, pad_i = sb("seg_i", STREAMS, I32), sb("keep_i", STREAMS * P, U8), sb("pad_i", STREAMS * P, I32)
        seg_f, seg_lo = sb("seg_f", STREAMS), sb("seg_lo", STREAMS)
        valid = sb("valid", STREAMS)
        above, below = sb("above", STREAMS * P), sb("below", STREAMS * P)
        mask1, mask2, mask3 = (per_stream(n, P, BF16) for n in ("mask1", "mask2", "mask3"))
        shifted = sb("shifted", 2 * GROUP * P)
        probs = sb("probs", 4 * 4 * P)
        narrow_out = sb("narrow_out", 2 * GROUP * SLOT)
        peak = sb("peak", 2 * GROUP)
        inverse = sb("inverse", 2 * GROUP)
        q_rows, q_swap = shifted, probs
        tiny = sb("tiny", 10)

        score_psum = [ctx.enter_context(nc.psum_tensor(f"score_psum{i}", [P, 1024], F32)) for i in range(2)]
        turn_psum = [ctx.enter_context(nc.psum_tensor(f"turn_psum{i}", [P, 512], F32)) for i in range(2)]
        general_psum = [ctx.enter_context(nc.psum_tensor(f"general_psum{i}", [P, 512], F32)) for i in range(2)]

        for ring, name, banks in ((score, "score", score_psum), (turn, "turn", turn_psum), (general, "general", general_psum)):
            ring.banks = banks
            ring.filled = [sem(f"{name}_filled{i}") for i in range(2)]
            ring.emptied = [sem(f"{name}_emptied{i}") for i in range(2)]

        loaded = {n: sem(f"{n}_loaded") for n in
                  ["w0", "w0f", "w1", "w1f", "wm", "w2f", "w3", "w3f", "const", "constb", "rows", "prep"]}
        x_loaded, cx_loaded, cxT_loaded = ([sem(f"{n}_loaded{s}") for s in range(STREAMS)] for n in ("x", "cx", "cxT"))
        masks_loaded, x_stored = sem("masks_loaded"), sem("x_stored")
        prep_filled, prep_steps, prep_done = sem("prep_filled"), sem("prep_steps"), sem("prep_done")
        vec_steps = sem("vec_steps")
        power_in, power_out = sem("power_in"), sem("power_out")
        z_ready = sem("z_ready")
        x_in_biased = sem("x_in_biased")
        x_biased = sem("x_biased")
        act_read = sem("act_read")
        q_rotated, qk_ready = sem("q_rotated"), sem("qk_ready")
        gates_in, gates_exp = sem("gates_in"), sem("gates_exp")
        z_squared, h_squared = sem("z_squared"), sem("h_squared")
        onehot_ready = sem("onehot_ready")
        rows_ready = sem("rows_ready")
        router_exp = sem("router_exp")
        tanh_done = sem("tanh_done")
        x_free = sem("x_free")
        keys_copied, keys_turned = sem("keys_copied"), sem("keys_turned")
        keys_ready = sem("keys_ready")
        relu_squared = sem("relu_squared")
        mask_steps, masks_ready = sem("mask_steps"), sem("masks_ready")
        ones_ready, holds = sem("ones_ready"), sem("holds")

        def count(r, events, *event):
            return r * len(events) + events.index(event) + 1

        def nth(r, s):
            return r * STREAMS + s + 1

        waited = {}

        def wait_slot(eng, semaphore, r, uses, k):
            if waited.get((eng, semaphore.name), 0) < k:
                waited[eng, semaphore.name] = k
                eng.wait_ge(semaphore, r * uses + k)

        def filled(eng, ring, r, *job):
            slot, k = ring.place[job]
            wait_slot(eng, ring.filled[slot], r, ring.uses[slot], k)
            return ring.banks[slot]

        def hold(eng):
            eng.sem_inc(holds, 1)

        def free(eng, ring, r, *job):
            slot, k = ring.place[job]
            wait_slot(eng, ring.emptied[slot], r, ring.uses[slot], k)
            return ring.banks[slot]

        def moved(eng, ring, r, *job):
            slot, k = ring.place[job]
            wait_slot(eng, ring.emptied[slot], r, ring.uses[slot], k + 1)

        def all_moved(eng, ring, r, jobs):
            for job in sorted(jobs, key=lambda job: -ring.place[job][1]):
                moved(eng, ring, r, *job)

        def emptied(ring, *job):
            return ring.emptied[ring.place[job][0]]

        def fill(ring, *job):
            return ring.filled[ring.place[job][0]]

        def cell(i):
            return small[:, 8 * STREAMS * i:8 * STREAMS * (i + 1)]

        def of_each(i, n=8):
            return cell(i).rearrange("p (s n) -> p s n", s=STREAMS)[:, :, 0:n]

        def lone(i):
            at = (6 * 8 + i) * STREAMS
            return small[:, at:at + STREAMS]

        def heads(ap, n):
            return ap.rearrange("p (h n) -> p h n", h=n)

        def spread(ap, n):
            return ap.unsqueeze(2).to_broadcast([P, ap.shape[1], n])

        def repeat(ap, n):
            return ap.unsqueeze(1).to_broadcast([P, n, ap.shape[1]])

        def same_slot_before(tag, s, g):
            at = attention.index((tag, s, g))
            slot = score.place[(f"{tag} s", s, g)][0]
            for u in reversed(attention[:at]):
                if score.place[(f"{u[0]} s", u[1], u[2])][0] == slot:
                    return u
            return None

        def last_turn(tag, s, g):
            return (f"{tag} t", s, g, 0 if tag == "2" else 1)

        def small_head(g, i):
            q, c, e = i // 4, (i % 4) // 2, i % 2
            return c * 8 + 4 * g + 2 * q + e

        W1P = {"uqT": big[0][:, 0:H1 * QC], "ukT": big[1][:, 0:H1 * KVC], "uvT": big[1][:, 1024:1024 + H1 * KVC],
               "o0": big[2][:, :], "o1": big[3][:, :],
               "kvcT": shifted[:, 0:KB * P], "qr": shifted[:, 256:256 + H1 * ROPE], "kr": shifted[:, 1280:1280 + 2 * ROPE]}
        w2f_rows = shifted[:, 1408:1408 + KB * WIDTH]
        sel_prod = big[0][:, H1 * QC:H1 * QC + KB * SELW]
        alpha, total, ternary = inverse[:, 0:KB], inverse[:, 2:4], inverse[:, 4:10]

        block = ctx.enter_context(nc.Block())

        @block.sync
        def _(sp):
            sp.dma_start(w0f[:, :], A["w0f"]).then_inc(loaded["w0f"], 16)
            sp.dma_start(w3f[:, :], A["w3f"]).then_inc(loaded["w3f"], 16)
            sp.dma_start(w2f_rows[:, :], A["w2f"]).then_inc(loaded["w2f"], 16)
            sp.dma_start(const[:, :], A["const"]).then_inc(loaded["const"], 16)
            sp.dma_start(w1[:, :], A["w1"]).then_inc(loaded["w1"], 16)
            at = 0
            for part in W1P.values():
                cols = part.shape[1]
                sp.dma_start(part, A["w1p"][:, at:at + cols]).then_inc(loaded["prep"], 16)
                at += cols
            sp.dma_start(constb[:, :], A["constb"]).then_inc(loaded["constb"], 16)
            sp.dma_start(rows[:, :], A["rows"].partition_broadcast(P)).then_inc(loaded["rows"], 16)
            sp.dma_start(w0[:, :], A["w0"]).then_inc(loaded["w0"], 16)
            for s in range(STREAMS):
                sp.dma_start(cxT[s][:, :], A["ctxT"][bass.ds(s, 1)].squeeze(0)).then_inc(cxT_loaded[s], 16)

            def load_context(s, sequence):
                sp.dma_start(cxT[s][:, :], A["ctxT"][sequence].squeeze(0)).then_inc(cxT_loaded[s], 16)

            def load_rows(s, sequence):
                sp.dma_start(cx[s][:, 0:WIDTH], A["ctx"][sequence].squeeze(0)).then_inc(cx_loaded[s], 16)

            def load_x(s, sequence):
                sp.dma_start(x_in[s][:, :], A["x"][sequence].squeeze(0)).then_inc(x_loaded[s], 16)

            def load_masks(now):
                sp.dma_start(seg_i[:, :], A["seg"][now].squeeze(0)).then_inc(masks_loaded, 16)
                sp.dma_start(keep_i[:, :], A["keep"][now].to_broadcast([P, STREAMS * P])).then_inc(masks_loaded, 16)
                sp.dma_start(pad_i[:, :], A["pad"][now].to_broadcast([P, STREAMS * P])).then_inc(masks_loaded, 16)

            def store(r):
                for s in range(STREAMS):
                    moved(sp, general, r, "3f out", s)
                    hold(sp)
                    sp.dma_start(A["out"][bass.ds(r * STREAMS + s, 1)].squeeze(0), x[s][:, :]).then_inc(x_stored, 16)
                sp.wait_ge(x_stored, r * (16 * STREAMS) + 16 * STREAMS)
                sp.sem_inc(x_free, 1)

            sp.sem_inc(x_free, 1)
            load_masks(bass.ds(0, 1))
            for load in (load_x, load_rows):
                for s in range(STREAMS):
                    load(s, bass.ds(s, 1))
            with sp.Fori(0, ROUNDS - 1) as r:
                sp.wait_ge(masks_ready, r + 1)
                hold(sp)
                sp.wait_ge(z_ready, count(r, normalised, "0f", STREAMS - 1))
                hold(sp)
                load_masks(bass.ds(r + 1, 1))
                for s in range(STREAMS):
                    load_x(s, bass.ds(r * STREAMS + (STREAMS + s), 1))
                for s in (STREAMS - 1, STREAMS - 2):
                    filled(sp, general, r, "2 av", s, 0, 0)
                    hold(sp)
                for s in range(STREAMS):
                    load_rows(s, bass.ds(r * STREAMS + (STREAMS + s), 1))
                for s in range(STREAMS):
                    filled(sp, general, r, "3 k", s)
                    hold(sp)
                    load_context(s, bass.ds(r * STREAMS + (STREAMS + s), 1))
                store(r)
            waited.clear()
            store(ROUNDS - 1)

        @block.gpsimd
        def _(pool):
            nc.gpsimd.memset(minus_half[:, :], -0.5)
            for s in range(STREAMS):
                for tile in (values[s], values1[s]):
                    nc.gpsimd.memset(tile[:, :], 1.0)
                nc.gpsimd.memset(cx[s][:, WIDTH:WIDTH + 2], 1.0)
            nc.gpsimd.memset(onehot[:, :], 0.0)
            nc.gpsimd.memset(expert_w[:, :], 0.5 / EXPERT_SCALE)
            nc.gpsimd.memset(ones[:, :], 1.0).then_inc(ones_ready, 1)
            pool.wait_ge(ones_ready, 1)
            pool.wait_ge(loaded["w0"], 16)
            for name, tile in (("w1f", w1f), ("wm", wm), ("w3", w3)):
                pool.dma_start(tile[:, :], A[name]).then_inc(loaded[name], 16)
            for name in ("const", "constb", "rows"):
                pool.wait_ge(loaded[name], 16)

            def power(r, name, n=2):
                for p in range(PAIRS):
                    pool.wait_ge(power_in, count(r, powers, name, p))
                    nc.gpsimd.tensor_tensor(rstd[:, 4 * p:4 * p + n], var_eps[:, 4 * p:4 * p + n], minus_half[:, 0:n],
                                            ALU.pow).then_inc(power_out, 1)

            def add_bias(r, tag, tile, bias, done=x_biased):
                for s in range(STREAMS):
                    pool.wait_ge(z_ready, count(r, normalised, tag, s))
                    nc.gpsimd.tensor_tensor(tile[s][:, :], tile[s][:, :], bias, ALU.add).then_inc(done, 1)

            with pool.Fori(0, ROUNDS) as r:
                power(r, "0")
                pool.wait_ge(masks_loaded, r * 48 + 48)
                hold(pool)
                nc.gpsimd.tensor_copy(seg_f[:, :], seg_i[:, :]).then_inc(mask_steps, 1)
                pool.wait_ge(mask_steps, r * 3 + 1)
                hold(pool)
                nc.gpsimd.tensor_scalar(seg_lo[:, :], seg_f[:, :], float(LOOKBACK), None, ALU.subtract)
                for s in range(STREAMS):
                    own = slice(s * P, s * P + P)
                    nc.gpsimd.tensor_scalar(above[:, own], C["key"], seg_f[:, s:s + 1], MASKED, ALU.is_gt, ALU.mult)
                    nc.gpsimd.tensor_scalar(mask2[s][:, :], keep_i[:, own], 1.0, -MASKED, ALU.subtract, ALU.mult)
                    ins = nc.gpsimd.tensor_scalar(mask3[s][:, :], pad_i[:, own], 0.0, MASKED, ALU.is_equal, ALU.mult)
                ins.then_inc(mask_steps, 1)
                pool.wait_ge(mask_steps, r * 3 + 2)
                hold(pool)
                for s in range(STREAMS):
                    own = slice(s * P, s * P + P)
                    ins = nc.gpsimd.tensor_scalar(below[:, own], C["key"], seg_lo[:, s:s + 1], MASKED, ALU.is_lt, ALU.mult)
                ins.then_inc(mask_steps, 1)
                for s in range(STREAMS):
                    nc.gpsimd.tensor_tensor(mask3[s][:, :], mask3[s][:, :], causal_b, ALU.add)
                pool.wait_ge(mask_steps, r * 3 + 3)
                for s in range(STREAMS):
                    own = slice(s * P, s * P + P)
                    ins = nc.gpsimd.tensor_tensor(mask1[s][:, :], above[:, own], below[:, own], ALU.add)
                ins.then_inc(masks_ready, 1)
                add_bias(r, "0", x_in, R["b_v"], x_in_biased)
                for s in range(STREAMS):
                    pool.wait_ge(x_in_biased, nth(r, s))
                    moved(pool, general, r, "0 ref rows", s)
                    nc.gpsimd.tensor_tensor(x_in[s][:, :], x_in[s][:, :], z[s][:, :], ALU.add).then_inc(x_biased, 1)
                power(r, "0f")
                for s in range(STREAMS):
                    pool.wait_ge(keys_copied, nth(r, s))
                    both = tB[s][KVC:P, :]
                    nc.gpsimd.tensor_tensor(both, both, cos_sin_kT[KVC:P, :], ALU.mult).then_inc(keys_turned, 1)
                    pool.wait_ge(keys_turned, nth(r, s))
                    nc.gpsimd.tensor_tensor(kcT[s][KVC:P, :], both[:, 0:P], both[:, P:2 * P], ALU.add).then_inc(keys_ready, 1)
                pool.wait_ge(keys_ready, nth(r, STREAMS - 1))
                hold(pool)
                power(r, "1")
                power(r, "1f", 4)
                power(r, "1f h")
                for s in range(STREAMS):
                    moved(pool, general, r, "1f out", s)
                    nc.gpsimd.tensor_tensor(x[s][:, :], x[s][:, :], hres[s][:, :], ALU.add).then_inc(x_biased, 1)
                power(r, "2")
                power(r, "2f")
                add_bias(r, "2f", x, R["bias2"])
                power(r, "3")
                add_bias(r, "3", x, R["b_o"])
                power(r, "3f")

        @block.scalar
        def _(act):
            for name in ("const", "w0"):
                act.wait_ge(loaded[name], 16)
            act.wait_ge(prep_done, 4)

            def copy_out(r, ring, job, out, source=lambda bank: bank[:, :]):
                bank = filled(act, ring, r, *job)
                nc.scalar.activation(out, source(bank), ACT.Copy).then_inc(emptied(ring, *job), 1)

            def turned(r, name, streams=range(STREAMS)):
                for s in streams:
                    copy_out(r, general, (name, s), zT[s][:, :], lambda bank: bank[:, 0:WIDTH])

            def biased_blocks(r, name, out, func, bias):
                for s in range(STREAMS):
                    bank = filled(act, general, r, name, s)
                    for b in range(KB):
                        ins = nc.scalar.activation(out[s][:, b * P:b * P + P], bank[:, b * P:b * P + P], func,
                                                   bias=bias[:, b:b + 1], scale=1.0)
                    ins.then_inc(emptied(general, name, s), 1)

            def copy_narrow(r, tag, u, unit):
                at = u % 2 * GROUP * SLOT
                copy_out(r, general, (f"{tag} av",) + unit, narrow_out[:, at:at + GROUP * SLOT], lambda bank: bank[:, 0:GROUP * SLOT])

            def exponentials(r, tag, groups, scale, turns=2, per_turn=4, narrow=True, between=()):
                order = units(groups)
                for u, (s, g) in enumerate(order):
                    for a in range(turns):
                        job = (f"{tag} t", s, g, a)
                        n = prob_jobs.index((tag, s, g, a))
                        if n >= 4:
                            before = prob_jobs[n - 4]
                            filled(act, general, r, f"{before[0]} av", before[1], before[2], *([before[3]] if before[0] in "12" else []))
                        bank = filled(act, turn, r, *job)
                        at = (n % 4) * 512
                        nc.scalar.activation(probs[:, at:at + per_turn * P], bank[:, 0:per_turn * P], ACT.Exp,
                                             scale=scale).then_inc(emptied(turn, *job), 1)
                    if narrow and u:
                        copy_narrow(r, tag, u - 1, order[u - 1])
                    for at_group, work in between:
                        if u == at_group:
                            work()
                if narrow:
                    copy_narrow(r, tag, len(order) - 1, order[-1])

            def keys3_out(r, streams):
                for s in streams:
                    bank = filled(act, general, r, "3 k", s)
                    out = big[s][:, 0:KB * HPG * P].rearrange("p (b h k) -> p b h k", b=KB, h=HPG)
                    for h in range(HPG):
                        ins = nc.scalar.activation(out[:, :, h, :], heads(bank[:, 0:WIDTH], KB), ACT.Copy, scale=C["quarter"][:, h:h + 1])
                    ins.then_inc(emptied(general, "3 k", s), 1)

            with act.Fori(0, ROUNDS) as r:
                biased_blocks(r, "0 sup", tB, ACT.Relu, W0["b_fc"])
                for s in KEYS_BY_SCALAR:
                    bank = filled(act, general, r, "0 k", s)
                    for b in range(KB):
                        for e, mask in enumerate(("even", "odd")):
                            at = (2 * b + e) * P
                            ins = nc.scalar.activation(big[s][:, at:at + P], bank[:, b * P:b * P + P], ACT.Identity,
                                                       bias=bias_k[:, 2 * b + e:2 * b + e + 1], scale=C[mask])
                    ins.then_inc(emptied(general, "0 k", s), 1)
                for s in range(STREAMS):
                    copy_out(r, general, ("0 v", s), heads(values[s][:, :], H0)[:, :, 0:HD0],
                             lambda bank: heads(bank[:, 0:WIDTH], H0))
                turned(r, "0 zT")
                biased_blocks(r, "0 ref", tA, ACT.Relu, W0["b_fc"])
                biased_blocks(r, "0 q", zT, ACT.Identity, W0["b_q"])
                for s in range(STREAMS):
                    copy_out(r, general, ("0 ref rows", s), z[s][:, :], lambda bank: bank[:, 0:WIDTH])
                exponentials(r, "0", 2, HD0 ** -0.5)
                turned(r, "0f zT")
                for s in range(STREAMS):
                    act.wait_ge(z_ready, count(r, normalised, "0f", s))
                    nc.scalar.activation(big[s][:, 1536:1792], z[s][:, :], ACT.Square,
                                         accum_out=square_sum[:, s:s + 1]).then_inc(z_squared, 1)
                for s in range(STREAMS):
                    bank = filled(act, general, r, "1 k", s)
                    nc.scalar.activation(tB[s][KVC:P, :], bank[KVC:P, 0:2 * P], ACT.Copy).then_inc(keys_copied, 1)
                    nc.scalar.activation(kcT[s][0:KVC, :], bank[0:KVC, 0:P], ACT.Copy).then_inc(emptied(general, "1 k", s), 1)
                for s in range(STREAMS):
                    copy_out(r, general, ("1 kv", s), values1[s][:, 0:KVC], lambda bank: bank[:, 0:KVC])
                act.wait_ge(gates_in, r + 1)
                nc.scalar.activation(cell(3), cell(2), ACT.Exp, scale=-1.0).then_inc(gates_exp, 1)
                for s in range(STREAMS):
                    copy_out(r, turn, ("0f onehot", s), onehotT[s][:, :], lambda bank: bank[:, 0:P])
                for pair in BOTH:
                    turned(r, "1 zT", pair)
                    for s in pair:
                        copy_out(r, general, ("1 qc", s), qcT[s][0:QC, :], lambda bank: bank[0:QC, 0:P])
                order = units(2)
                for t in range(len(order) + 1):
                    if t < len(order):
                        s, g = order[t]
                        slot = score.place[("1 q", s, g)][0]
                        if t >= 2:
                            filled(act, turn, r, "1 q", *order[t - 2], 1)
                        bank = filled(act, score, r, "1 q", s, g)
                        nc.scalar.activation(heads(q_rows[:, slot * 1024:(slot + 1) * 1024], GROUP)[:, :, 0:KVC],
                                             heads(bank[:, :], GROUP)[:, :, 0:KVC], ACT.Copy).then_inc(act_read, 1)
                    if t >= 1:
                        s, g = order[t - 1]
                        for a in range(2):
                            at = (g * GROUP + a * 4) * P
                            copy_out(r, turn, ("1 q", s, g, a), big[s][:, at:at + 512])

                def outputs1(streams):
                    for s in streams:
                        for a in range(2):
                            copy_out(r, turn, ("1 o", s, a), big[s][:, a * 1024 + 512:(a + 1) * 1024])

                exponentials(r, "1", 2, float((HD1 + ROPE) ** -0.5), narrow=False, between=[(5, lambda: outputs1(BOTH[0]))])
                outputs1(BOTH[1])
                for pair in BOTH:
                    turned(r, "1f zT", pair)
                    for s in pair:
                        copy_out(r, general, ("1f kq", s), qcT[s][:, :], lambda bank: bank[:, 0:P])
                    for s in pair:
                        bank = filled(act, score, r, "1f rows", s)
                        nc.scalar.activation(heads(heads_out[s][:, 0:512], 2 * LF)[:, :, 0:RD],
                                             heads(bank[:, 0:2 * P], 2 * LF), ACT.Copy)
                        nc.scalar.activation(heads(values[s][:, :], LF)[:, :, 0:2 * RD],
                                             heads(bank[:, 512:512 + WIDTH], LF), ACT.Copy).then_inc(act_read, 1)
                for s in range(STREAMS):
                    bank = filled(act, turn, r, "1f qk", s)
                    nc.scalar.activation(tB[s][:, :], bank[:, 0:WIDTH], ACT.Copy)
                    out = big[s][:, 0:4 * P].rearrange("p (b e k) -> p b e k", b=KB, e=2)
                    for e, mask in enumerate(("even", "odd")):
                        ins = nc.scalar.activation(out[:, :, e, :], heads(bank[:, WIDTH:2 * WIDTH], KB), ACT.Copy, scale=C[mask])
                    ins.then_inc(emptied(turn, "1f qk", s), 1)

                def heads_turned(name, streams):
                    for s in streams:
                        copy_out(r, turn, (name, s), headsT[s][:, :], lambda bank: bank[:, 0:WIDTH])

                def square_h(streams):
                    for s in streams:
                        moved(act, general, r, "1f out", s)
                        nc.scalar.activation(tB[s][:, :], hres[s][:, :], ACT.Square,
                                             accum_out=square_sum[:, s:s + 1]).then_inc(h_squared, 1)

                exponentials(r, "1f", 2, (2 * RD) ** -0.5, between=[(6, lambda: heads_turned("1f o", BOTH[0]))])
                square_h(BOTH[0])
                heads_turned("1f o", BOTH[1])
                square_h(BOTH[1])
                for s in range(STREAMS):
                    copy_out(r, turn, ("1f h", s), zT[s][:, :], lambda bank: bank[:, 0:WIDTH])
                all_moved(act, general, r, [("1f router", s) for s in range(STREAMS)])
                nc.scalar.activation(cell(1), cell(0), ACT.Exp, scale=-1.0).then_inc(router_exp, 1)
                order = units(2)
                for t in range(len(order) + 1):
                    if t < len(order):
                        s, g = order[t]
                        slot = score.place[("1f gu", s, g)][0]
                        bank = filled(act, score, r, "1f gu", s, g)
                        gate = bank[:, :].rearrange("p (e u n) -> p e u n", e=4, u=2)[:, :, 0, :]
                        nc.scalar.activation(heads(q_rows[:, slot * 1024:slot * 1024 + 512], 4), gate, ACT.Tanh,
                                             scale=0.5).then_inc(tanh_done, 1)
                    if t >= 1:
                        s, g = order[t - 1]
                        copy_out(r, turn, ("1f m", s, g), big[s][:, 1024 + g * 512:1536 + g * 512])
                for s in range(STREAMS):
                    copy_out(r, general, ("3 v", s), heads(values[s][:, 0:G3 * SLOT], G3)[:, :, 0:HD3],
                             lambda bank: heads(bank[:, 0:G3 * HD3], G3))
                turned(r, "2 zT")
                exponentials(r, "2", 1, WIDTH ** -0.5, turns=1, per_turn=1, narrow=False)
                keys3_out(r, (0, 1))
                turned(r, "2f zT")
                keys3_out(r, (2, 3))
                for pair in BOTH:
                    turned(r, "3 zT", pair)
                    for s in pair:
                        copy_out(r, general, ("3 q", s), zT[s][:, :], lambda bank: bank[:, 0:WIDTH])
                exponentials(r, "3", 4, HD3 ** -0.5, between=[(10, lambda: heads_turned("3 o", BOTH[0]))])
                heads_turned("3 o", BOTH[1])
                for pair in BOTH:
                    turned(r, "3f zT", pair)
                    for s in pair:
                        bank = filled(act, score, r, "3f h", s)
                        nc.scalar.activation(big[s][:, 0:FF3], bank[:, 0:FF3], ACT.Relu).then_inc(emptied(score, "3f h", s), 1)

        @block.vector
        def _(vec):
            steps, marks = [0], {}

            def prep(ins):
                steps[0] += 1
                ins.then_inc(prep_steps, 1)
                vec.wait_ge(prep_steps, steps[0])

            V = nc.vector
            for name in ("w0f", "w3f"):
                vec.wait_ge(loaded[name], 16)
            for b in range(KB):
                w = W0F["sel"][:, b * SELW:(b + 1) * SELW]
                mean = w[:, P:P + N_SEL]
                out = sel_prod[:, b * SELW:(b + 1) * SELW]
                V.tensor_tensor(heads(out[:, 0:64], N_SEL), heads(w[:, 0:64], N_SEL), spread(mean, SEL), ALU.mult)
                V.tensor_tensor(heads(out[:, 64:128], N_SEL), heads(w[:, 64:128], N_SEL),
                                spread(W0F["debias"][:, b * N_SEL:(b + 1) * N_SEL], LORA), ALU.mult)
                prep(V.tensor_tensor(out[:, P:P + N_SEL], mean, mean, ALU.mult))
            for i, (w, tmp) in enumerate(((W3F["fc"], probs[:, 0:KB * FF3]), (W3F["proj"], probs[:, 0:FB3 * WIDTH]))):
                prep(V.scalar_tensor_tensor(out=tmp, in0=w, scalar=-1.0, in1=w, op0=ALU.mult, op1=ALU.max))
                prep(V.tensor_reduce(total[:, i:i + 1], tmp, X_AXIS, ALU.add))
            V.memset(tiny[:, 0:1], 0.0).then_inc(prep_done, 1)
            vec.wait_ge(loaded["w2f"], 16)
            tmp = probs[:, 0:KB * WIDTH]
            w = w2f_rows[:, :]
            prep(V.scalar_tensor_tensor(out=tmp, in0=w, scalar=-1.0, in1=w, op0=ALU.mult, op1=ALU.max))
            prep(V.tensor_reduce(alpha, heads(tmp, KB), X_AXIS, ALU.add))
            prep(V.tensor_scalar(alpha, alpha, 1.0 / WIDTH, None, ALU.mult))
            prep(V.tensor_scalar(tmp, w, 0.0, 2.0, ALU.is_ge, ALU.mult))
            for b in range(KB):
                own = slice(b * WIDTH, (b + 1) * WIDTH)
                ins = V.tensor_scalar(tmp[:, own], tmp[:, own], -1.0, alpha[:, b:b + 1], ALU.add, ALU.mult)
            prep(ins)
            prep(V.tensor_tensor(tmp, tmp, w, ALU.subtract))
            prep(V.tensor_tensor(w, tmp, w, ALU.add))
            V.memset(tiny[:, 9:10], 0.0).then_inc(prep_done, 1)
            vec.wait_ge(prep_filled, 1)
            V.tensor_copy(sel_const[:, :], general_psum[0][:, 0:SELW])
            scale, thr, low = (ternary[:, i:i + 2] for i in (0, 2, 4))
            prep(V.tensor_scalar(scale, general_psum[0][:, SELW:SELW + 2], 1.0 / (FF3 * WIDTH), 1e-5, ALU.mult, ALU.max))
            V.tensor_scalar(thr, scale, 0.7, None, ALU.mult)
            prep(V.tensor_scalar(low, scale, -0.7, None, ALU.mult))
            for i, w in enumerate((W3F["fc"], W3F["proj"])):
                tmp = probs[:, 0:FB3 * WIDTH]
                prep(V.tensor_scalar(tmp, w, low[:, i:i + 1], None, ALU.is_lt))
                prep(V.scalar_tensor_tensor(out=tmp, in0=w, scalar=thr[:, i:i + 1], in1=tmp, op0=ALU.is_gt, op1=ALU.subtract))
                prep(V.scalar_tensor_tensor(out=tmp, in0=tmp, scalar=scale[:, i:i + 1], in1=w, op0=ALU.mult, op1=ALU.subtract))
                prep(V.tensor_tensor(w, w, tmp, ALU.add))
            vec.wait_ge(loaded["prep"], 16 * len(W1P))
            vec.wait_ge(loaded["w1"], 16)
            V.tensor_copy(heads(w_query[0:QC, :], H1)[:, :, KVC:P], heads(W1P["qr"][0:QC, :], H1))
            V.tensor_copy(heads(w_kv[:, :], KB)[:, :, 0:KVC], heads(W1["kvc"], KB))
            vec.wait_ge(prep_filled, 2)
            V.tensor_copy(w2f[:, :], turn_psum[0][:, :])
            vec.wait_ge(prep_filled, 3)
            kr = turn_psum[1][:, 0:KB * P].rearrange("p (b n) -> p b n", b=KB)
            V.tensor_copy(heads(w_kv[:, :], KB)[:, :, KVC:P], kr[:, :, 0:ROPE])
            V.tensor_copy(heads(w_kv_swap[:, :], KB), kr[:, :, ROPE:P])
            vec.wait_ge(prep_filled, 4)
            for i in range(2):
                bank = (general_psum[1], score_psum[0])[i]
                V.tensor_copy(heads(w_query[0:QC, :], H1)[:, GROUP * i:GROUP * (i + 1), 0:KVC], heads(bank[0:QC, 0:512], GROUP))
            V.memset(tiny[:, 1:2], 0.0).then_inc(prep_done, 1)
            vec.wait_ge(prep_filled, 5)
            for i in range(2):
                V.tensor_copy(w_out[:, 1024 * i:1024 * (i + 1)], score_psum[i][:, :])
            vec.wait_ge(loaded["w0"], 16)
            vec.wait_ge(loaded["const"], 16)
            for b in range(KB):
                for e, mask in enumerate(("even", "odd")):
                    ins = V.tensor_tensor(bias_k[:, 2 * b + e:2 * b + e + 1], W0["b_k"][:, b:b + 1], C[mask], ALU.mult)
            prep(ins)
            V.memset(tiny[:, 2:3], 0.0).then_inc(prep_done, 1)
            for i, s in enumerate(general.emptied + score.emptied + turn.emptied):
                V.memset(tiny[:, 3 + i:4 + i], 0.0).then_inc(s, 1)
            vec.wait_ge(loaded["rows"], 16)

            def step(key, ins):
                steps[0] += 1
                marks[key if isinstance(key, tuple) else (key,)] = steps[0]
                ins.then_inc(vec_steps, 1)

            def after(r, *key):
                vec.wait_ge(vec_steps, r * STEPS + marks[key])

            def root(s, kind=0):
                at = 4 * (s // 2) + 2 * kind + s % 2
                return rstd[:, at:at + 1]

            def z_of(r, tag, source, s):
                vec.wait_ge(power_out, count(r, powers, tag, s // 2))
                V.tensor_scalar(z[s][:, :], source[s][:, :], mean_var[:, 2 * s:2 * s + 1], root(s), ALU.subtract, ALU.mult)\
                    .then_inc(z_ready, 1)

            def by_pairs(*stages, last=None, part=None):
                if part:
                    for stage in (stages if part[1] == "first" else (last,)):
                        for s in BOTH[part[0]]:
                            stage(s)
                    return
                for p in range(PAIRS + 1):
                    pair = (2 * p, 2 * p + 1)
                    if p < PAIRS:
                        for s in pair:
                            stages[0](s)
                    if p and last:
                        for s in (2 * p - 2, 2 * p - 1):
                            last(s)
                    if p < PAIRS:
                        for stage in stages[1:]:
                            for s in pair:
                                stage(s)

            def normalise(r, tag, source, made=None, before=(), also=None, finish=None, while_asked=None, part=None):

                def stats_of(s):
                    if made:
                        made(s)
                    step(("stats", tag, s), V.bn_stats(stats[s][:, :], source[s][:, :]))

                def mean_of(s):
                    after(r, "stats", tag, s)
                    hold(vec)
                    step(("mean", tag, s), V.bn_aggr(mean_var[:, 2 * s:2 * s + 2], stats[s][:, :]))

                def ask(s):
                    if s % 2:
                        after(r, "mean", tag, s)
                        at = 2 * s - 2
                        variances = mean_var[:, at:at + 4].rearrange("p (s k) -> p k s", k=2)[:, 1, :]
                        if also:
                            also(s // 2, variances)
                        V.tensor_scalar(var_eps[:, at:at + 2], variances, EPS, None, ALU.add).then_inc(power_in, 1)

                by_pairs(*before, stats_of, mean_of, ask, *([while_asked] if while_asked else []), last=finish or (lambda s: z_of(r, tag, source, s)),
                         part=part)

            def from_slot(r, *job):
                return lambda s: moved(vec, general, r, job[0], s, *job[1:])

            def update(r, job, bias=None):

                def stage(s):
                    bank = filled(vec, general, r, job, s)
                    if bias is not None:
                        vec.wait_ge(x_biased, count(r, biased, bias, s))
                    V.tensor_tensor(x[s][:, :], x[s][:, :], bank[:, 0:WIDTH], ALU.add).then_inc(emptied(general, job, s), 1)
                return stage

            def update_and_norm(r, job, bias, tag):
                normalise(r, tag, x, from_slot(r, job), [update(r, job, bias)])

            def soften(r, tag, s, g, n):
                job = (f"{tag} s", s, g)
                slot = score.place[job][0]
                bank = filled(vec, score, r, *job)
                top = peak[:, slot * GROUP:slot * GROUP + n]
                step(("peak", tag, s, g), V.tensor_reduce(top, heads(bank[:, 0:n * P], n), X_AXIS, ALU.max))
                before = same_slot_before(tag, s, g)
                if before:
                    filled(vec, turn, r, *last_turn(*before))
                after(r, "peak", tag, s, g)
                V.tensor_tensor(heads(shifted[:, slot * 1024:slot * 1024 + n * P], n), heads(bank[:, 0:n * P], n),
                                spread(top, P), ALU.subtract).then_inc(emptied(score, *job), 1)

            def divide(r, tag, s, g, a, n, cols, out):
                job = (f"{tag} av", s, g, a)
                slot = general.place[job][0]
                bank = filled(vec, general, r, *job)
                result = heads(bank[:, 0:n * (cols + 1)], n)
                inv = inverse[:, slot * GROUP:slot * GROUP + n]
                step(("inverse", tag, s, g, a), V.reciprocal(inv, result[:, :, cols]))
                after(r, "inverse", tag, s, g, a)
                out(result[:, :, 0:cols], inv).then_inc(emptied(general, *job), 1)

            def divide_narrow(r, tag, s, g, out):
                job = (f"{tag} ao", s, g)
                slot = general.place[job][0]
                bank = filled(vec, general, r, *job)
                result = heads(bank[:, 0:GROUP * SLOT], GROUP)
                inv = inverse[:, slot * GROUP:(slot + 1) * GROUP]
                step(("inverse", tag, s, g), V.reciprocal(inv, result[:, :, HD0]))
                after(r, "inverse", tag, s, g)
                cols = out.shape[3]
                V.tensor_tensor(out, result[:, :, 0:cols].rearrange("p (c h) j -> p c h j", c=2),
                                spread(inv, cols).rearrange("p (c h) j -> p c h j", c=2), ALU.mult).then_inc(emptied(general, *job), 1)

            def attend(r, tag, groups, n, normal, behind=3, between=(), after_normal=()):
                order = units(groups)
                for t in range(len(order) + behind):
                    for at_step, work in between:
                        if t == at_step:
                            work()
                    if t < len(order):
                        soften(r, tag, *order[t], n)
                    if t >= behind:
                        normal(*order[t - behind])
                    for at_step, work in after_normal:
                        if t == at_step:
                            work()

            def rotate(r, target, turning, cosine, sine, n, width, tmp, slot_free):
                half = width // 2
                V.tensor_tensor(target, turning, repeat(cosine, n), ALU.mult)
                V.tensor_tensor(tmp[:, :, 0:half], turning[:, :, half:width], repeat(sine[:, 0:half], n), ALU.mult)
                V.tensor_tensor(tmp[:, :, half:width], turning[:, :, 0:half], repeat(sine[:, half:width], n), ALU.mult)\
                    .then_inc(slot_free, 1)

            with vec.Fori(0, ROUNDS) as r:
                steps[0] = 0
                for s in range(STREAMS):
                    vec.wait_ge(x_loaded[s], r * 16 + 16)
                normalise(r, "0", x_in)
                for s in KEYS_BY_VECTOR:
                    bank = filled(vec, general, r, "0 k", s)
                    out = big[s][:, 0:4 * P].rearrange("p (b e k) -> p b e k", b=KB, e=2)
                    for b in range(KB):
                        for e, mask in enumerate(("even", "odd")):
                            ins = V.tensor_scalar(out[:, b, e, :], bank[:, b * P:b * P + P], W0["b_k"][:, b:b + 1], C[mask],
                                                  ALU.add, ALU.mult)
                    ins.then_inc(emptied(general, "0 k", s), 1)
                vec.wait_ge(masks_loaded, r * 48 + 48)
                V.tensor_reduce(valid[:, :], heads(keep_i[:, :], STREAMS), X_AXIS, ALU.max)
                def divide_small(tag):
                    return lambda s, g: divide_narrow(r, tag, s, g, heads_out[s][:, 0:WIDTH].rearrange(
                        "p (c h j) -> p c h j", c=KB, h=GROUP)[:, :, 4 * g:4 * g + 4, :])

                def plus_attention(s):
                    if s == 0:
                        vec.wait_ge(x_free, r + 1)
                    moved(vec, general, r, "0 ao", s, 1)
                    vec.wait_ge(x_biased, count(r, biased, "0", s))
                    step(("x0", s), V.tensor_tensor(x[s][:, :], x_in[s][:, :], heads_out[s][:, 0:WIDTH], ALU.add))

                def finish0(pair, which):
                    normalise(r, "0f", x, lambda s: after(r, "x0", s), [plus_attention], part=(pair, which))

                attend(r, "0", 2, GROUP, divide_small("0"), after_normal=[(7, lambda: finish0(0, "first")), (8, lambda: finish0(0, "last"))])
                finish0(1, "first")
                finish0(1, "last")

                for s in range(STREAMS):
                    vec.wait_ge(z_ready, count(r, normalised, "0f", s))
                    step(("x+z", s), V.tensor_tensor(x[s][:, :], x[s][:, :], z[s][:, :], ALU.add))
                for s in range(STREAMS):
                    bank = filled(vec, general, r, "0f sel", s)
                    ins = V.tensor_tensor(sel[:, s * P:(s + 1) * P], bank[:, 0:P], sel_const[:, 0:P], ALU.subtract)
                    if s == STREAMS - 1:
                        step("diff", ins)
                    ins = V.scalar_tensor_tensor(out=cell(0)[:, s * 8:s * 8 + 8], in0=bank[:, P:P + N_SEL], scalar=-2.0,
                                                 in1=sel_const[:, P:P + N_SEL], op0=ALU.mult, op1=ALU.add)
                    ins.then_inc(emptied(general, "0f sel", s), 1)
                after(r, "diff")
                chosen, lora = heads(sel[:, :], STREAMS)[:, :, 0:64], heads(sel[:, :], STREAMS)[:, :, 64:P]
                step("square", V.tensor_tensor(heads(squares[:, :], STREAMS), chosen, chosen, ALU.mult))
                all_moved(vec, general, r, [("0f sel", s) for s in range(STREAMS)])
                vec.wait_ge(z_squared, nth(r, STREAMS - 1))
                step("length", V.tensor_tensor(of_each(0), of_each(0), spread(square_sum[:, :], N_SEL), ALU.add))
                after(r, "square")
                step("content", V.tensor_reduce(cell(1), heads(squares[:, :], STREAMS * N_SEL), X_AXIS, ALU.add))
                after(r, "length")
                step("1/length", V.reciprocal(cell(0), cell(0)))
                after(r, "1/length")
                step("ratio", V.tensor_tensor(cell(1), cell(1), cell(0), ALU.mult))
                after(r, "ratio")
                step("score", V.tensor_tensor(of_each(1), of_each(1), repeat(R["center"], STREAMS), ALU.subtract))
                after(r, "score")
                V.tensor_tensor(of_each(2), of_each(1), repeat(R["slope"], STREAMS), ALU.mult).then_inc(gates_in, 1)
                vec.wait_ge(gates_exp, r + 1)
                step("1+exp", V.tensor_scalar(cell(3), cell(3), 1.0, None, ALU.add))
                after(r, "1+exp")
                step("gate", V.reciprocal(cell(3), cell(3)))
                after(r, "gate")
                step("largest", V.tensor_reduce(largest[:, :], of_each(3), X_AXIS, ALU.max))
                after(r, "largest")
                step("-gate", V.tensor_scalar(less_gate[:, :], largest[:, :], -1.0, None, ALU.mult))
                step("are largest", V.tensor_tensor(of_each(4), of_each(3), spread(largest[:, :], N_SEL), ALU.is_ge))
                after(r, "are largest")
                step("candidates", V.tensor_tensor(of_each(4), of_each(4), repeat(C["falling"], STREAMS), ALU.mult))
                after(r, "candidates")
                step("first", V.tensor_reduce(lone(0), of_each(4), X_AXIS, ALU.max))
                after(r, "first")
                step("which", V.tensor_tensor(heads(onehot[:, :], STREAMS)[:, :, 64:72], of_each(4), spread(lone(0), N_SEL), ALU.is_equal))
                after(r, "which")
                for s in range(STREAMS):
                    V.tensor_tensor(heads(onehot[:, s * P:s * P + 64], N_SEL), heads(lora[:, s, :], N_SEL),
                                    spread(onehot[:, s * P + 64:s * P + 72], LORA), ALU.mult).then_inc(onehot_ready, 1)

                after(r, "-gate")
                def gated(s):
                    bank = filled(vec, general, r, "0f mod", s)
                    after(r, "x+(1-gate)z", s)
                    V.scalar_tensor_tensor(out=x[s][:, :], in0=bank[:, 0:WIDTH], scalar=largest[:, s:s + 1], in1=x[s][:, :],
                                           op0=ALU.mult, op1=ALU.add).then_inc(emptied(general, "0f mod", s), 1)

                for s in range(STREAMS):
                    after(r, "x+z", s)
                    step(("x+(1-gate)z", s), V.scalar_tensor_tensor(out=x[s][:, :], in0=z[s][:, :], scalar=less_gate[:, s:s + 1],
                                                                    in1=x[s][:, :], op0=ALU.mult, op1=ALU.add))
                normalise(r, "1", x, from_slot(r, "0f mod"), [gated])

                for i, (s, g) in enumerate(units(2)):
                    slot = score.place[("1 q", s, g)][0]
                    bank = filled(vec, score, r, "1 q", s, g)
                    vec.wait_ge(act_read, count(r, act_reads, "1 q", s, g))
                    rope = heads(q_rows[:, slot * 1024:(slot + 1) * 1024], GROUP)[:, :, KVC:P]
                    tmp = heads(q_swap[:, slot * 512:(slot + 1) * 512], GROUP)
                    rotate(r, rope, heads(bank[:, :], GROUP)[:, :, KVC:P], C["cos_q"], C["sin_q"], GROUP, ROPE, tmp,
                           emptied(score, "1 q", s, g))
                    moved(vec, score, r, "1 q", s, g)
                    V.tensor_tensor(rope, rope, tmp, ALU.add).then_inc(q_rotated, 1)

                def divide1(s, g):
                    for a in range(2):
                        at = g * 1024 + a * 4 * KVC
                        out = heads(big[s][:, at:at + 4 * KVC], 4)
                        divide(r, "1", s, g, a, 4, KVC, lambda result, inv: V.tensor_tensor(out, result, spread(inv, KVC), ALU.mult))


                def second_root(p, variances):
                    V.tensor_scalar(var_eps[:, 4 * p + 2:4 * p + 4], variances, 1.0 + EPS, EPS * EPS, ALU.mult, ALU.add)

                def weighted(s):
                    after(r, "mean", "1f", s)
                    step(("weighted", s), V.scalar_tensor_tensor(out=hrow[s][:, :], in0=x[s][:, :], scalar=mean_var[:, 2 * s:2 * s + 1],
                                                                 in1=R["ln1"], op0=ALU.subtract, op1=ALU.mult))

                def both_rows(s):
                    vec.wait_ge(power_out, count(r, powers, "1f", s // 2))
                    after(r, "weighted", s)
                    V.tensor_scalar(hrow[s][:, :], hrow[s][:, :], root(s, 1), None, ALU.mult).then_inc(rows_ready, 1)
                    z_of(r, "1f", x, s)

                def finish1(pair, which):
                    normalise(r, "1f", x, from_slot(r, "1 out"), (), second_root, both_rows, weighted, part=(pair, which))

                update1 = update(r, "1 out")

                attend(r, "1", 2, GROUP, divide1, behind=2, between=[(8, lambda: update1(0)), (9, lambda: update1(1))],
                       after_normal=[(9, lambda: finish1(0, "first"))])
                update1(2)
                finish1(0, "last")
                update1(3)
                finish1(1, "first")
                finish1(1, "last")

                for s in range(STREAMS):
                    bank = filled(vec, score, r, "1f rows", s)
                    vec.wait_ge(act_read, count(r, act_reads, "1f rows", s))
                    rope = heads(heads_out[s][:, 0:512], 2 * LF)[:, :, RD:2 * RD]
                    tmp = heads(tA[s][:, :], 2 * LF)
                    rotate(r, rope, heads(bank[:, 2 * P:4 * P], 2 * LF), C["cos_f"], C["sin_f"], 2 * LF, RD, tmp,
                           emptied(score, "1f rows", s))
                    moved(vec, score, r, "1f rows", s)
                    V.tensor_tensor(rope, rope, tmp, ALU.add).then_inc(qk_ready, 1)

                def residual(s):
                    bank = filled(vec, general, r, "1f out", s)
                    V.tensor_tensor(hres[s][:, :], z[s][:, :], bank[:, 0:WIDTH], ALU.add).then_inc(emptied(general, "1f out", s), 1)

                def ask_h(s):
                    if s % 2:
                        vec.wait_ge(h_squared, nth(r, s))
                        V.tensor_scalar(var_eps[:, 2 * s - 2:2 * s], square_sum[:, s - 1:s + 1], 1.0 / WIDTH, EPS, ALU.mult, ALU.add)\
                            .then_inc(power_in, 1)

                def h_rows(s):
                    vec.wait_ge(power_out, count(r, powers, "1f h", s // 2))
                    V.scalar_tensor_tensor(out=hrow[s][:, :], in0=hres[s][:, :], scalar=root(s), in1=R["ln2"],
                                           op0=ALU.mult, op1=ALU.mult).then_inc(rows_ready, 1)

                attend(r, "1f", 2, GROUP, divide_small("1f"), between=[(9, lambda: residual(0)), (10, lambda: residual(1))])
                ask_h(1)
                residual(2)
                residual(3)
                h_rows(0)
                h_rows(1)
                ask_h(3)
                h_rows(2)
                h_rows(3)

                N = EXPERTS - 1

                for s in range(STREAMS):
                    bank = filled(vec, general, r, "1f router", s)
                    V.tensor_tensor(cell(0)[:, s * 8:s * 8 + 8], bank[:, 0:8], R["router_b"], ALU.add).then_inc(emptied(general, "1f router", s), 1)
                vec.wait_ge(router_exp, r + 1)
                step("1+exp r", V.tensor_scalar(cell(1), cell(1), 1.0, None, ALU.add))
                after(r, "1+exp r")
                step("probability", V.reciprocal(cell(1), cell(1)))
                after(r, "probability")

                def take(name, source, best, target):
                    step(name + " best", V.tensor_reduce(best, source, X_AXIS, ALU.max))
                    after(r, name + " best")
                    step(name + " are", V.tensor_tensor(of_each(2, N), source, spread(best, N), ALU.is_ge))
                    after(r, name + " are")
                    step(name + " candidates", V.tensor_tensor(of_each(2, N), of_each(2, N), repeat(C["falling"][:, 0:N], STREAMS), ALU.mult))
                    after(r, name + " candidates")
                    step(name + " first", V.tensor_reduce(lone(0), of_each(2, N), X_AXIS, ALU.max))
                    after(r, name + " first")
                    step(name, V.tensor_tensor(target, of_each(2, N), spread(lone(0), N), ALU.is_equal))
                    after(r, name)

                take("one", of_each(1, N), lone(1), of_each(3, N))
                step("without one", V.scalar_tensor_tensor(out=of_each(4, N), in0=of_each(3, N), scalar=-2.0, in1=of_each(1, N),
                                                           op0=ALU.mult, op1=ALU.add))
                after(r, "without one")
                take("two", of_each(4, N), lone(2), of_each(5, N))
                step("both", V.tensor_tensor(of_each(5, N), of_each(5, N), of_each(3, N), ALU.add))
                step("sum", V.tensor_tensor(lone(1), lone(1), lone(2), ALU.add))
                after(r, "sum")
                step("1/sum", V.reciprocal(lone(1), lone(1)))
                after(r, "1/sum")
                step("scaled", V.tensor_scalar(lone(1), lone(1), 0.5 / EXPERT_SCALE, None, ALU.mult))
                step("chosen", V.tensor_tensor(of_each(5, N), of_each(5, N), of_each(1, N), ALU.mult))
                after(r, "chosen")
                step("expert weights", V.tensor_tensor(heads(expert_w[:, :], STREAMS)[:, :, 1:8], of_each(5, N), spread(lone(1), N), ALU.mult))

                update1f = update(r, "1f moe", "1f")

                def finish1f(pair, which):
                    normalise(r, "2", x, from_slot(r, "1f moe"), part=(pair, which))

                for u, (s, g) in enumerate(units(2)):
                    job = ("1f gu", s, g)
                    slot = score.place[job][0]
                    bank = filled(vec, score, r, *job)
                    vec.wait_ge(tanh_done, count(r, units(2), s, g))
                    gu = bank[:, :].rearrange("p (e u n) -> p e u n", e=4, u=2)
                    th = heads(q_rows[:, slot * 1024:slot * 1024 + 512], 4)
                    ga = heads(q_rows[:, slot * 1024 + 512:slot * 1024 + 1024], 4)
                    step(("silu", s, g), V.scalar_tensor_tensor(out=ga, in0=th, scalar=1.0, in1=gu[:, :, 0, :],
                                                                op0=ALU.add, op1=ALU.mult))
                    after(r, "expert weights")
                    after(r, "silu", s, g)
                    for e in range(4):
                        ins = V.scalar_tensor_tensor(
                            out=big[s][:, (4 * g + e) * INNER:(4 * g + e + 1) * INNER], in0=ga[:, e, :],
                            scalar=expert_w[:, s * EXPERTS + 4 * g + e:s * EXPERTS + 4 * g + e + 1], in1=gu[:, e, 1, :], op0=ALU.mult, op1=ALU.mult)
                    ins.then_inc(emptied(score, *job), 1)
                    if u in (3, 5):
                        update1f((u - 3) // 2)
                finish1f(0, "first")
                update1f(2)
                finish1f(0, "last")
                update1f(3)
                finish1f(1, "first")
                finish1f(1, "last")

                def divide2(s, g):
                    def out(result, inv):
                        step(("kept inverse", s), V.tensor_tensor(inv, inv, valid[:, s:s + 1], ALU.mult))
                        after(r, "kept inverse", s)
                        return V.scalar_tensor_tensor(out=x[s][:, :], in0=result[:, 0, :], scalar=inv, in1=x[s][:, :],
                                                      op0=ALU.mult, op1=ALU.add)
                    divide(r, "2", s, g, 0, 1, WIDTH, out)

                attend(r, "2", 1, 1, divide2, behind=2)
                normalise(r, "2f", x, from_slot(r, "2 av", 0, 0))
                update_and_norm(r, "2f out", "2f", "3")

                def divide3(s, g):
                    divide_narrow(r, "3", s, g, heads_out[s][:, g * GROUP * HD3:(g + 1) * GROUP * HD3].rearrange(
                        "p (c h j) -> p c h j", c=2, h=HPG))

                update3 = update(r, "3 out", "3")

                def finish3(pair, which):
                    normalise(r, "3f", x, from_slot(r, "3 out"), part=(pair, which))

                attend(r, "3", 4, GROUP, divide3, between=[(13, lambda: update3(0)), (14, lambda: update3(1))],
                       after_normal=[(14, lambda: finish3(0, "first")), (15, lambda: finish3(0, "last"))])
                update3(2)
                update3(3)
                finish3(1, "first")
                finish3(1, "last")

                for s in range(STREAMS):
                    moved(vec, score, r, "3f h", s)
                    V.tensor_tensor(big[s][:, 1024:1024 + FF3], big[s][:, 0:FF3], big[s][:, 0:FF3], ALU.mult).then_inc(relu_squared, 1)
                by_pairs(update(r, "3f out"))
                assert steps[0] < STEPS, steps[0]
                vec.sem_inc(vec_steps, STEPS - steps[0])

        @block.tensor
        def _(pe):
            T = nc.tensor
            ident = C["ident"]

            pe.wait_ge(ones_ready, 1)
            pe.wait_ge(prep_done, 1)
            for b in range(KB):
                T.matmul(general_psum[0][:, 0:SELW], ones[:, :], sel_prod[:, b * SELW:(b + 1) * SELW], start=(b == 0), stop=(b == KB - 1))
            T.matmul(general_psum[0][:, SELW:SELW + 2], ones[:, :], total, start=True, stop=True).then_inc(prep_filled, 1)
            pe.wait_ge(loaded["const"], 16)
            pe.wait_ge(prep_done, 2)
            for i in range(KB):
                for b in range(KB):
                    ins = T.transpose(turn_psum[0][:, i * WIDTH + b * P:i * WIDTH + b * P + P],
                                      w2f_rows[:, b * WIDTH + i * P:b * WIDTH + i * P + P], ident)
            ins.then_inc(prep_filled, 1)
            pe.wait_ge(loaded["prep"], 16 * len(W1P))
            pe.wait_ge(loaded["w1"], 16)
            for b in range(KB):
                ins = T.matmul(turn_psum[1][:, b * P:b * P + P], W1P["kvcT"][0:KVC, b * P:b * P + P], W1P["kr"][0:KVC, :],
                               start=True, stop=True)
            ins.then_inc(prep_filled, 1)
            for h in range(H1):
                bank = (general_psum[1], score_psum[0])[h // GROUP]
                at = h % GROUP * KVC
                ins = T.matmul(bank[0:QC, at:at + KVC], W1P["uqT"][:, h * QC:(h + 1) * QC], W1P["ukT"][:, h * KVC:(h + 1) * KVC],
                               start=True, stop=True)
            ins.then_inc(prep_filled, 1)
            pe.wait_ge(prep_done, 3)
            for h in range(H1):
                pair, row = h // 2, h % 2 * KVC
                out = score_psum[pair // 4][row:row + KVC, pair % 4 * WIDTH:(pair % 4 + 1) * WIDTH]
                ins = T.matmul(out, W1P["uvT"][:, h * KVC:(h + 1) * KVC], W1P[f"o{h // GROUP}"][:, h % GROUP * WIDTH:(h % GROUP + 1) * WIDTH],
                               start=True, stop=True)
            ins.then_inc(prep_filled, 1)
            pe.wait_ge(loaded["w0"], 16)
            pe.wait_ge(loaded["constb"], 16)

            def turn_rows(bank, source, n=KB):
                for b in range(n):
                    ins = T.transpose(bank[:, b * P:b * P + P], source[:, b * P:b * P + P], ident)
                return ins

            def blocks_out(bank, w, cols, actT, n=KB):
                for m in range(n):
                    for b in range(KB):
                        ins = T.matmul(bank[:, m * P:m * P + P], w[:, b * cols + m * P:b * cols + m * P + P], actT[:, b * P:b * P + P],
                                       start=(b == 0), stop=(b == KB - 1))
                return ins

            def rows_out(out, actT, w, cols, n=KB, at=0):
                wide = out.shape[1]
                for b in range(n):
                    ins = T.matmul(out, actT[:, b * P:b * P + P], w[:, b * cols + at:b * cols + at + wide], start=(b == 0), stop=(b == n - 1))
                return ins

            def job(ring, r, *key):
                return free(pe, ring, r, *key)

            def done(ins, ring, *key):
                ins.then_inc(fill(ring, *key), 1)

            def stay_warm(bank, n):
                for _ in range(n):
                    T.matmul(bank[:, 0:2 * P], ident_b, constb[:, :], start=True, stop=True)

            def turn_z(r, name, tag, streams=range(STREAMS), warm=WARM_Z):
                for s in streams:
                    bank = job(general, r, name, s)
                    stay_warm(bank, warm[s])
                    pe.wait_ge(z_ready, count(r, normalised, tag, s))
                    done(turn_rows(bank, z[s]), general, name, s)

            def masked(bank, mask, n, last=False):
                return T.matmul(bank, ident_b, repeat(mask[:, :], n), start=True, stop=last)

            def scores_and_turns(r, tag, t, order, per, turns, scores):
                if t < len(order):
                    s, g = order[t]
                    bank = job(score, r, f"{tag} s", s, g)
                    done(scores(s, g, bank), score, f"{tag} s", s, g)
                if 1 <= t <= len(order):
                    s, g = order[t - 1]
                    slot = score.place[(f"{tag} s", s, g)][0]
                    for a in range(turns):
                        bank = job(turn, r, f"{tag} t", s, g, a)
                        if a == 0:
                            if t == 1:
                                stay_warm(bank, WARM_T[tag])
                            moved(pe, score, r, f"{tag} s", s, g)
                        done(turn_rows(bank, shifted[:, slot * 1024 + a * 512:slot * 1024 + a * 512 + per * P], per),
                             turn, f"{tag} t", s, g, a)

            def attend(r, tag, groups, n, scores, value, wide, turns=2, between=()):
                order = units(groups)
                per = n // turns
                for t in range(len(order) + 2):
                    scores_and_turns(r, tag, t, order, per, turns, scores)
                    if t >= 2:
                        s, g = order[t - 2]
                        for a in range(turns):
                            key = (f"{tag} av", s, g, a)
                            bank = job(general, r, *key)
                            moved(pe, turn, r, f"{tag} t", s, g, a)
                            at = (prob_jobs.index((tag, s, g, a)) % 4) * 512
                            for i in range(per):
                                ins = T.matmul(bank[:, i * wide:(i + 1) * wide], probs[:, at + i * P:at + i * P + P], value(s),
                                               start=True, stop=True)
                            done(ins, general, *key)
                    for at_step, work in between:
                        if t == at_step:
                            work()

            def attend_narrow(r, tag, groups, scores, place, between=()):
                order = units(groups)
                for t in range(len(order) + 3):
                    scores_and_turns(r, tag, t, order, 4, 2, scores)
                    if 2 <= t < len(order) + 2:
                        s, g = order[t - 2]
                        bank = job(general, r, f"{tag} av", s, g)
                        for a in range(2):
                            moved(pe, turn, r, f"{tag} t", s, g, a)
                            at = (prob_jobs.index((tag, s, g, a)) % 4) * 512
                            for i in range(4):
                                v, block, row = place(g, a * 4 + i)
                                ins = T.matmul(bank[SLOT * row:SLOT * (row + 1), block * P:(block + 1) * P],
                                               values[s][:, v * SLOT:(v + 1) * SLOT], probs[:, at + i * P:at + i * P + P],
                                               start=True, stop=True)
                        done(ins, general, f"{tag} av", s, g)
                    if t >= 3:
                        s, g = order[t - 3]
                        bank = job(general, r, f"{tag} ao", s, g)
                        moved(pe, general, r, f"{tag} av", s, g)
                        at = (t - 3) % 2 * GROUP * SLOT
                        done(turn_rows(bank, narrow_out[:, at:at + GROUP * SLOT]), general, f"{tag} ao", s, g)
                    for at_step, work in between:
                        if t == at_step:
                            work()

            def keys3_in(r, streams):
                for s in streams:
                    done(blocks_out(job(general, r, "3 k", s), W3["k"], WIDTH, cxT[s]), general, "3 k", s)

            with pe.Fori(0, ROUNDS) as r:
                for s in range(STREAMS):
                    pe.wait_ge(cxT_loaded[s], r * 16 + 16)
                    done(blocks_out(job(general, r, "0 sup", s), W0["fc"], WIDTH, cxT[s]), general, "0 sup", s)
                for s in range(STREAMS):
                    bank = job(general, r, "0 k", s)
                    moved(pe, general, r, "0 sup", s)
                    done(blocks_out(bank, W0["k"], WIDTH, tB[s]), general, "0 k", s)
                for s in range(STREAMS):
                    done(rows_out(job(general, r, "0 v", s)[:, 0:WIDTH], tB[s], W0["v"], WIDTH), general, "0 v", s)
                turn_z(r, "0 zT", "0", warm=(0, 0, 0, 0))
                for s in range(STREAMS):
                    bank = job(general, r, "0 ref", s)
                    moved(pe, general, r, "0 zT", s)
                    done(blocks_out(bank, W0["fc"], WIDTH, zT[s]), general, "0 ref", s)
                for s in range(STREAMS):
                    bank = job(general, r, "0 q", s)
                    moved(pe, general, r, "0 ref", s)
                    done(blocks_out(bank, W0["q"], WIDTH, tA[s]), general, "0 q", s)
                for s in range(STREAMS):
                    done(turn_rows(job(general, r, "0 ref rows", s), tA[s]), general, "0 ref rows", s)

                def small_scores(tag, queries, mask=None):
                    def scores(s, g, bank):
                        if g == 0:
                            if tag == "0":
                                moved(pe, general, r, "0 k", s)
                                moved(pe, general, r, "0 q", s)
                                moved(pe, general, r, "0 v", s)
                            else:
                                moved(pe, turn, r, "1f qk", s)
                        keys = big[s][:, 0:4 * P].rearrange("p (b e k) -> p b (e k)", b=KB, e=2)
                        for q in range(2):
                            row = 32 * (2 * g + q)
                            if mask is not None:
                                masked(bank[:, q * 512:(q + 1) * 512], mask, 4)
                            for b in range(KB):
                                at = q * 512 + b * 256
                                ins = T.matmul(bank[:, at:at + 256], queries[s][row:row + 32, b * P:b * P + P], keys[row:row + 32, b, :],
                                               start=(mask is None), stop=(mask is None or b == KB - 1))
                        return ins
                    return scores

                def small_place(g, i):
                    return small_head(g, i), i % 4 // 2, i // 4 * 2 + i % 2

                attend_narrow(r, "0", 2, small_scores("0", zT), small_place)

                for pair in BOTH:
                    turn_z(r, "0f zT", "0f", pair)
                    for s in pair:
                        bank = job(general, r, "0f sel", s)
                        moved(pe, general, r, "0f zT", s)
                        done(rows_out(bank[:, 0:SELW], zT[s], W0F["sel"], SELW), general, "0f sel", s)
                for s in range(STREAMS):
                    bank = job(general, r, "1 k", s)
                    blocks_out(bank, w_kv, P, cxT[s], 1)
                    for b in range(KB):
                        ins = T.matmul(bank[KVC:P, P:2 * P], w_kv_swap[:, b * ROPE:(b + 1) * ROPE], cxT[s][:, b * P:b * P + P],
                                       start=(b == 0), stop=(b == KB - 1))
                    done(ins, general, "1 k", s)
                for s in range(STREAMS):
                    done(rows_out(job(general, r, "1 kv", s)[:, 0:KVC], cxT[s], W1["kvc"], KVC), general, "1 kv", s)
                for s in range(STREAMS):
                    bank = job(turn, r, "0f onehot", s)
                    if s == 0:
                        stay_warm(bank, WARM_O)
                    pe.wait_ge(onehot_ready, nth(r, s))
                    done(turn_rows(bank, onehot[:, s * P:(s + 1) * P], 1), turn, "0f onehot", s)
                for s in range(STREAMS):
                    bank = job(general, r, "0f mod", s)
                    moved(pe, turn, r, "0f onehot", s)
                    done(T.matmul(bank[:, 0:WIDTH], onehotT[s][:, :], W0F["lift"], start=True, stop=True), general, "0f mod", s)

                for pair in BOTH:
                    turn_z(r, "1 zT", "1", pair)
                    for s in pair:
                        bank = job(general, r, "1 qc", s)
                        moved(pe, general, r, "1 zT", s)
                        for b in range(KB):
                            ins = T.matmul(bank[0:QC, 0:P], W1["dq"][:, b * QC:(b + 1) * QC], zT[s][:, b * P:b * P + P],
                                           start=(b == 0), stop=(b == KB - 1))
                        done(ins, general, "1 qc", s)
                order = units(2)
                for t in range(len(order) + 1):
                    if t < len(order):
                        s, g = order[t]
                        bank = job(score, r, "1 q", s, g)
                        moved(pe, general, r, "1 qc", s)
                        for q in range(2):
                            at = g * 1024 + q * 512
                            ins = T.matmul(bank[:, q * 512:(q + 1) * 512], qcT[s][0:QC, :], w_query[0:QC, at:at + 512], start=True, stop=True)
                        done(ins, score, "1 q", s, g)
                    if t >= 1:
                        s, g = order[t - 1]
                        slot = score.place[("1 q", s, g)][0]
                        for a in range(2):
                            bank = job(turn, r, "1 q", s, g, a)
                            pe.wait_ge(q_rotated, r * len(order) + t)
                            done(turn_rows(bank, q_rows[:, slot * 1024 + a * 512:slot * 1024 + (a + 1) * 512], 4), turn, "1 q", s, g, a)

                def scores1(s, g, bank):
                    if g == 0:
                        moved(pe, turn, r, "1 q", s, 1, 1)
                        pe.wait_ge(keys_ready, nth(r, s))
                        pe.wait_ge(masks_ready, r + 1)
                    for q in range(2):
                        masked(bank[:, q * 512:(q + 1) * 512], mask1[s], 4)
                        for i in range(4):
                            at = (q * 4 + i) * P
                            h = g * GROUP + q * 4 + i
                            ins = T.matmul(bank[:, at:at + P], big[s][:, h * P:h * P + P], kcT[s][:, :], start=False, stop=(i == 3))
                    return ins

                def turn_outputs1(streams):
                    for s in streams:
                        for a in range(2):
                            bank = job(turn, r, "1 o", s, a)
                            for i in range(2):
                                moved(pe, general, r, "1 av", s, a, i)
                            done(turn_rows(bank, big[s][:, a * 1024:a * 1024 + 512], 4), turn, "1 o", s, a)

                def output1(s):
                    bank = job(general, r, "1 out", s)
                    for a in range(2):
                        moved(pe, turn, r, "1 o", s, a)
                    for pair in range(H1 // 2):
                        at = pair // 4 * 1024 + 512 + pair % 4 * P
                        ins = T.matmul(bank[:, 0:WIDTH], big[s][:, at:at + P], w_out[:, pair * WIDTH:(pair + 1) * WIDTH],
                                       start=(pair == 0), stop=(pair == H1 // 2 - 1))
                    done(ins, general, "1 out", s)

                attend(r, "1", 2, GROUP, scores1, lambda s: values1[s][:, 0:KVC + 1], KVC + 1,
                       between=[(6, lambda: turn_outputs1(BOTH[0])), (7, lambda: output1(0)), (8, lambda: output1(1))])
                turn_outputs1(BOTH[1])
                for s in BOTH[1]:
                    output1(s)

                pe.wait_ge(loaded["w1f"], 16)
                for pair in BOTH:
                    for s in pair:
                        bank = job(general, r, "1f zT", s)
                        stay_warm(bank, WARM_R[s])
                        pe.wait_ge(rows_ready, count(r, weighted_rows, "1f z", s))
                        done(turn_rows(bank, hrow[s]), general, "1f zT", s)
                    for s in pair:
                        bank = job(general, r, "1f kq", s)
                        moved(pe, general, r, "1f zT", s)
                        done(blocks_out(bank, W1F["down_kq"], P, zT[s], 1), general, "1f kq", s)
                    for s in pair:
                        bank = job(score, r, "1f rows", s)
                        moved(pe, general, r, "1f kq", s)
                        T.matmul(bank[:, 0:3 * P], qcT[s][:, :], W1F["up"][:, 0:3 * P], start=True, stop=True)
                        rows_out(bank[:, 3 * P:4 * P], zT[s], W1F["rope_k"], P)
                        done(T.matmul(bank[:, 512:512 + WIDTH], qcT[s][:, :], W1F["up"][:, 3 * P:3 * P + WIDTH], start=True, stop=True),
                             score, "1f rows", s)
                for s in range(STREAMS):
                    bank = job(turn, r, "1f qk", s)
                    pe.wait_ge(qk_ready, nth(r, s))
                    done(turn_rows(bank, heads_out[s][:, 0:512], 4), turn, "1f qk", s)

                def turn_heads(name, attention, groups, streams):
                    for s in streams:
                        bank = job(turn, r, name, s)
                        all_moved(pe, general, r, [(attention, s, g) for g in range(groups)])
                        done(turn_rows(bank, heads_out[s]), turn, name, s)

                def output(name, turned, w, s):
                    bank = job(general, r, name, s)
                    moved(pe, turn, r, turned, s)
                    done(rows_out(bank[:, 0:WIDTH], headsT[s], w, WIDTH), general, name, s)

                attend_narrow(r, "1f", 2, small_scores("1f", tB, causal_b), small_place, between=[
                    (7, lambda: turn_heads("1f o", "1f ao", 2, BOTH[0])),
                    (8, lambda: output("1f out", "1f o", W1F["o"], 0)), (9, lambda: output("1f out", "1f o", W1F["o"], 1))])
                turn_heads("1f o", "1f ao", 2, BOTH[1])
                for s in BOTH[1]:
                    output("1f out", "1f o", W1F["o"], s)
                for s in range(STREAMS):
                    bank = job(turn, r, "1f h", s)
                    pe.wait_ge(rows_ready, count(r, weighted_rows, "1f h", s))
                    done(turn_rows(bank, hrow[s]), turn, "1f h", s)
                for s in range(STREAMS):
                    bank = job(general, r, "1f router", s)
                    moved(pe, turn, r, "1f h", s)
                    done(rows_out(bank[:, 0:EXPERTS], zT[s], W1F["router"], EXPERTS), general, "1f router", s)
                pe.wait_ge(loaded["wm"], 16)
                order = units(2)
                for t in range(len(order) + 2):
                    if t < len(order):
                        s, g = order[t]
                        bank = job(score, r, "1f gu", s, g)
                        for q in range(2):
                            ins = rows_out(bank[:, q * 512:(q + 1) * 512], zT[s], WM["gate_up"], EXPERTS * 2 * INNER,
                                           at=g * 1024 + q * 512)
                        done(ins, score, "1f gu", s, g)
                    if 1 <= t <= len(order):
                        s, g = order[t - 1]
                        bank = job(turn, r, "1f m", s, g)
                        moved(pe, score, r, "1f gu", s, g)
                        done(turn_rows(bank, big[s][:, g * 512:(g + 1) * 512], 4), turn, "1f m", s, g)
                    if t >= 2:
                        s, g = order[t - 2]
                        if g == 1:
                            if s == STREAMS - 1:
                                pe.wait_ge(loaded["w3"], 16)
                                for i in range(STREAMS):
                                    done(rows_out(job(general, r, "3 v", i)[:, 0:G3 * HD3], cxT[i], W3["v"], G3 * HD3), general, "3 v", i)
                            bank = job(general, r, "1f moe", s)
                            for half in range(2):
                                moved(pe, turn, r, "1f m", s, half)
                            done(rows_out(bank[:, 0:WIDTH], big[s][:, 1024:2048], WM["down"], WIDTH, EXPERTS), general, "1f moe", s)

                turn_z(r, "2 zT", "2")

                def scores2(s, g, bank):
                    moved(pe, general, r, "2 zT", s)
                    pe.wait_ge(cx_loaded[s], r * 16 + 16)
                    masked(bank[:, 0:P], mask2[s], 1)
                    for b in range(KB):
                        ins = T.matmul(bank[:, 0:P], zT[s][:, b * P:b * P + P], cxT[s][:, b * P:b * P + P], start=False, stop=(b == KB - 1))
                    return ins

                attend(r, "2", 1, 1, scores2, lambda s: cx[s][:, 0:WIDTH + 1], WIDTH + 1, turns=1)
                keys3_in(r, (0, 1))
                for pair in BOTH:
                    turn_z(r, "2f zT", "2f", pair)
                    for s in pair:
                        bank = job(general, r, "2f out", s)
                        moved(pe, general, r, "2f zT", s)
                        done(rows_out(bank[:, 0:WIDTH], zT[s], w2f, WIDTH), general, "2f out", s)
                keys3_in(r, (2, 3))

                for pair in BOTH:
                    turn_z(r, "3 zT", "3", pair)
                    for s in pair:
                        bank = job(general, r, "3 q", s)
                        moved(pe, general, r, "3 zT", s)
                        done(blocks_out(bank, W3["q"], WIDTH, zT[s]), general, "3 q", s)

                def scores3(s, g, bank):
                    if g == 0:
                        all_moved(pe, general, r, [("3 k", s), ("3 v", s), ("3 q", s)])
                    for q in range(2):
                        b, row = (2 * g + q) // 4, 32 * ((2 * g + q) % 4)
                        masked(bank[:, q * 512:(q + 1) * 512], mask3[s], 4)
                        ins = T.matmul(bank[:, q * 512:(q + 1) * 512], zT[s][row:row + 32, b * P:b * P + P],
                                       big[s][row:row + 32, b * 512:(b + 1) * 512], start=False, stop=True)
                    return ins

                attend_narrow(r, "3", 4, scores3, lambda g, i: (2 * g + i // HPG, i // HPG, i % HPG), between=[
                    (11, lambda: turn_heads("3 o", "3 ao", 4, BOTH[0])),
                    (12, lambda: output("3 out", "3 o", W3["o"], 0)), (13, lambda: output("3 out", "3 o", W3["o"], 1))])
                turn_heads("3 o", "3 ao", 4, BOTH[1])
                for s in BOTH[1]:
                    output("3 out", "3 o", W3["o"], s)

                for pair in BOTH:
                    turn_z(r, "3f zT", "3f", pair)
                    for s in pair:
                        bank = job(score, r, "3f h", s)
                        moved(pe, general, r, "3f zT", s)
                        done(blocks_out(bank, W3F["fc"], FF3, zT[s], FB3), score, "3f h", s)
                for s in range(STREAMS):
                    bank = job(general, r, "3f out", s)
                    pe.wait_ge(relu_squared, nth(r, s))
                    done(rows_out(bank[:, 0:WIDTH], big[s][:, 1024:1024 + FF3], W3F["proj"], WIDTH, FB3), general, "3f out", s)


INPUT_SHAPES = [("x", (SEQUENCES, P, WIDTH), F32), ("ctx", (SEQUENCES, P, WIDTH), F32), ("ctxT", (SEQUENCES, P, WIDTH), F32),
                ("seg", (ROUNDS, P, STREAMS), I32), ("keep", (ROUNDS, STREAMS * P), U8), ("pad", (ROUNDS, STREAMS * P), I32),
                ("const", (P, width(CONST_NAMES)), F32), ("constb", (P, 2 * P), BF16), ("rows", (width(ROW_NAMES),), F32),
                ("w0", (P, width(W0_NAMES)), F32), ("w0f", (P, width(W0F_NAMES)), F32), ("w1", (P, width(W1_NAMES)), F32),
                ("w1p", (P, width(W1P_NAMES)), F32), ("w1f", (P, width(W1F_NAMES)), F32), ("wm", (P, width(WM_NAMES)), F32),
                ("w2f", (P, KB * WIDTH), F32), ("w3", (P, width(W3_NAMES)), F32), ("w3f", (P, width(W3F_NAMES)), F32)]


def by_block(w):
    n = w.shape[1]
    return w.reshape(-1, P, n).transpose(1, 0, 2).reshape(P, -1)


def pad_rows(w, at=0):
    out = np.zeros((P, w.shape[1]), w.dtype)
    out[at:at + w.shape[0]] = w
    return out


def constants():
    part = np.arange(P)
    t = np.arange(P, dtype=np.float32)

    def angles(half):
        inv = (1.0 / np.float32(10000.0) ** (np.arange(half, dtype=np.float32) / np.float32(half))).astype(np.float32)
        return (t[:, None] * inv).astype(np.float32)
    a, f = angles(ROPE // 2), angles(RD // 2)
    cos_q = np.concatenate([np.cos(a), np.cos(a)], 1)
    sin_q = np.concatenate([-np.sin(a), np.sin(a)], 1)
    parts = {
        "ident": np.eye(P), "even": (part // HD0 % 2 == 0)[:, None], "odd": (part // HD0 % 2 == 1)[:, None],
        "quarter": part[:, None] // HD3 % HPG == np.arange(HPG)[None, :], "key": np.tile(t, (P, 1)),
        "falling": np.tile(np.arange(EXPERTS, 0, -1), (P, 1)), "cos_q": cos_q, "sin_q": sin_q,
        "cos_kT": pad_rows(cos_q.T, KVC), "sin_kT": pad_rows(sin_q.T, KVC),
        "cos_f": np.concatenate([np.cos(f), np.cos(f)], 1), "sin_f": np.concatenate([-np.sin(f), np.sin(f)], 1)}
    return np.concatenate([np.asarray(parts[n], np.float32) for n, _ in CONST_NAMES], 1)


def kernel(**inputs):
    import concourse.bacc as bacc
    import ml_dtypes
    from concourse.bass_utils import run_bass_kernel_spmd

    I = {k: np.asarray(v) for k, v in inputs.items()}

    def pack(names, parts):
        for n, cols in names:
            assert parts[n].shape == (P, cols), (n, parts[n].shape, cols)
        return np.ascontiguousarray(np.concatenate([parts[n] for n, _ in names], 1))

    def of(prefix):
        return {k[len(prefix):]: v for k, v in I.items() if k.startswith(prefix)}
    x0, f0, x1, f1 = of("L0_xattn_"), of("L0_ffn_"), of("L1_xattn_"), of("L1_ffn_")
    x3, f3 = of("L3_xattn_"), of("L3_ffn_")

    def features_first(w):
        return w.transpose(1, 0, 2).reshape(w.shape[1], -1)

    def swapped(w):
        half = w.shape[1] // 2
        return np.concatenate([w[:, half:], w[:, :half]], 1)

    causal = np.where(np.tril(np.ones((P, P), bool)), 0.0, MASKED)
    tail = np.zeros((WIDTH, 1), np.float32)
    gate_up = np.stack([np.concatenate([f1["sh_gate"][None], f1["r_gate"]]),
                        np.concatenate([f1["sh_up"][None], f1["r_up"]])], 1)
    k_repeated = np.repeat(x3["w_k"].reshape(G3, 1, HD3, WIDTH), HPG, 1).reshape(WIDTH, WIDTH)
    none = np.zeros((LATENT, P), np.float32)
    up = np.concatenate([np.concatenate([none, f1["k_u_w"], none, f1["v_u_w"]], 1),
                         np.concatenate([f1["q_u_w"], none, f1["rope_q_w"], none, none], 1)], 0)
    arrays = {
        "x": I["x"], "ctx": I["ctx_2048"],
        "ctxT": I["ctx_2048"].transpose(0, 2, 1).reshape(SEQUENCES, KB, P, P).transpose(0, 2, 1, 3).reshape(SEQUENCES, P, WIDTH),
        "seg": I["itok_BxS_0_1023"].reshape(ROUNDS, STREAMS, P).transpose(0, 2, 1),
        "keep": I["mask_BxS2_bk0"].reshape(ROUNDS, STREAMS * P),
        "pad": I["mask_BxS2_if1"].reshape(ROUNDS, STREAMS * P),
        "const": constants(), "constb": np.concatenate([np.eye(P), causal], 1).astype(ml_dtypes.bfloat16),
        "rows": np.concatenate([x0["b_v"], f1["ln1_w"], f1["ln2_w"], I["L2_ffn_bias"], x3["b_o"], f1["router_b"],
                                np.zeros(1, np.float32), f0["imp_center"], f0["imp_slope"]]),
        "w0": pack(W0_NAMES, {"fc": by_block(x0["W_fc"].T), "q": by_block(x0["W_q"].T), "k": by_block(x0["W_k"].T),
                              "v": by_block(x0["W_v"].reshape(WIDTH, WIDTH).T), "b_fc": x0["b_fc"].reshape(KB, P).T,
                              "b_q": x0["b_q"].reshape(KB, P).T, "b_k": x0["b_k"].reshape(KB, P).T}),
        "w0f": pack(W0F_NAMES, {
            "sel": by_block(np.concatenate([features_first(f0["select_weight"]), features_first(f0["lora_update"]),
                                            f0["select_mean_diff"].T], 1)),
            "debias": by_block(f0["debias_w"].T),
            "lift": pad_rows(np.concatenate([f0["lora_degen"].transpose(0, 2, 1).reshape(-1, WIDTH), f0["bias_w"]]))}),
        "w1": pack(W1_NAMES, {"kvc": by_block(x1["W_kvc"]), "dq": by_block(x1["W_dq"])}),
        "w1p": pack(W1P_NAMES, {"uqT": x1["W_uq"].reshape(QC, H1, P).transpose(2, 1, 0).reshape(P, -1),
                                "ukT": x1["W_uk"].reshape(KVC, H1, P).transpose(2, 1, 0).reshape(P, -1),
                                "uvT": x1["W_uv"].reshape(KVC, H1, P).transpose(2, 1, 0).reshape(P, -1),
                                "o": by_block(x1["W_o"]), "kvcT": pad_rows(x1["W_kvc"].T), "qr": pad_rows(x1["W_qr"]),
                                "kr": pad_rows(np.concatenate([x1["W_kr"], swapped(x1["W_kr"])], 1))}),
        "w1f": pack(W1F_NAMES, {"down_kq": by_block(np.concatenate([f1["kv_d_w"], f1["q_d_w"]], 1)), "up": up,
                                "rope_k": by_block(f1["rope_k_w"]), "o": by_block(f1["o_w"]),
                                "router": by_block(np.concatenate([f1["router_w"], tail], 1))}),
        "wm": pack(WM_NAMES, {"gate_up": by_block(gate_up.transpose(2, 0, 1, 3).reshape(WIDTH, -1)),
                              "down": by_block(np.concatenate([f1["sh_down"][None], f1["r_down"]]).reshape(-1, WIDTH))}),
        "w2f": by_block(I["L2_ffn_weight"]),
        "w3": pack(W3_NAMES, {"q": by_block(x3["w_q"].T), "k": by_block(k_repeated.T), "v": by_block(x3["w_v"].T),
                              "o": by_block(x3["w_o"].T)}),
        "w3f": pack(W3F_NAMES, {"fc": by_block(f3["w_fc"].T), "proj": by_block(f3["w_proj"].T)}),
    }
    nc = bacc.Bacc("TRN2", target_bir_lowering=False, num_devices=1)
    A = {n: nc.dram_tensor(f"in_{n}", shape, dt, kind="ExternalInput").ap() for n, shape, dt in INPUT_SHAPES}
    A["out"] = nc.dram_tensor("out", (SEQUENCES, P, WIDTH), F32, kind="ExternalOutput").ap()
    program(nc, A)
    data = {f"in_{n}": np.ascontiguousarray(arrays[n]) for n, _, _ in INPUT_SHAPES}
    for n, shape, _ in INPUT_SHAPES:
        assert data[f"in_{n}"].shape == shape, (n, data[f"in_{n}"].shape)
    return run_bass_kernel_spmd(nc, [data], core_ids=[0]).results[0]["out"]
```
